# Optimizing a Trainium2 kernel written in Bass

```python
import numpy as np
import jax
import jax.numpy as jnp

def _softmax(x, axis=-1):
    return jax.nn.softmax(x, axis=axis)

def _gelu(x):
    return jax.nn.gelu(x, approximate=True)

def _silu(x):
    return jax.nn.silu(x)

def _sigmoid(x):
    return jax.nn.sigmoid(x)

def _layernorm(x, axis=-1, eps=1e-05):
    m = jnp.mean(x, axis=axis, keepdims=True)
    v = jnp.var(x, axis=axis, keepdims=True)
    return (x - m) / jnp.sqrt(v + eps)

def _scatter_add(tgt, idx, src, axis=0):
    return tgt.at[idx].add(src)

def _segment_sum(src, seg, n):
    return jax.ops.segment_sum(src, seg, n)
kernel_name = 'mk_decoder_postln_d2_seqx_r8_d8f667'

def setup_inputs(seed: int=0):
    np.random.seed(seed)
    _w = jnp.asarray

    def _rec_inputs():
        import jax
        import jax.numpy as jnp
        _rk = jax.random.key(seed)
        x = 7.22e-05 + 1 * jax.random.normal(jax.random.fold_in(_rk, 1), (4, 512, 128), jnp.float32)
        _lenS = 512 - jax.random.randint(jax.random.fold_in(_rk, 7), (4,), 0, max(1, 512 // 4) + 1, jnp.int32)
        _lenS2 = 77 - jax.random.randint(jax.random.fold_in(_rk, 8), (4,), 0, max(1, 77 // 4) + 1, jnp.int32)
        _ctx_1024P = jax.random.normal(jax.random.fold_in(_rk, 11), (4, 16, 128), jnp.float32)
        _ctx_1024c = jax.random.dirichlet(jax.random.fold_in(_rk, 511), 0.3 * jnp.ones((16,), jnp.float32), (4, 77))
        _ctx_1024t = jnp.einsum('bsk,bkd->bsd', _ctx_1024c, _ctx_1024P)
        _ctx_1024t = _ctx_1024t * jax.lax.rsqrt(jnp.mean(jnp.square(_ctx_1024t)) + 1e-12) * 0.953939
        ctx_1024 = 4.13588e-05 + 0.999923 * (_ctx_1024t + 0.3 * jax.random.normal(jax.random.fold_in(_rk, 611), (4, 77, 128), jnp.float32))
        _validS = jnp.arange(512)[None, :] < _lenS[:, None]
        _validS2 = jnp.arange(77)[None, :] < _lenS2[:, None]
        _causal = jnp.tril(jnp.ones((512, 512), dtype=bool))
        mask_1x1xSxS2_ff0 = jnp.where(jnp.ones((1, 1, 512, 77), dtype=bool), 0.0, -1000000000.0).astype(jnp.float32)
        return (x, ctx_1024, mask_1x1xSxS2_ff0)
    x, ctx_1024, mask_1x1xSxS2_ff0 = _rec_inputs()

    def _L0_attn_setup():
        import jax, jax.numpy as jnp
        import numpy as np
        B, T, E, H = (2, 256, 128, 16)
        HD = E // H

        def _xavier(key, shape):
            limit = float(np.sqrt(6.0 / (shape[0] + shape[1])))
            return jax.random.uniform(key, shape, dtype=jnp.float32, minval=-limit, maxval=limit)
        key = jax.random.key(seed)
        kx, kq, kk, kv = jax.random.split(key, 4)
        return {'x': jax.random.normal(kx, (B, T, E), dtype=jnp.float32), 'w_Q': _xavier(kq, (E, E)), 'w_K': _xavier(kk, (E, E)), 'w_V': _xavier(kv, (E, E))}
    _L0_attn_all = _L0_attn_setup()
    _L0_attn_in = {k: v for k, v in _L0_attn_all.items() if k in ('w_Q', 'w_K', 'w_V')}
    del _L0_attn_all

    def _L0_xattn_setup():
        import jax, jax.numpy as jnp
        import numpy as np
        import math
        B, S, D, H = (4, 256, 128, 16)
        HD = D // H
        key = jax.random.key(seed)
        ks = jax.random.split(key, 7)
        scale = 1.0 / math.sqrt(D)
        return {'q': jax.random.normal(ks[0], (B, S, D), jnp.float32), 'k': jax.random.normal(ks[1], (B, S, D), jnp.float32), 'v': jax.random.normal(ks[2], (B, S, D), jnp.float32), 'mask': jnp.zeros((1, 1, S, S), jnp.float32), 'wq': jax.random.normal(ks[3], (D, D), jnp.float32) * scale, 'wk': jax.random.normal(ks[4], (D, D), jnp.float32) * scale, 'wv': jax.random.normal(ks[5], (D, D), jnp.float32) * scale, 'wo': jax.random.normal(ks[6], (D, D), jnp.float32) * scale}
    _L0_xattn_all = _L0_xattn_setup()
    _L0_xattn_in = {k: v for k, v in _L0_xattn_all.items() if k in ('wq', 'wk', 'wv', 'wo')}
    del _L0_xattn_all

    def _L0_ffn_setup():
        import jax, jax.numpy as jnp
        import numpy as np
        import math
        BETA = 0.9
        THRESHOLD = 1.0
        NUM_STEPS = 5
        ALPHA = 2.0

        @jax.custom_vjp
        def spike_fn(u):
            return (u > 0).astype(u.dtype)

        def _spike_fwd(u):
            return (spike_fn(u), u)

        def _spike_bwd(u, g):
            s = jnp.pi / 2.0 * ALPHA * u
            return (g * (ALPHA / 2.0) / (1.0 + s * s),)
        spike_fn.defvjp(_spike_fwd, _spike_bwd)
        key = jax.random.key(seed)
        k1, k2, k3 = jax.random.split(key, 3)
        n_embd = 128
        x = jax.random.normal(k1, (4, 256, n_embd), dtype=jnp.float32)
        W_fc = jax.random.normal(k2, (4 * n_embd, n_embd), dtype=jnp.float32) / math.sqrt(n_embd)
        W_proj = jax.random.normal(k3, (n_embd, 4 * n_embd), dtype=jnp.float32) / math.sqrt(4 * n_embd)
        return {'x': x, 'W_fc': W_fc, 'W_proj': W_proj}
    _L0_ffn_all = _L0_ffn_setup()
    _L0_ffn_in = {k: v for k, v in _L0_ffn_all.items() if k in ('W_fc', 'W_proj')}
    del _L0_ffn_all

    def _L1_attn_setup():
        import jax, jax.numpy as jnp
        import numpy as np
        from jax import lax
        B, T, H, D = (8, 256, 128, 128)
        RMS_EPS = 1e-08

        def rms_norm(x, w):
            var = jnp.mean(jnp.square(x), axis=-1, keepdims=True)
            return x * lax.rsqrt(var + RMS_EPS) * w

        def act_quant(x):
            scale = 127.0 / jnp.clip(jnp.max(jnp.abs(x), axis=-1, keepdims=True), 1e-05, None)
            return jnp.clip(jnp.round(x * scale), -128, 127) / scale

        def weight_quant(w):
            scale = 1.0 / jnp.clip(jnp.mean(jnp.abs(w)), 1e-05, None)
            return jnp.clip(jnp.round(w * scale), -1, 1) / scale

        def bit_linear(x, w, rms_w):
            xn = rms_norm(x, rms_w)
            xq = xn + lax.stop_gradient(act_quant(xn) - xn)
            wq = w + lax.stop_gradient(weight_quant(w) - w)
            return xq @ wq.T

        def wkv_with_eps(time_decay, time_first, k, v):
            w_log = -jnp.exp(time_decay)
            u = time_first
            Bz, Tz, Dz = k.shape
            init = (jnp.zeros((Bz, Dz), k.dtype), jnp.zeros((Bz, Dz), k.dtype), jnp.zeros((Bz, Dz), k.dtype))

            def step(carry, kv):
                alpha, beta, eps = carry
                kt, vt = kv
                ukt = u + kt
                tau = jnp.maximum(ukt, eps)
                e1 = jnp.exp(eps - tau)
                e2 = jnp.exp(ukt - tau)
                out = (e1 * alpha + e2 * vt) / (e1 * beta + e2)
                w_eps = eps + w_log
                eps_n = jnp.maximum(w_eps, kt)
                e1n = jnp.exp(w_eps - eps_n)
                e2n = jnp.exp(kt - eps_n)
                return ((e1n * alpha + e2n * vt, e1n * beta + e2n, eps_n), out)
            _, outs = lax.scan(step, init, (jnp.swapaxes(k, 0, 1), jnp.swapaxes(v, 0, 1)))
            return jnp.swapaxes(outs, 0, 1)
        key = jax.random.key(seed)
        ks = jax.random.split(key, 16)
        std = 0.02
        return {'hidden': jax.random.normal(ks[0], (B, T, H), jnp.float32), 'time_decay': jax.random.normal(ks[1], (D,), jnp.float32), 'time_first': jax.random.normal(ks[2], (D,), jnp.float32), 'time_mix_key': jax.random.uniform(ks[3], (1, 1, H), jnp.float32), 'time_mix_value': jax.random.uniform(ks[4], (1, 1, H), jnp.float32), 'time_mix_receptance': jax.random.uniform(ks[5], (1, 1, H), jnp.float32), 'w_key': std * jax.random.normal(ks[6], (D, H), jnp.float32), 'w_value': std * jax.random.normal(ks[7], (D, H), jnp.float32), 'w_receptance': std * jax.random.normal(ks[8], (D, H), jnp.float32), 'w_output': std * np.sqrt(1.0 / 2 * 24) * jax.random.normal(ks[9], (H, D), jnp.float32), 'rms_key': jnp.ones((H,), jnp.float32), 'rms_value': jnp.ones((H,), jnp.float32), 'rms_receptance': jnp.ones((H,), jnp.float32), 'rms_output': jnp.ones((D,), jnp.float32)}
    _L1_attn_all = _L1_attn_setup()
    _L1_attn_in = {k: v for k, v in _L1_attn_all.items() if k in ('time_decay', 'time_first', 'time_mix_key', 'time_mix_value', 'time_mix_receptance', 'w_key', 'w_value', 'w_receptance', 'w_output', 'rms_key', 'rms_value', 'rms_receptance', 'rms_output')}
    del _L1_attn_all

    def _L1_xattn_setup():
        import jax, jax.numpy as jnp
        import numpy as np
        DIM = 128
        N_HEADS = 16
        HEAD_DIM = DIM // N_HEADS
        GAMMA = 10.0

        def larope_cos_sin(seq_len, gamma, head_dim):
            inv_freq = 1.0 / 10000.0 ** (jnp.arange(0, head_dim, 2, dtype=jnp.float32) / head_dim)
            t = jnp.arange(seq_len, dtype=jnp.float32)
            freqs = jnp.outer(gamma * (t / seq_len), inv_freq)
            emb = jnp.concatenate([freqs, freqs], axis=-1)
            return (jnp.cos(emb), jnp.sin(emb))

        def apply_rope(x, cos, sin):
            d = x.shape[-1] // 2
            x1, x2 = (x[..., :d], x[..., d:])
            c = cos[None, None, :, :d]
            s = sin[None, None, :, :d]
            return jnp.concatenate([x1 * c - x2 * s, x1 * s + x2 * c], axis=-1)
        key = jax.random.key(seed)
        ks = jax.random.split(key, 11)
        B, Lq, Lk = (4, 256, 128)
        std = 1.0 / np.sqrt(DIM)
        inp = {'query': jax.random.normal(ks[0], (B, Lq, DIM), dtype=jnp.float32), 'key': jax.random.normal(ks[1], (B, Lk, DIM), dtype=jnp.float32), 'value': jax.random.normal(ks[2], (B, Lk, DIM), dtype=jnp.float32), 'Wq': jax.random.normal(ks[3], (DIM, DIM), dtype=jnp.float32) * std, 'bq': jnp.zeros((DIM,), dtype=jnp.float32), 'Wk': jax.random.normal(ks[4], (DIM, DIM), dtype=jnp.float32) * std, 'bk': jnp.zeros((DIM,), dtype=jnp.float32), 'Wv': jax.random.normal(ks[5], (DIM, DIM), dtype=jnp.float32) * std, 'bv': jnp.zeros((DIM,), dtype=jnp.float32), 'Wo': jax.random.normal(ks[6], (DIM, DIM), dtype=jnp.float32) * std, 'bo': jnp.zeros((DIM,), dtype=jnp.float32)}
        return inp
    _L1_xattn_all = _L1_xattn_setup()
    _L1_xattn_in = {k: v for k, v in _L1_xattn_all.items() if k in ('Wq', 'bq', 'Wk', 'bk', 'Wv', 'bv', 'Wo', 'bo')}
    del _L1_xattn_all

    def _L1_ffn_setup():
        import jax, jax.numpy as jnp
        import numpy as np
        H = 16
        E = 8
        EPS = 1e-05

        def _layernorm(x, g, b):
            mu = jnp.mean(x, axis=-1, keepdims=True)
            var = jnp.mean(jnp.square(x - mu), axis=-1, keepdims=True)
            return (x - mu) * jax.lax.rsqrt(var + EPS) * g + b
        key = jax.random.key(seed)
        T, B, C = (128, 8, 128)
        ks = jax.random.split(key, 12)
        s = 0.02
        return {'x': jax.random.normal(ks[0], (T, B, C), jnp.float32), 'in_proj_w': jax.random.normal(ks[1], (3 * C, C), jnp.float32) * s, 'in_proj_b': jnp.zeros((3 * C,), jnp.float32), 'out_w': jax.random.normal(ks[2], (C, C), jnp.float32) * s, 'out_b': jnp.zeros((C,), jnp.float32), 'ln1_g': jnp.ones((C,), jnp.float32), 'ln1_b': jnp.zeros((C,), jnp.float32), 'router_w': jax.random.normal(ks[3], (E, C), jnp.float32) * s, 'router_b': jnp.zeros((E,), jnp.float32), 'w1': jax.random.normal(ks[4], (E, C, C), jnp.float32) * s, 'b1': jnp.zeros((E, C), jnp.float32), 'w2': jax.random.normal(ks[5], (E, C, C), jnp.float32) * s, 'b2': jnp.zeros((E, C), jnp.float32), 'ln2_g': jnp.ones((C,), jnp.float32), 'ln2_b': jnp.zeros((C,), jnp.float32)}
    _L1_ffn_all = _L1_ffn_setup()
    _L1_ffn_in = {k: v for k, v in _L1_ffn_all.items() if k in ('in_proj_w', 'in_proj_b', 'out_w', 'out_b', 'ln1_g', 'ln1_b', 'router_w', 'router_b', 'w1', 'b1', 'w2', 'b2', 'ln2_g', 'ln2_b')}
    del _L1_ffn_all
    return {'x': x, 'ctx_1024': ctx_1024, 'mask_1x1xSxS2_ff0': mask_1x1xSxS2_ff0, 'L0_attn_w_Q': _L0_attn_in['w_Q'], 'L0_attn_w_K': _L0_attn_in['w_K'], 'L0_attn_w_V': _L0_attn_in['w_V'], 'L0_xattn_wq': _L0_xattn_in['wq'], 'L0_xattn_wk': _L0_xattn_in['wk'], 'L0_xattn_wv': _L0_xattn_in['wv'], 'L0_xattn_wo': _L0_xattn_in['wo'], 'L0_ffn_W_fc': _L0_ffn_in['W_fc'], 'L0_ffn_W_proj': _L0_ffn_in['W_proj'], 'L1_attn_time_decay': _L1_attn_in['time_decay'], 'L1_attn_time_first': _L1_attn_in['time_first'], 'L1_attn_time_mix_key': _L1_attn_in['time_mix_key'], 'L1_attn_time_mix_value': _L1_attn_in['time_mix_value'], 'L1_attn_time_mix_receptance': _L1_attn_in['time_mix_receptance'], 'L1_attn_w_key': _L1_attn_in['w_key'], 'L1_attn_w_value': _L1_attn_in['w_value'], 'L1_attn_w_receptance': _L1_attn_in['w_receptance'], 'L1_attn_w_output': _L1_attn_in['w_output'], 'L1_attn_rms_key': _L1_attn_in['rms_key'], 'L1_attn_rms_value': _L1_attn_in['rms_value'], 'L1_attn_rms_receptance': _L1_attn_in['rms_receptance'], 'L1_attn_rms_output': _L1_attn_in['rms_output'], 'L1_xattn_Wq': _L1_xattn_in['Wq'], 'L1_xattn_bq': _L1_xattn_in['bq'], 'L1_xattn_Wk': _L1_xattn_in['Wk'], 'L1_xattn_bk': _L1_xattn_in['bk'], 'L1_xattn_Wv': _L1_xattn_in['Wv'], 'L1_xattn_bv': _L1_xattn_in['bv'], 'L1_xattn_Wo': _L1_xattn_in['Wo'], 'L1_xattn_bo': _L1_xattn_in['bo'], 'L1_ffn_in_proj_w': _L1_ffn_in['in_proj_w'], 'L1_ffn_in_proj_b': _L1_ffn_in['in_proj_b'], 'L1_ffn_out_w': _L1_ffn_in['out_w'], 'L1_ffn_out_b': _L1_ffn_in['out_b'], 'L1_ffn_ln1_g': _L1_ffn_in['ln1_g'], 'L1_ffn_ln1_b': _L1_ffn_in['ln1_b'], 'L1_ffn_router_w': _L1_ffn_in['router_w'], 'L1_ffn_router_b': _L1_ffn_in['router_b'], 'L1_ffn_w1': _L1_ffn_in['w1'], 'L1_ffn_b1': _L1_ffn_in['b1'], 'L1_ffn_w2': _L1_ffn_in['w2'], 'L1_ffn_b2': _L1_ffn_in['b2'], 'L1_ffn_ln2_g': _L1_ffn_in['ln2_g'], 'L1_ffn_ln2_b': _L1_ffn_in['ln2_b']}

def reference(x, ctx_1024, mask_1x1xSxS2_ff0, L0_attn_w_Q, L0_attn_w_K, L0_attn_w_V, L0_xattn_wq, L0_xattn_wk, L0_xattn_wv, L0_xattn_wo, L0_ffn_W_fc, L0_ffn_W_proj, L1_attn_time_decay, L1_attn_time_first, L1_attn_time_mix_key, L1_attn_time_mix_value, L1_attn_time_mix_receptance, L1_attn_w_key, L1_attn_w_value, L1_attn_w_receptance, L1_attn_w_output, L1_attn_rms_key, L1_attn_rms_value, L1_attn_rms_receptance, L1_attn_rms_output, L1_xattn_Wq, L1_xattn_bq, L1_xattn_Wk, L1_xattn_bk, L1_xattn_Wv, L1_xattn_bv, L1_xattn_Wo, L1_xattn_bo, L1_ffn_in_proj_w, L1_ffn_in_proj_b, L1_ffn_out_w, L1_ffn_out_b, L1_ffn_ln1_g, L1_ffn_ln1_b, L1_ffn_router_w, L1_ffn_router_b, L1_ffn_w1, L1_ffn_b1, L1_ffn_w2, L1_ffn_b2, L1_ffn_ln2_g, L1_ffn_ln2_b):
    import jax
    import jax.numpy as jnp

    def _L0_attn_ref(x, w_Q, w_K, w_V):
        import jax, jax.numpy as jnp
        import numpy as np
        B, T, E, H = (2, 256, 128, 16)
        HD = E // H

        def _xavier(key, shape):
            limit = float(np.sqrt(6.0 / (shape[0] + shape[1])))
            return jax.random.uniform(key, shape, dtype=jnp.float32, minval=-limit, maxval=limit)
        Bs, Ts, Es = x.shape
        q = (x @ w_Q).reshape(Bs, Ts, H, HD).transpose(0, 2, 1, 3)
        k = (x @ w_K).reshape(Bs, Ts, H, HD).transpose(0, 2, 1, 3)
        v = (x @ w_V).reshape(Bs, Ts, H, HD).transpose(0, 2, 1, 3)
        scores = jnp.einsum('bhtd,bhsd->bhts', q, k) / jnp.sqrt(jnp.asarray(HD, x.dtype))
        probs = jax.nn.softmax(scores, axis=-1)
        attn = jnp.einsum('bhts,bhsd->bhtd', probs, v)
        return attn.transpose(0, 2, 1, 3).reshape(Bs, Ts, H * HD)

    def _L0_xattn_ref(q, k, v, mask, wq, wk, wv, wo):
        import jax, jax.numpy as jnp
        import numpy as np
        import math
        B, S, D, H = (4, 256, 128, 16)
        HD = D // H
        bsz, seqlen, _ = q.shape
        xq = (q @ wq).reshape(bsz, seqlen, H, HD).transpose(0, 2, 1, 3)
        xk = (k @ wk).reshape(bsz, k.shape[1], H, HD).transpose(0, 2, 1, 3)
        xv = (v @ wv).reshape(bsz, v.shape[1], H, HD).transpose(0, 2, 1, 3)
        scores = jnp.einsum('bhqd,bhkd->bhqk', xq, xk) / math.sqrt(HD)
        scores = scores + mask
        attn = jax.nn.softmax(scores.astype(jnp.float32), axis=-1)
        out = jnp.einsum('bhqk,bhkd->bhqd', attn, xv)
        out = out.transpose(0, 2, 1, 3).reshape(bsz, seqlen, -1)
        return out @ wo

    def _L0_ffn_ref(x, W_fc, W_proj):
        import jax, jax.numpy as jnp
        import numpy as np
        import math
        BETA = 0.9
        THRESHOLD = 1.0
        NUM_STEPS = 5
        ALPHA = 2.0

        @jax.custom_vjp
        def spike_fn(u):
            return (u > 0).astype(u.dtype)

        def _spike_fwd(u):
            return (spike_fn(u), u)

        def _spike_bwd(u, g):
            s = jnp.pi / 2.0 * ALPHA * u
            return (g * (ALPHA / 2.0) / (1.0 + s * s),)
        spike_fn.defvjp(_spike_fwd, _spike_bwd)
        h = jnp.square(jax.nn.relu(jnp.einsum('bsd,fd->bsf', x, W_fc)))
        y = jnp.einsum('bsf,df->bsd', h, W_proj)

        def step(mem, _):
            reset = jax.lax.stop_gradient(spike_fn(mem - THRESHOLD))
            mem_new = BETA * mem + y - reset * THRESHOLD
            spk = spike_fn(mem_new - THRESHOLD)
            return (mem_new, spk)
        mem0 = jnp.zeros_like(y)
        _, spks = jax.lax.scan(step, mem0, None, length=NUM_STEPS)
        return jnp.sum(spks, axis=0) / NUM_STEPS

    def _L1_attn_ref(hidden, time_decay, time_first, time_mix_key, time_mix_value, time_mix_receptance, w_key, w_value, w_receptance, w_output, rms_key, rms_value, rms_receptance, rms_output):
        import jax, jax.numpy as jnp
        import numpy as np
        from jax import lax
        B, T, H, D = (8, 256, 128, 128)
        RMS_EPS = 1e-08

        def rms_norm(x, w):
            var = jnp.mean(jnp.square(x), axis=-1, keepdims=True)
            return x * lax.rsqrt(var + RMS_EPS) * w

        def act_quant(x):
            scale = 127.0 / jnp.clip(jnp.max(jnp.abs(x), axis=-1, keepdims=True), 1e-05, None)
            return jnp.clip(jnp.round(x * scale), -128, 127) / scale

        def weight_quant(w):
            scale = 1.0 / jnp.clip(jnp.mean(jnp.abs(w)), 1e-05, None)
            return jnp.clip(jnp.round(w * scale), -1, 1) / scale

        def bit_linear(x, w, rms_w):
            xn = rms_norm(x, rms_w)
            xq = xn + lax.stop_gradient(act_quant(xn) - xn)
            wq = w + lax.stop_gradient(weight_quant(w) - w)
            return xq @ wq.T

        def wkv_with_eps(time_decay, time_first, k, v):
            w_log = -jnp.exp(time_decay)
            u = time_first
            Bz, Tz, Dz = k.shape
            init = (jnp.zeros((Bz, Dz), k.dtype), jnp.zeros((Bz, Dz), k.dtype), jnp.zeros((Bz, Dz), k.dtype))

            def step(carry, kv):
                alpha, beta, eps = carry
                kt, vt = kv
                ukt = u + kt
                tau = jnp.maximum(ukt, eps)
                e1 = jnp.exp(eps - tau)
                e2 = jnp.exp(ukt - tau)
                out = (e1 * alpha + e2 * vt) / (e1 * beta + e2)
                w_eps = eps + w_log
                eps_n = jnp.maximum(w_eps, kt)
                e1n = jnp.exp(w_eps - eps_n)
                e2n = jnp.exp(kt - eps_n)
                return ((e1n * alpha + e2n * vt, e1n * beta + e2n, eps_n), out)
            _, outs = lax.scan(step, init, (jnp.swapaxes(k, 0, 1), jnp.swapaxes(v, 0, 1)))
            return jnp.swapaxes(outs, 0, 1)
        shifted = jnp.pad(hidden, ((0, 0), (1, 0), (0, 0)))[:, :-1]
        k_in = hidden * time_mix_key + shifted * (1 - time_mix_key)
        v_in = hidden * time_mix_value + shifted * (1 - time_mix_value)
        r_in = hidden * time_mix_receptance + shifted * (1 - time_mix_receptance)
        k = bit_linear(k_in, w_key, rms_key)
        v = bit_linear(v_in, w_value, rms_value)
        r = jax.nn.sigmoid(bit_linear(r_in, w_receptance, rms_receptance))
        rwkv = wkv_with_eps(time_decay, time_first, k, v)
        return bit_linear(r * rwkv, w_output, rms_output)

    def _L1_xattn_ref(query, key, value, Wq, bq, Wk, bk, Wv, bv, Wo, bo):
        import jax, jax.numpy as jnp
        import numpy as np
        DIM = 128
        N_HEADS = 16
        HEAD_DIM = DIM // N_HEADS
        GAMMA = 10.0

        def larope_cos_sin(seq_len, gamma, head_dim):
            inv_freq = 1.0 / 10000.0 ** (jnp.arange(0, head_dim, 2, dtype=jnp.float32) / head_dim)
            t = jnp.arange(seq_len, dtype=jnp.float32)
            freqs = jnp.outer(gamma * (t / seq_len), inv_freq)
            emb = jnp.concatenate([freqs, freqs], axis=-1)
            return (jnp.cos(emb), jnp.sin(emb))

        def apply_rope(x, cos, sin):
            d = x.shape[-1] // 2
            x1, x2 = (x[..., :d], x[..., d:])
            c = cos[None, None, :, :d]
            s = sin[None, None, :, :d]
            return jnp.concatenate([x1 * c - x2 * s, x1 * s + x2 * c], axis=-1)
        B, Lq, _ = query.shape
        Lk = key.shape[1]
        scale = HEAD_DIM ** (-0.5)

        def proj(x, W, b, L):
            y = x @ W.T + b
            return y.reshape(B, L, N_HEADS, HEAD_DIM).transpose(0, 2, 1, 3)
        q = proj(query, Wq, bq, Lq)
        k = proj(key, Wk, bk, Lk)
        v = proj(value, Wv, bv, Lk)
        q_cos, q_sin = larope_cos_sin(Lq, GAMMA, HEAD_DIM)
        k_cos, k_sin = larope_cos_sin(Lk, GAMMA, HEAD_DIM)
        q = apply_rope(q, q_cos, q_sin)
        k = apply_rope(k, k_cos, k_sin)
        scores = jnp.einsum('bhqd,bhkd->bhqk', q, k) * scale
        attn = jax.nn.softmax(scores, axis=-1)
        out = jnp.einsum('bhqk,bhkd->bhqd', attn, v)
        out = out.transpose(0, 2, 1, 3).reshape(B, Lq, DIM)
        return out @ Wo.T + bo

    def _L1_ffn_ref(x, in_proj_w, in_proj_b, out_w, out_b, ln1_g, ln1_b, router_w, router_b, w1, b1, w2, b2, ln2_g, ln2_b):
        import jax, jax.numpy as jnp
        import numpy as np
        H = 16
        E = 8
        EPS = 1e-05

        def _layernorm(x, g, b):
            mu = jnp.mean(x, axis=-1, keepdims=True)
            var = jnp.mean(jnp.square(x - mu), axis=-1, keepdims=True)
            return (x - mu) * jax.lax.rsqrt(var + EPS) * g + b
        T, B, C = x.shape
        D = C // H
        qkv = x @ in_proj_w.T + in_proj_b
        q, k, v = jnp.split(qkv, 3, axis=-1)
        q = q.reshape(T, B, H, D)
        k = k.reshape(T, B, H, D)
        v = v.reshape(T, B, H, D)
        scale = 1.0 / np.sqrt(D).astype(np.float32)
        scores = jnp.einsum('tbhd,sbhd->bhts', q, k) * scale
        attn = jax.nn.softmax(scores, axis=-1)
        ctx = jnp.einsum('bhts,sbhd->tbhd', attn, v).reshape(T, B, C)
        attn_out = ctx @ out_w.T + out_b
        h = _layernorm(x + attn_out, ln1_g, ln1_b)
        flat = h.reshape(-1, C)
        logits = flat @ router_w.T + router_b
        probs = jax.nn.softmax(logits, axis=-1)
        _, top_i = jax.lax.top_k(probs, 2)
        assign = jnp.max(top_i, axis=-1)
        out = jnp.zeros_like(flat)
        for e in range(E):
            he = jax.nn.gelu(flat @ w1[e].T + b1[e], approximate=False)
            oe = he @ w2[e].T + b2[e]
            out = jnp.where((assign == e)[:, None], oe, out)
        moe_out = out.reshape(T, B, C)
        return _layernorm(h + moe_out, ln2_g, ln2_b)
    x = _layernorm(x + _L0_attn_ref(x, L0_attn_w_Q, L0_attn_w_K, L0_attn_w_V), axis=-1)
    x = _layernorm(x + _L0_xattn_ref(x, ctx_1024, ctx_1024, mask_1x1xSxS2_ff0, L0_xattn_wq, L0_xattn_wk, L0_xattn_wv, L0_xattn_wo), axis=-1)
    x = _layernorm(x + _L0_ffn_ref(x, L0_ffn_W_fc, L0_ffn_W_proj), axis=-1)
    x = _layernorm(x + _L1_attn_ref(x, L1_attn_time_decay, L1_attn_time_first, L1_attn_time_mix_key, L1_attn_time_mix_value, L1_attn_time_mix_receptance, L1_attn_w_key, L1_attn_w_value, L1_attn_w_receptance, L1_attn_w_output, L1_attn_rms_key, L1_attn_rms_value, L1_attn_rms_receptance, L1_attn_rms_output), axis=-1)
    x = _layernorm(x + _L1_xattn_ref(x, ctx_1024, ctx_1024, L1_xattn_Wq, L1_xattn_bq, L1_xattn_Wk, L1_xattn_bk, L1_xattn_Wv, L1_xattn_bv, L1_xattn_Wo, L1_xattn_bo), axis=-1)
    x = _layernorm(x + _L1_ffn_ref(x, L1_ffn_in_proj_w, L1_ffn_in_proj_b, L1_ffn_out_w, L1_ffn_out_b, L1_ffn_ln1_g, L1_ffn_ln1_b, L1_ffn_router_w, L1_ffn_router_b, L1_ffn_w1, L1_ffn_b1, L1_ffn_w2, L1_ffn_b2, L1_ffn_ln2_g, L1_ffn_ln2_b), axis=-1)
    return x

_drawn_inputs = setup_inputs


def setup_inputs(seed=0):
    import zlib

    import numpy as np

    out = dict(_drawn_inputs(seed))
    spreads = {'L1_attn_rms_key': (1.0, 0.6),
     'L1_attn_rms_value': (1.0, 0.2),
     'L1_attn_rms_receptance': (1.0, 0.6),
     'L1_attn_rms_output': (1.0, 0.2),
     'L1_xattn_bq': (0.0, 0.353),
     'L1_xattn_bk': (0.0, 0.8),
     'L1_xattn_bv': (0.0, 0.1),
     'L1_xattn_bo': (0.0, 0.1),
     'L1_ffn_in_proj_b': (0.0, 0.443),
     'L1_ffn_out_b': (0.0, 0.1),
     'L1_ffn_ln1_g': (1.0, 0.2),
     'L1_ffn_ln1_b': (0.0, 0.1),
     'L1_ffn_router_b': (0.0, 0.1),
     'L1_ffn_b1': (0.0, 0.8),
     'L1_ffn_b2': (0.0, 0.1),
     'L1_ffn_ln2_g': (1.0, 0.2),
     'L1_ffn_ln2_b': (0.0, 0.1)}
    factors = {'L1_attn_time_mix_key': 3.914,
     'L1_attn_time_mix_receptance': 3.258,
     'L1_ffn_in_proj_w': 3.568,
     'L1_ffn_out_w': 2.844,
     'L1_ffn_w1': 4.178,
     'L1_ffn_w2': 3.859}
    for name, (base, spread) in spreads.items():
        noise = np.random.default_rng([zlib.crc32(name.encode()), seed]).standard_normal(out[name].shape)
        drawn = base * np.exp(spread * noise) if base else spread * noise
        out[name] = jnp.asarray(drawn.astype(out[name].dtype))
    for name, factor in factors.items():
        out[name] = (out[name] * factor).astype(out[name].dtype)
    return out
```

```python
from contextlib import ExitStack

import numpy as np
import concourse.bass as bass
from concourse import mybir

ALU = mybir.AluOpType
ACT = mybir.ActivationFunctionType
F32 = mybir.dt.float32
BF16 = mybir.dt.bfloat16
AX_X = mybir.AxisListType.X

P = 128
NB = 4
SEQ = 512
TB = SEQ // P
NT = NB * TB
NH = 16
HD = P // NH
CTX = 77
NCTX = NB * CTX
SCALE = HD ** -0.5
FC = 4
NE = 8
EPS = 1e-5
MAGIC = 1.5 * 2.0 ** 23
PENALTY = -1e30
NEG_LANES = 32

Q_PART = (0, 0, 1, 1, 0, 2)
K_PART = (0, 1, 0, 1, 2, 0)
SLOTS = len(Q_PART)
STACK = SLOTS * HD
AUG = STACK + 3
HALF = NH // 2

MATS = ["q0", "k0", "v0", "xq", "xk", "xv", "xo", "fc0", "fc1", "fc2", "fc3", "pj0", "pj1", "pj2", "pj3",
        "rk", "rv", "rr", "ro", "cq", "cqs", "ck", "cks", "cv", "co", "iq", "ik", "iv", "io"]
MATS += [f"w1_{e}" for e in range(NE)] + [f"w2_{e}" for e in range(NE)] + ["ident"]
ROWS = ["cv_b", "co_b", "iq_b", "ik_b", "iv_b", "io_b", "ln1_g", "ln1_b", "ln2_g", "ln2_b",
        "rms_k", "rms_v", "rms_r", "rms_o", "router_b"]
COLS = ["decay", "first", "mix_k", "mix_v", "mix_r", "cq_b", "cqs_b", "ck_b", "cks_b"]
COLS += [f"b1_{e}" for e in range(NE)]
LAYERS = 6


def transformer(nc, d, LAYERS=LAYERS):
    ctx = ExitStack()
    with ctx:
        def sb(name, shape, dt=F32):
            return ctx.enter_context(nc.sbuf_tensor(name, shape, dt))

        mats = sb("mats", [P, len(MATS), P])
        rows = sb("rows", [P, len(ROWS), P])
        cols = sb("cols", [P, len(COLS)])
        router = sb("router", [P, NE])
        b2 = sb("b2", [NE, P])
        ctx_f = sb("ctx_f", [P, NCTX])
        mask = sb("mask", [P, TB, CTX])
        rope_q = sb("rope_q", [P, 2, SEQ])
        rope_k = sb("rope_k", [P, 2, CTX])
        tri = sb("tri", [P, NE * NE])
        iota = sb("iota", [P, NE])
        ident_b = sb("ident_b", [P, P], BF16)
        ones = sb("ones", [P, P])
        pen = sb("pen", [NE, NE, P], BF16)
        consts = sb("consts", [P, 4])
        x_t = sb("x_t", [P, NT, P])
        x_f = sb("x_f", [P, NB, SEQ])
        d_t = sb("d_t", [P, NT, P])
        ln_in = sb("ln_in", [P, 2, TB, P])
        ln_st = sb("ln_st", [P, 2, TB, 6])
        ln_mv = sb("ln_mv", [P, 2, TB, 2])
        ln_rs = sb("ln_rs", [P, 2, TB, 4])
        parts = sb("parts", [P, 4, 3, SEQ], BF16)
        rest = sb("rest", [P, 2, SEQ])
        v_aug = sb("v_aug", [P, NT * NH * (HD + 1) + NEG_LANES])
        o_f = sb("o_f", [P, 2, SEQ])
        recip = sb("recip", [P, 2, TB, 4])
        q_st = sb("q_st", [P, 2, NH, SEQ], BF16)
        max_t = sb("max_t", [P, 2, TB, HALF])
        max_p = sb("max_p", [HALF, 2, 3, SEQ], BF16)
        max_r = sb("max_r", [HALF, SEQ])
        w_q = sb("w_q", [P, 4, P], BF16)
        w_abs = sb("w_abs", [P, 4])
        w_mean = sb("w_mean", [P, 4])
        w_inv = sb("w_inv", [P, 4])
        mix_c = sb("mix_c", [P, 3])
        log_w = sb("log_w", [P, 2])
        oh_b = sb("oh_b", [NE, 2, SEQ], BF16)
        tok = sb("tok", [P, 2, 8, TB])
        arena = sb("arena", [P, 16384])

        ps = ctx.enter_context(nc.psum_tensor("ps", [P, 8, 512], F32))

        names = """load_x load_w load_s setup setup_dve
            q_raw k_raw v_raw q_hi k_hi v_sb q_mid k_mid q_res k_res q_lo k_lo
            a_s a_max m_t m_hi m_res m_mid m_lo st exp pv ot ott attn
            ln_mv ln_rs ln_x ln_g ln_t ln_f
            x_raw x_rope x_hi x_res x_mid x_lo x_vraw x_v x_s x_z x_mx x_sub x_p x_pt x_pa x_pd x_pv
            c_s c_mx c_st c_exp
            x_ot x_ott x_attn x_at x_af x_wo
            f_h f_r f_sq f_yraw f_y f_spk
            r_abs r_sum r_wq r_mix r_zt r_u r_sq r_ss r_is r_r2 r_q r_xq r_xt r_xf r_mm r_kt r_ktt r_kf
            r_eps r_arg1 r_exp1 r_ev r_scan r_arg2 r_exp2 r_w r_wt r_z r_tanh
            i_raw i_qkv i_prod i_sc i_exp i_p i_pp i_ctx i_ct i_cf i_out
            g_ht g_hf g_raw g_d g_exp g_oh g_oht g_ohf e_h e_g e_o out
            dve pool act""".split()
        names += [f"stack_dma{b}" for b in range(NB)] + [f"m_dma{u}" for u in range(2 * NB)]
        names += [f"x_dma{n}" for n in range(2 * (NB + 1))]
        S = {n: ctx.enter_context(nc.semaphore("s_" + n)) for n in names}

        def mat(n):
            return mats[:, MATS.index(n), :]

        def row(n, tiles):
            return rows[:, ROWS.index(n):ROWS.index(n) + 1, :].to_broadcast([P, tiles, P])

        def col(n):
            return cols[:, COLS.index(n):COLS.index(n) + 1]

        def per_token(ap, width=P):
            return ap.unsqueeze(2).to_broadcast([P, ap.shape[1], width])

        def tiles(bank):
            return ps[:, bank, :].rearrange("p (t c) -> p t c", t=TB)

        VW = NH * (HD + 1)
        v_heads = v_aug[:, 0:NT * VW].rearrange("p (g h e) -> p g h e", g=NT, h=NH)

        def v_lhs(rows_, g, h):
            at = g * VW + h * (HD + 1)
            return v_aug[0:rows_, at:at + NEG_LANES]

        def stack(t, b, rows_, h, lo, hi):
            at = 64 * (b % 2)
            return t[at:at + rows_, b // 2, h, lo:hi]

        k_st = arena[:, 8192:].bitcast(BF16).rearrange("p (u h q) -> p u h q", u=2, h=NH)
        e_buf = arena[:, 0:8192].rearrange("p (u h c q) -> p u h c q", u=2, h=4, c=2)
        zs = arena[:, 0:2 * TB * NH * CTX].rearrange("p (u t h k) -> p u t h k", u=2, t=TB, h=NH)
        at_ = 2 * TB * NH * CTX
        pt_b = arena[0:CTX, at_:at_ + 2 * 4 * SEQ].rearrange("p (u h q) -> p u h q", u=2, h=4)
        at_ += 2 * 4 * SEQ
        x_mx = arena[:, at_:at_ + 2 * NH].rearrange("p (u h) -> p u h", u=2)
        at_ += 32
        a_f = arena[:, at_:at_ + SEQ]
        at_ += SEQ
        kc_st = arena[:, at_:at_ + NH * CTX].bitcast(BF16).rearrange("p (u h k) -> p u h k", u=2, h=NH)
        at_ += NH * CTX
        assert 8192 <= at_ <= 16384
        rp = d_t[:, 0:3 * TB, :].rearrange("p (i t) c -> p i (t c)", i=3)
        e_c = arena[0:CTX, 0:4096].rearrange("p (u h q) -> p u h q", u=2, h=4)
        cm_t = arena[:, 4096:4096 + 2 * TB * NH].rearrange("p (u t h) -> p u t h", u=2, t=TB)
        cm_p = arena[0:NH, 4224:4224 + 3 * SEQ].bitcast(BF16).rearrange("p (u j q) -> p u j q", u=2, j=3)
        cm_r = arena[0:NH, 5760:5760 + SEQ]
        ca_f = arena[:, 6272:6272 + SEQ]
        kr_st = arena[:, 6784:6784 + NH * CTX].bitcast(BF16).rearrange("p (u h k) -> p u h k", u=2, h=NH)
        fr = arena[:, 0:1024].rearrange("p (u q) -> p u q", u=2)
        fh = arena[:, 1024:1024 + 2 * FC * SEQ].rearrange("p (u f q) -> p u f q", u=2, f=FC)
        fy = arena[:, 5120:5120 + 1024].rearrange("p (u q) -> p u q", u=2)
        fs = arena[:, 6144:6144 + 6 * 512].rearrange("p (i q) -> p i q", i=6)

        r0 = q_st[:, :, :, :].rearrange("p u h q -> p (u h q)").bitcast(F32)

        def two(at):
            return r0[:, at:at + 2 * SEQ].rearrange("p (u q) -> p u q", u=2)
        mixed, weighed, squares, shifted_q, lin = (two(2 * SEQ * i) for i in range(5))
        x_q, x_qf = (two(5120).bitcast(BF16)[:, i, :].rearrange("p (u q) -> p u q", u=2) for i in range(2))
        key_f, val_f = two(6144), two(7168)
        r1 = arena[:, 9216:16384]
        arg, ex = (r1[:, 2048 * i:2048 * i + 2048].rearrange("p (i q) -> p i q", i=4) for i in range(2))
        alpha, beta, eps = (r1[:, 4096 + 514 * i:4096 + 514 * i + SEQ + 1] for i in range(3))
        wkv, gate = (r1[:, 5638 + SEQ * i:5638 + SEQ * i + SEQ] for i in range(2))
        gated = d_t[:, 0:TB, :]
        qkv = r0[:, 0:NT * 3 * P].rearrange("p (b t c) -> p b t c", b=NB, t=TB)
        sc, pr = (r0[:, 6144 + 512 * i:6656 + 512 * i].rearrange("p (u q s h) -> p u q s h", u=2, q=NB, s=NB)
                  for i in range(2))
        sc_n = r0[:, 7168:7168 + 6 * NB * NH].rearrange("p (i q h) -> p i q h", i=6, q=NB)
        prod = arena[:, 0:2 * NB * NB * P].rearrange("p (u q s c) -> p u q s c", u=2, q=NB, s=NB)
        pv_t = arena[:, 4096:8192].rearrange("p (u q s c) -> p u q s c", u=2, q=NB, s=NB)
        h_t = arena[:, 8192:10240].rearrange("p (g c) -> p g c", g=NT)
        h_f = arena[:, 10240:12288].rearrange("p (b q) -> p b q", b=NB)
        hid = arena[:, 12288:13312].rearrange("p (u q) -> p u q", u=2)
        c_f = arena[:, 13312:14336].rearrange("p (u q) -> p u q", u=2)
        oh_f = arena[0:NE, 14336:15360].rearrange("p (u q) -> p u q", u=2)
        rank = arena[:, 15360:16128].rearrange("p (i t e f) -> p i t e f", i=3, t=TB, e=NE)
        gates = r0[:, 7552:8064].rearrange("p (i t e) -> p i t e", i=16, t=TB)

        block = ctx.enter_context(nc.Block())

        def self_attention():
            made = 0
            yield ("proj", 0)
            yield ("proj", 1)
            n_a = NB * NH * TB
            for k in range(NB * NH * 2):
                if k in (16, 40):
                    yield ("proj", 2 if k == 16 else 3)
                while made < min(n_a, 2 * k + 46):
                    yield ("a", made)
                    made += 1
                    if made % (HALF * TB) == 0:
                        yield ("max", made // (HALF * TB) - 1)
                g, hh = k // 4, k % 4
                yield ("b", k)
                if hh == 1 and g > 0:
                    yield ("pv", g - 1)
                if hh == 2 and g > 0 and g % 2 == 0:
                    yield ("copy", g // 2 - 1)
                if hh == 3 and g > 0 and g % 2 == 0:
                    yield ("norm", g // 2 - 1)
                    if (g // 2) % 4 == 0:
                        yield ("ln_a", g // 8 - 1)
                if hh == 3 and g % 8 == 1 and g > 8:
                    yield ("ln_b", g // 8 - 1)
            g = NB * NH * 2 // 4
            yield ("pv", g - 1)
            yield ("copy", g // 2 - 1)
            yield ("norm", g // 2 - 1)
            yield ("ln_a", NB - 1)
            yield ("ln_b", NB - 1)

        def cross_attention():
            yield ("k", 0, 0)
            for b in range(NB):
                yield ("q", b, 0)
            for k in range(NT + 14):
                for kind, lag in (("pt", 5), ("s", 0), ("p", 1), ("pv", 6), ("norm", 7)):
                    if 0 <= k - lag < NT:
                        yield (kind, (k - lag) // TB, (k - lag) % TB)
                for kind, lag in (("at", 8), ("wo", 9), ("ln_b", 12)):
                    if 0 <= k - lag < NT and (k - lag) % TB == TB - 1:
                        yield (kind, (k - lag) // TB, 0)

        def rotated_attention():
            yield ("k", 0)
            for b in range(NB):
                yield ("q", b)
            made = 0
            for i in range(NB * NH // 2 + 8):
                while made < min(NT, i // 2 + 6):
                    yield ("a", made)
                    made += 1
                    if made % TB == 0:
                        yield ("max", made // TB - 1)
                if i < NB * NH // 2:
                    yield ("b", i)
                for kind, lag in (("pv", 2), ("copy", 3), ("norm", 4)):
                    if i >= lag and (i - lag) % 2 == 0 and (i - lag) // 2 < NT:
                        yield (kind, (i - lag) // 2)
                for kind, lag in (("at", 11), ("wo", 12), ("ln_b", 17)):
                    if i >= lag and (i - lag) % (NH // 2) == 0 and (i - lag) // (NH // 2) < NB:
                        yield (kind, (i - lag) // (NH // 2))
            yield ("ln_b", NB - 1)

        def recurrent():
            slots, n = [], 0
            for s in range(4 * NB + 4):
                b, w = (s // 4, s % 4) if s % 4 < 3 else (s // 4 - 1, 3)
                there = 0 <= b < NB
                slots.append((n, b, w) if there else None)
                n += there
            for s in range(len(slots) + 6):
                b = (s - 5) // 4
                chain = s % 4 in (1, 2) and 0 <= b < NB
                for kind, lag in (("mix", 0), ("wkv", 1), ("lin", 3), ("quant", 2), ("rms", 0), ("wkv", 2),
                                  ("scale", 1), ("sums", 0), ("turned", 3), ("ln_b", 5)):
                    if kind == "wkv":
                        if chain:
                            yield (f"wkv{2 * (s % 4 - 1) + lag}", 0, b, 0)
                    elif 0 <= s - lag < len(slots) and slots[s - lag]:
                        if kind != "ln_b" or slots[s - lag][2] == 3:
                            yield (kind, *slots[s - lag])

        def unit(u):
            return u // 2, (u % 2) * HALF

        def last_layer():
            n = 5 * NB
            for s in range(NB + 2):
                if s < NB:
                    yield ("router", s, n)
                    n += 1
                if 1 <= s <= NB:
                    yield ("experts", s - 1, n_of_norms(s - 1))
                if s >= 2:
                    yield ("norms", s - 2, n)
                    n += 2

        def n_of_norms(b):
            return 5 * NB + min(NB, b + 3) + 2 * b

        def final(b):
            return (LAYERS - 1) * NB + b if LAYERS < 6 else n_of_norms(b) + 1

        N_SMALL = 13

        @block.sync
        def _(sp):
            sp.dma_start(x_f[:, :, :], d["x_f"]).then_inc(S["load_x"], 16)
            sp.dma_start(mats[:, 0:3, :], d["mats"][:, 0:3, :]).then_inc(S["load_x"], 16)
            sp.dma_start(cols[:, :], d["cols"]).then_inc(S["load_s"], 16)
            sp.dma_start(mats[:, len(MATS) - 1, :], d["mats"][:, len(MATS) - 1, :]).then_inc(S["load_s"], 16)
            sp.dma_start(ctx_f[:, :], d["ctx_f"]).then_inc(S["load_s"], 16)
            sp.dma_start(x_t[:, :, :], d["x_t"]).then_inc(S["load_s"], 16)
            sp.dma_start(mask[:, :, :], d["mask"]).then_inc(S["load_s"], 16)
            sp.dma_start(rope_q[:, :, :], d["rope_q"]).then_inc(S["load_s"], 16)
            sp.dma_start(rope_k[:, :, :], d["rope_k"]).then_inc(S["load_s"], 16)
            sp.dma_start(router[:, :], d["router"]).then_inc(S["load_s"], 16)
            sp.dma_start(b2[:, :], d["b2"]).then_inc(S["load_s"], 16)
            sp.dma_start(tri[:, :], d["tri"]).then_inc(S["load_s"], 16)
            sp.dma_start(iota[:, :], d["iota"]).then_inc(S["load_s"], 16)
            sp.dma_start(pen[:, :, :], d["pen"]).then_inc(S["load_s"], 16)
            sp.dma_start(rows[:, :, :], d["rows"].partition_broadcast(P)).then_inc(S["load_s"], 16)
            sp.dma_start(mats[:, 3:len(MATS) - 1, :], d["mats"][:, 3:len(MATS) - 1, :]).then_inc(S["load_w"], 16)

            def stacks(t, b, src, part_of):
                for s in range(SLOTS):
                    at = 64 * (b % 2) + s * HD
                    sp.dma_start(t[at:at + HD, b // 2, :, :], src[:, part_of[s], :])\
                      .then_inc(S[f"stack_dma{b}"], 16)

            sp.wait_ge(S["setup_dve"], 1)
            for kind, i in self_attention():
                if kind == "proj":
                    sp.wait_ge(S["q_lo"], i + 1)
                    stacks(q_st, i, parts[:, 2 * (i % 2)], Q_PART)
                    sp.wait_ge(S["k_lo"], i + 1)
                    stacks(k_st, i, parts[:, 2 * (i % 2) + 1], K_PART)
                elif kind == "max":
                    b, h0 = unit(i)
                    sp.wait_ge(S["m_lo"], i + 1)
                    for j in range(3):
                        at = 64 * (b % 2) + STACK + j
                        sp.dma_start(q_st[at:at + 1, b // 2, h0:h0 + HALF, :], max_p[:, i % 2, j, :])\
                          .then_inc(S[f"m_dma{i}"], 16)

            def cross_stack(n, t, b, width, part_of, columns):
                for s in range(SLOTS):
                    at = 64 * (b % 2) + s * HD
                    sp.dma_start(t[at:at + HD, b // 2, :, :], parts[:, n % 4, part_of[s], columns:columns + width])\
                      .then_inc(S[f"x_dma{n}"], 16)

            def cross():
                for kind, b, t in cross_attention():
                    if kind == "k":
                        sp.wait_ge(S["x_lo"], 1)
                        sp.wait_ge(S["st"], NB * NH * 2)
                        for c in range(NB):
                            cross_stack(0, kc_st, c, CTX, K_PART, c * CTX)
                    elif kind == "q":
                        sp.wait_ge(S["x_lo"], b + 2)
                        cross_stack(1 + b, q_st, b, SEQ, Q_PART, 0)

            def rotated():
                for kind, i in rotated_attention():
                    if kind == "k":
                        sp.wait_ge(S["x_lo"], 6)
                        for c in range(NB):
                            cross_stack(5, kr_st, c, CTX, K_PART, c * CTX)
                    elif kind == "q":
                        sp.wait_ge(S["x_lo"], 7 + i)
                        cross_stack(6 + i, q_st, i, SEQ, Q_PART, 0)
                    elif kind == "max":
                        sp.wait_ge(S["m_lo"], 2 * NB + i + 1)
                        for j in range(3):
                            at = 64 * (i % 2) + STACK + j
                            sp.dma_start(q_st[at:at + 1, i // 2, :, :], cm_p[:, i % 2, j, :])\
                              .then_inc(S[f"m_dma{i}"], 16)

            if LAYERS > 1:
                cross()
            if LAYERS > 4:
                rotated()
            for b in range(NB):
                sp.wait_ge(S["ln_x"], TB * (final(b) + 1))
                src = x_t[:, TB * b:TB * b + TB, :]
                sp.dma_start(d["out"][b].rearrange("(t p) c -> p t c", p=P), src).then_inc(S["out"], 16)
            sp.wait_ge(S["out"], 16 * NB)

        @block.tensor
        def _(pe):
            readers = [[] for _ in range(8)]

            def take(bank, *by):
                for s, n in readers[bank]:
                    pe.wait_ge(S[s], n)
                readers[bank] = list(by)
                return ps[:, bank, :]

            def mm(out, lhs, rhs, start=True, stop=True, **k):
                return nc.tensor.matmul(out, lhs, rhs, start=start, stop=stop, **k)

            ident = mat("ident")

            def turn(out, src, n=TB):
                for t in range(n):
                    last = nc.tensor.transpose(out[:, t * P:(t + 1) * P], src[:, t, :], ident)
                return last

            def ln_b(n):
                pe.wait_ge(S["ln_x"], TB * (n + 1))
                out = take(7, ("ln_f", n + 1))
                b = n % NB
                turn(out, x_t[:, TB * b:TB * b + TB, :]).then_inc(S["ln_t"], 1)

            pe.wait_ge(S["load_x"], 32)
            for kind, i in self_attention():
                if kind == "proj":
                    if i == 2:
                        pass
                    bq, bk, bv = (0, 1, 2) if i == 0 else (3, 6, 7) if i == 1 else (7, 7, 7)
                    for w, bank, res in (("q", bq, "q_res"), ("k", bk, "k_res")):
                        out = take(bank, (res, i + 1))
                        mm(out, mat(w + "0"), x_f[:, i, :]).then_inc(S[w + "_raw"], 1)
                    out = take(bv, ("v_sb", i + 1))
                    for t in range(TB):
                        last = mm(out[:, t * P:(t + 1) * P], x_f[:, i, t * P:(t + 1) * P], mat("v0"))
                    last.then_inc(S["v_raw"], 1)
                elif kind == "a":
                    u, r = divmod(i, HALF * TB)
                    b, h0 = unit(u)
                    h, t = h0 + r // TB, r % TB
                    if r == 0:
                        pe.wait_ge(S[f"stack_dma{b}"], 16 * 2 * SLOTS)
                    out = take(4 + i % 2, ("a_max", i + 1))
                    mm(out, stack(q_st, b, STACK, h, t * P, t * P + P), stack(k_st, b, STACK, h, 0, SEQ))\
                        .then_inc(S["a_s"], 1)
                elif kind == "max":
                    if i == 0:
                        pe.wait_ge(S["load_s"], 16 * N_SMALL)
                    pe.wait_ge(S["a_max"], HALF * TB * (i + 1))
                    out = take(7, ("m_res", i + 1))
                    for t in range(TB):
                        last = nc.tensor.transpose(out[0:HALF, t * P:(t + 1) * P], max_t[:, i % 2, t, :], ident)
                    last.then_inc(S["m_t"], 1)
                elif kind == "b":
                    g, hh = divmod(i, 4)
                    q, sp_ = divmod(g, 2)
                    b, h = q // 4, 4 * (q % 4) + hh
                    if i % 16 == 0:
                        pe.wait_ge(S[f"m_dma{i // 16}"], 48)
                    for j in range(2):
                        c = 2 * sp_ + j
                        out = take(2 * (i % 2) + j, ("exp", i + 1))
                        last = mm(out, stack(k_st, b, AUG, h, c * P, c * P + P), stack(q_st, b, AUG, h, 0, SEQ))
                    last.then_inc(S["st"], 1)
                elif kind == "pv":
                    q, sp_ = divmod(i, 2)
                    b = q // 4
                    pe.wait_ge(S["exp"], 4 * (i + 1))
                    if sp_ == 0:
                        pe.wait_ge(S["v_sb"], b + 1)
                        take(6, ("ot", q + 1))
                    for j in range(2):
                        for hh in range(4):
                            last = mm(ps[32 * hh:32 * hh + 32, 6, :],
                                      v_lhs(P, TB * b + 2 * sp_ + j, 4 * (q % 4) + hh),
                                      e_buf[:, i % 2, hh, j, :],
                                      start=(sp_ == 0 and j == 0), stop=(sp_ == 1 and j == 1))
                    last.then_inc(S["pv"], 1)
                elif kind == "norm":
                    pe.wait_ge(S["ot"], i + 1)
                    turn(take(7, ("attn", i + 1)), o_f[:, i % 2, :].rearrange("p (t c) -> p t c", t=TB))\
                        .then_inc(S["ott"], 1)
                elif kind == "ln_b":
                    ln_b(i)

            def cross_v(x):
                out = take(4, ("x_v", x + 1))
                for c in range(NB):
                    last = mm(out[0:CTX, c * P:(c + 1) * P], ctx_f[:, c * CTX:(c + 1) * CTX], mat("xc"[x] + "v"))
                last.then_inc(S["x_vraw"], 1)

            def cross():
                for kind, b, t in cross_attention():
                    n = TB * b + t
                    if kind == "k":
                        mm(take(0, ("x_res", 1))[:, 0:NCTX], mat("xk"), ctx_f[:, :]).then_inc(S["x_raw"], 1)
                        cross_v(0)
                    elif kind == "q":
                        pe.wait_ge(S["ln_f"], b + 1)
                        mm(take((1 + b) % 2, ("x_res", b + 2)), mat("xq"), x_f[:, b, :]).then_inc(S["x_raw"], 1)
                    elif kind == "s":
                        if t == 0:
                            pe.wait_ge(S["x_dma0"], 16 * SLOTS * NB)
                            pe.wait_ge(S[f"x_dma{1 + b}"], 16 * SLOTS)
                        for i in range(3):
                            out = take(i, ("x_z", 3 * n + i + 1))
                            for h in range(6 * i, min(6 * i + 6, NH)):
                                at = (h - 6 * i) * CTX
                                last = mm(out[:, at:at + CTX], stack(q_st, b, STACK, h, t * P, t * P + P),
                                          stack(kc_st, b, STACK, h, 0, CTX))
                            last.then_inc(S["x_s"], 1)
                    elif kind == "pt":
                        if t == 0:
                            pe.wait_ge(S["x_p"], n + TB)
                        for j in range(4):
                            out = take(3 + j % 2, ("x_pd", n + 1) if j == 3 else ("x_pa", 3 * n + j + 1))
                            for tt in range(TB):
                                last = nc.tensor.transpose(out[0:CTX, tt * P:(tt + 1) * P],
                                                           zs[:, b % 2, tt, 4 * t + j, :], ident)
                            last.then_inc(S["x_pt"], 1)
                    elif kind == "pv":
                        take(5, ("x_ot", n + 1))
                        pe.wait_ge(S["x_pa"], 3 * (n + 1))
                        pe.wait_ge(S["x_pd"], n + 1)
                        pe.wait_ge(S["x_v"], 1)
                        for j in range(4):
                            last = mm(ps[32 * j:32 * j + 32, 5, :], v_lhs(CTX, b, 4 * t + j), pt_b[:, n % 2, j, :])
                        last.then_inc(S["x_pv"], 1)
                    elif kind == "norm":
                        pe.wait_ge(S["x_ot"], n + 1)
                        turn(take(6, ("x_attn", n + 1)), o_f[:, n % 2, :].rearrange("p (t c) -> p t c", t=TB))\
                            .then_inc(S["x_ott"], 1)
                    elif kind == "at":
                        pe.wait_ge(S["x_attn"], 4 * (b + 1))
                        turn(take(6, ("x_af", b + 1)), d_t[:, TB * b:TB * b + TB, :]).then_inc(S["x_at"], 1)
                    elif kind == "wo":
                        pe.wait_ge(S["x_af"], b + 1)
                        out = take(7, ("ln_mv", NB + b + 1))
                        for c in range(TB):
                            last = mm(out[:, c * P:(c + 1) * P], a_f[:, c * P:(c + 1) * P], mat("xo"))
                        last.then_inc(S["x_wo"], 1)
                    elif kind == "ln_b":
                        ln_b(NB + b)

            def rotated():
                for kind, i in rotated_attention():
                    if kind in ("k", "q"):
                        n = 5 if kind == "k" else 6 + i
                        width = NCTX if kind == "k" else SEQ
                        rhs = ctx_f[:, :] if kind == "k" else x_f[:, i, :]
                        if kind == "q":
                            pe.wait_ge(S["ln_f"], 3 * NB + i + 1)
                        mm(take(n % 2, ("x_rope", n - 4))[:, 0:width], mat("c" + kind), rhs)
                        mm(take(2 + n % 2, ("x_rope", n - 4))[:, 0:width], mat("c" + kind + "s"), rhs)\
                            .then_inc(S["x_raw"], 1)
                        if kind == "k":
                            cross_v(1)
                    elif kind == "a":
                        b, t = divmod(i, TB)
                        if t == 0:
                            pe.wait_ge(S["x_dma5"], 16 * SLOTS * NB)
                            pe.wait_ge(S[f"x_dma{6 + b}"], 16 * SLOTS)
                        for j in range(3):
                            out = take(4 + (3 * i + j) % 2, ("c_mx", 3 * i + j + 1))
                            for h in range(6 * j, min(6 * j + 6, NH)):
                                at = (h - 6 * j) * CTX
                                last = mm(out[:, at:at + CTX], stack(q_st, b, STACK, h, t * P, t * P + P),
                                          stack(kr_st, b, STACK, h, 0, CTX))
                            last.then_inc(S["c_s"], 1)
                    elif kind == "max":
                        pe.wait_ge(S["c_mx"], 3 * TB * (i + 1))
                        out = take(7, ("m_res", 2 * NB + i + 1))
                        for t in range(TB):
                            last = nc.tensor.transpose(out[0:NH, t * P:(t + 1) * P], cm_t[:, i % 2, t, :], ident)
                        last.then_inc(S["m_t"], 1)
                    elif kind == "b":
                        b, h = divmod(2 * i, NH)
                        if h == 0:
                            pe.wait_ge(S[f"m_dma{b}"], 96)
                        for j in range(2):
                            out = take(2 * (i % 2) + j, ("c_exp", i + 1))
                            last = mm(out[0:CTX, :], stack(kr_st, b, AUG, h + j, 0, CTX),
                                      stack(q_st, b, AUG, h + j, 0, SEQ))
                        last.then_inc(S["c_st"], 1)
                    elif kind == "pv":
                        pe.wait_ge(S["c_exp"], 2 * (i + 1))
                        take(6, ("x_ot", NT + i + 1))
                        if i == 0:
                            pe.wait_ge(S["x_v"], 2)
                        for j in range(4):
                            last = mm(ps[32 * j:32 * j + 32, 6, :], v_lhs(CTX, i // 4, 4 * (i % 4) + j),
                                      e_c[:, i % 2, j, :])
                        last.then_inc(S["x_pv"], 1)
                    elif kind == "norm":
                        pe.wait_ge(S["x_ot"], NT + i + 1)
                        turn(take(7, ("x_attn", NT + i + 1)), o_f[:, i % 2, :].rearrange("p (t c) -> p t c", t=TB))\
                            .then_inc(S["x_ott"], 1)
                    elif kind == "at":
                        pe.wait_ge(S["x_attn"], NT + TB * (i + 1))
                        turn(take(7, ("x_af", NB + i + 1)), d_t[:, TB * i:TB * i + TB, :]).then_inc(S["x_at"], 1)
                    elif kind == "wo":
                        pe.wait_ge(S["x_af"], NB + i + 1)
                        out = take(7, ("ln_mv", 4 * NB + i + 1))
                        for c in range(TB):
                            last = mm(out[:, c * P:(c + 1) * P], ca_f[:, c * P:(c + 1) * P], mat("co"))
                        last.then_inc(S["x_wo"], 1)
                    elif kind == "ln_b":
                        ln_b(4 * NB + i)

            pe.wait_ge(S["load_w"], 16)
            if LAYERS > 1:
                cross()
            if LAYERS > 2:
                for b in range(NB + 1):
                    if b < NB:
                        pe.wait_ge(S["ln_f"], NB + b + 1)
                        for f in range(FC):
                            n = FC * b + f
                            mm(take(n % 3, ("f_r", n + 1)), mat(f"fc{f}"), x_f[:, b, :]).then_inc(S["f_h"], 1)
                    if b > 0:
                        c = b - 1
                        pe.wait_ge(S["f_sq"], FC * (c + 1))
                        out = take(3 + c % 2, ("f_y", c + 1))
                        for t in range(TB):
                            for f in range(FC):
                                last = mm(out[:, t * P:(t + 1) * P], fh[:, c % 2, f, t * P:(t + 1) * P],
                                          mat(f"pj{f}"), start=(f == 0), stop=(f == FC - 1))
                        last.then_inc(S["f_yraw"], 1)
                for b in range(NB):
                    ln_b(2 * NB + b)
            if LAYERS > 3:
                pe.wait_ge(S["r_abs"], 4)
                pe.wait_ge(S["setup"], 1)
                mm(take(6, ("r_wq", 4))[:, 0:4], ones[:, :], w_abs[:, :]).then_inc(S["r_sum"], 1)
                for kind, n, b, w in recurrent():
                    if kind == "mix":
                        if w < 3:
                            pe.wait_ge(S["r_mix"], 3 * b + w + 1)
                            out, src = take(n % 2, ("r_u", n + 1), ("r_sq", n + 1)), mixed[:, n % 2, :]
                        else:
                            pe.wait_ge(S["r_w"], b + 1)
                            out, src = take(n % 2, ("r_z", b + 1)), wkv
                        turn(out, src.rearrange("p (t c) -> p t c", t=TB)).then_inc(S["r_zt"], 1)
                    elif kind == "quant":
                        pe.wait_ge(S["r_xq"], n + 1)
                        out = take(2, ("r_xf", n + 1)).bitcast(BF16)
                        for t in range(TB):
                            last = nc.tensor.transpose(out[:, t * P:(t + 1) * P], x_q[:, n % 2, t * P:(t + 1) * P],
                                                       ident_b[:, :])
                        last.then_inc(S["r_xt"], 1)
                    elif kind == "lin":
                        pe.wait_ge(S["r_xf"], n + 1)
                        if n == 0:
                            pe.wait_ge(S["r_wq"], 4)
                        out = take(3, ("r_kt", n + 1))
                        for t in range(TB):
                            last = mm(out[:, t * P:(t + 1) * P], x_qf[:, n % 2, t * P:(t + 1) * P], w_q[:, w, :])
                        last.then_inc(S["r_mm"], 1)
                    elif kind == "turned" and w < 2:
                        pe.wait_ge(S["r_kt"], n + 1)
                        turn(take(4 + w, ("r_kf", 2 * b + w + 1)),
                             lin[:, n % 2, :].rearrange("p (t c) -> p t c", t=TB)).then_inc(S["r_ktt"], 1)
                    elif kind == "ln_b":
                        ln_b(3 * NB + b)
            if LAYERS > 4:
                rotated()
            if LAYERS > 5:
                for b in range(NB):
                    pe.wait_ge(S["ln_f"], 4 * NB + b + 1)
                    for t in range(TB):
                        g = TB * b + t
                        i0 = MATS.index("iq")
                        mm(take(g % 3, ("i_qkv", g + 1))[:, 0:3 * P], x_f[:, b, t * P:(t + 1) * P],
                           mats[:, i0:i0 + 3, :]).then_inc(S["i_raw"], 1)
                for kind, b, n in last_layer():
                    if kind == "router":
                        pe.wait_ge(S["i_ctx"], TB * NB)
                        turn(take(4, ("i_cf", b + 1)), d_t[:, TB * b:TB * b + TB, :]).then_inc(S["i_ct"], 1)
                        pe.wait_ge(S["i_cf"], b + 1)
                        out = take(5, ("ln_mv", n + 1))
                        for t in range(TB):
                            last = mm(out[:, t * P:(t + 1) * P], c_f[:, b % 2, t * P:(t + 1) * P], mat("io"))
                        last.then_inc(S["i_out"], 1)
                        pe.wait_ge(S["ln_g"], b + 1)
                        turn(take(7, ("g_hf", b + 1)), h_t[:, TB * b:TB * b + TB, :]).then_inc(S["g_ht"], 1)
                        pe.wait_ge(S["g_hf"], b + 1)
                        out = take(6, ("g_d", b + 1))
                        for t in range(TB):
                            last = mm(out[:, t * NE:(t + 1) * NE], h_f[:, b, t * P:(t + 1) * P], router[:, :])
                        last.then_inc(S["g_raw"], 1)
                        pe.wait_ge(S["g_oh"], b + 1)
                        out = take(4, ("g_ohf", 2 * b + 2))
                        for t in range(TB):
                            last = nc.tensor.transpose(out[0:NE, t * P:(t + 1) * P], gates[:, 8 + b % 2, t, :], ident)
                        last.then_inc(S["g_oht"], 1)
                    elif kind == "experts":
                        pe.wait_ge(S["g_ohf"], 2 * b + 2)
                        acc = 2 + b % 2
                        out = take(acc, ("ln_mv", n + 1))
                        for t in range(TB):
                            mm(out[:, t * P:(t + 1) * P], oh_f[:, b % 2, t * P:(t + 1) * P], b2[:, :], start=(t == 0),
                               stop=False, skip_group_check=True)
                        for e in range(1, NE + 1):
                            m = (NE - 1) * b + e - 1
                            if e < NE:
                                h = take(m % 2, ("e_g", m + 1))
                                mm(h, mat(f"w1_{e}"), h_f[:, b, :], stop=False)
                                mm(h, pen[:, e, :], oh_b[:, b % 2, :], start=False).then_inc(S["e_h"], 1)
                            if e > 1:
                                pe.wait_ge(S["e_g"], m)
                                for t in range(TB):
                                    last = mm(out[:, t * P:(t + 1) * P], hid[:, (m - 1) % 2, t * P:(t + 1) * P],
                                              mat(f"w2_{e - 1}"), start=False, stop=(e == NE), skip_group_check=True)
                                last.then_inc(S["e_o"], 1)

        @block.scalar
        def _(act):
            def ln_scale(n, b, out):
                act.wait_ge(S["ln_rs"], n + 1)
                u = n % 2
                for t in range(TB):
                    nc.scalar.activation(out[:, t, :], ln_in[:, u, t, :], ACT.Identity,
                                         scale=ln_rs[:, u, t, 1:2], bias=ln_rs[:, u, t, 3:4])\
                        .then_inc(S["ln_x"], 1)

            def ln_apply(n):
                b = n % NB
                ln_scale(n, b, x_t[:, TB * b:TB * b + TB, :])
                act.wait_ge(S["ln_t"], n + 1)
                nc.scalar.copy(x_f[:, b, :], ps[:, 7, :]).then_inc(S["ln_f"], 1)

            for kind, i in self_attention():
                if kind == "proj":
                    bq, bk, bv = (0, 1, 2) if i == 0 else (3, 6, 7) if i == 1 else (7, 7, 7)
                    for w, bank, k in (("q", bq, 0), ("k", bk, 1)):
                        act.wait_ge(S[w + "_raw"], i + 1)
                        if i >= 2:
                            act.wait_ge(S[f"stack_dma{i - 2}"], 16 * 2 * SLOTS)
                        nc.scalar.copy(parts[:, 2 * (i % 2) + k, 0, :], ps[:, bank, :]).then_inc(S[w + "_hi"], 1)
                        act.wait_ge(S[w + "_res"], i + 1)
                        nc.scalar.copy(parts[:, 2 * (i % 2) + k, 1, :], rest[:, k, :]).then_inc(S[w + "_mid"], 1)
                    act.wait_ge(S["v_raw"], i + 1)
                    act.wait_ge(S["setup_dve"], 1)
                    nc.scalar.copy(v_heads[:, TB * i:TB * i + TB, :, 0:HD],
                                   ps[:, bv, :].rearrange("p (t h e) -> p t h e", t=TB, h=NH))\
                        .then_inc(S["v_sb"], 1)
                elif kind == "max":
                    act.wait_ge(S["m_t"], i + 1)
                    if i >= 2:
                        act.wait_ge(S[f"m_dma{i - 2}"], 48)
                    nc.scalar.copy(max_p[:, i % 2, 0, :], ps[0:HALF, 7, :]).then_inc(S["m_hi"], 1)
                    act.wait_ge(S["m_res"], i + 1)
                    nc.scalar.copy(max_p[:, i % 2, 1, :], max_r[:, :]).then_inc(S["m_mid"], 1)
                elif kind == "b":
                    g, hh = divmod(i, 4)
                    if hh == 0 and g >= 2:
                        act.wait_ge(S["pv"], g - 1)
                    act.wait_ge(S["st"], i + 1)
                    nc.scalar.activation(e_buf[:, g % 2, hh, :, :], ps[:, 2 * (i % 2):2 * (i % 2) + 2, :], ACT.Exp,
                                         scale=SCALE).then_inc(S["exp"], 1)
                elif kind == "copy":
                    act.wait_ge(S["pv"], 2 * (i + 1))
                    if i >= 2:
                        act.wait_ge(S["ott"], i - 1)
                    nc.scalar.copy(o_f[:, i % 2, :], ps[:, 6, :]).then_inc(S["ot"], 1)
                elif kind == "ln_b":
                    ln_apply(i)

            def high_and_middle(n, src, width):
                if n >= 4:
                    act.wait_ge(S[f"x_dma{n - 4}"], 16 * SLOTS * (NB if n % 5 == 4 else 1))
                nc.scalar.copy(parts[:, n % 4, 0, 0:width], src).then_inc(S["x_hi"], 1)
                act.wait_ge(S["x_res"], n + 1)
                nc.scalar.copy(parts[:, n % 4, 1, 0:width], rest[:, n % 2, 0:width]).then_inc(S["x_mid"], 1)

            def cross():
                for kind, b, t in cross_attention():
                    n = TB * b + t
                    if kind in ("k", "q"):
                        n = 0 if kind == "k" else 1 + b
                        width = NCTX if kind == "k" else SEQ
                        act.wait_ge(S["x_raw"], n + 1)
                        high_and_middle(n, ps[:, n % 2, 0:width], width)
                        if kind == "k":
                            act.wait_ge(S["x_vraw"], 1)
                            nc.scalar.copy(v_heads[0:CTX, 0:NB, :, 0:HD],
                                           ps[0:CTX, 4, :].rearrange("p (t h e) -> p t h e", t=NB, h=NH))\
                                .then_inc(S["x_v"], 1)
                    elif kind == "p":
                        z = zs[:, b % 2, t, :, :]
                        act.wait_ge(S["x_sub"], n + 1)
                        nc.scalar.activation(z, z, ACT.Exp).then_inc(S["x_p"], 1)
                    elif kind == "pt":
                        for j in range(3):
                            act.wait_ge(S["x_pt"], 4 * n + j + 1)
                            if n >= 2 and j == 0:
                                act.wait_ge(S["x_pv"], n - 1)
                            nc.scalar.copy(pt_b[:, n % 2, j, :], ps[0:CTX, 3 + j % 2, :]).then_inc(S["x_pa"], 1)
                    elif kind == "pv":
                        act.wait_ge(S["x_pv"], n + 1)
                        if n >= 2:
                            act.wait_ge(S["x_ott"], n - 1)
                        nc.scalar.copy(o_f[:, n % 2, :], ps[:, 5, :]).then_inc(S["x_ot"], 1)
                    elif kind == "at":
                        act.wait_ge(S["x_at"], b + 1)
                        if b:
                            act.wait_ge(S["x_wo"], b)
                        nc.scalar.copy(a_f[:, :], ps[:, 6, :]).then_inc(S["x_af"], 1)
                    elif kind == "ln_b":
                        ln_apply(NB + b)

            def rotated():
                for kind, i in rotated_attention():
                    if kind in ("k", "q"):
                        n = 5 if kind == "k" else 6 + i
                        width = NCTX if kind == "k" else SEQ
                        act.wait_ge(S["x_rope"], n - 4)
                        high_and_middle(n, rp[:, 2, 0:width], width)
                    elif kind == "max":
                        act.wait_ge(S["m_t"], 2 * NB + i + 1)
                        if i >= 2:
                            act.wait_ge(S[f"m_dma{i - 2}"], 96)
                        nc.scalar.copy(cm_p[:, i % 2, 0, :], ps[0:NH, 7, :]).then_inc(S["m_hi"], 1)
                        act.wait_ge(S["m_res"], 2 * NB + i + 1)
                        nc.scalar.copy(cm_p[:, i % 2, 1, :], cm_r[:, :]).then_inc(S["m_mid"], 1)
                    elif kind == "b":
                        g = i // 2
                        if i % 2 == 0 and g >= 2:
                            act.wait_ge(S["x_pv"], NT + g - 1)
                        act.wait_ge(S["c_st"], i + 1)
                        j, bank = 2 * (i % 2), 2 * (i % 2)
                        nc.scalar.activation(e_c[:, g % 2, j:j + 2, :], ps[0:CTX, bank:bank + 2, :], ACT.Exp,
                                             scale=SCALE).then_inc(S["c_exp"], 1)
                    elif kind == "copy":
                        act.wait_ge(S["x_pv"], NT + i + 1)
                        if i >= 2:
                            act.wait_ge(S["x_ott"], NT + i - 1)
                        nc.scalar.copy(o_f[:, i % 2, :], ps[:, 6, :]).then_inc(S["x_ot"], 1)
                    elif kind == "at":
                        act.wait_ge(S["x_at"], NB + i + 1)
                        if i:
                            act.wait_ge(S["x_wo"], NB + i)
                        nc.scalar.copy(ca_f[:, :], ps[:, 7, :]).then_inc(S["x_af"], 1)
                    elif kind == "ln_b":
                        ln_apply(4 * NB + i)

            if LAYERS > 1:
                cross()
            if LAYERS > 2:
                for b in range(NB + 1):
                    if b < NB:
                        for f in range(FC):
                            n = FC * b + f
                            act.wait_ge(S["f_h"], n + 1)
                            if n >= 2:
                                act.wait_ge(S["f_sq"], n - 1)
                            nc.scalar.activation(fr[:, n % 2, :], ps[:, n % 3, :], ACT.Relu).then_inc(S["f_r"], 1)
                    if b > 0:
                        act.wait_ge(S["f_yraw"], b)
                        if b > 2:
                            act.wait_ge(S["ln_mv"], 2 * NB + b - 2)
                        nc.scalar.copy(fy[:, (b - 1) % 2, :], ps[:, 3 + (b - 1) % 2, :]).then_inc(S["f_y"], 1)
                for b in range(NB):
                    ln_apply(2 * NB + b)
            if LAYERS > 3:
                for w in range(4):
                    nc.scalar.activation(wkv[:, w * P:(w + 1) * P], mat("r" + "kvro"[w]), ACT.Abs, accum_out=w_abs[:, w:w + 1])\
                        .then_inc(S["r_abs"], 1)
                nc.scalar.activation(log_w[:, 0:1], col("decay"), ACT.Exp).then_inc(S["r_eps"], 1)
                for kind, n, b, w in recurrent():
                    u = n % 2
                    if kind == "rms":
                        if n >= 2:
                            act.wait_ge(S["r_ss"], n - 1)
                        if w < 3:
                            act.wait_ge(S["r_u"], n + 1)
                            src = ps[:, u, :]
                        else:
                            act.wait_ge(S["r_z"], b + 1)
                            src = gated.rearrange("p t c -> p (t c)")
                        nc.scalar.activation(squares[:, u, :], src, ACT.Square).then_inc(S["r_sq"], 1)
                    elif kind == "scale":
                        act.wait_ge(S["r_r2"], n + 1)
                        if n >= 2:
                            act.wait_ge(S["r_xq"], n - 1)
                        for t in range(TB):
                            nc.scalar.activation(shifted_q[:, u, t * P:(t + 1) * P], weighed[:, u, t * P:(t + 1) * P],
                                                 ACT.Identity, scale=tok[:, u, 5, t:t + 1], bias=consts[:, 2:3])\
                                .then_inc(S["r_q"], 1)
                    elif kind == "quant":
                        act.wait_ge(S["r_xt"], n + 1)
                        if n >= 2:
                            act.wait_ge(S["r_mm"], n - 1)
                        nc.scalar.copy(x_qf[:, u, :], ps[:, 2, :].bitcast(BF16)[:, 0:SEQ]).then_inc(S["r_xf"], 1)
                    elif kind == "turned" and w < 2:
                        act.wait_ge(S["r_ktt"], 2 * b + w + 1)
                        if b >= 2:
                            act.wait_ge(S["r_w"], b - 1)
                        nc.scalar.copy((key_f, val_f)[w][:, b % 2, :], ps[:, 4 + w, :]).then_inc(S["r_kf"], 1)
                    elif kind == "turned" and w == 2:
                        act.wait_ge(S["r_kt"], n + 1)
                        if b:
                            act.wait_ge(S["r_z"], b)
                        nc.scalar.activation(gate, lin[:, u, :], ACT.Tanh, scale=0.5).then_inc(S["r_tanh"], 1)
                    elif kind == "ln_b":
                        ln_apply(3 * NB + b)
                    elif kind == "wkv2":
                        act.wait_ge(S["r_arg1"], b + 1)
                        if b:
                            act.wait_ge(S["r_w"], b)
                        nc.scalar.activation(ex[:, 0:2, :], arg[:, 0:2, :], ACT.Exp).then_inc(S["r_exp1"], 1)
                    elif kind == "wkv3":
                        act.wait_ge(S["r_arg2"], b + 1)
                        nc.scalar.activation(ex[:, 2:4, :], arg[:, 2:4, :], ACT.Exp).then_inc(S["r_exp2"], 1)
            if LAYERS > 4:
                rotated()
            if LAYERS > 5:
                for t in range(TB):
                    act.wait_ge(S["i_sc"], t + 1)
                    if t >= 2:
                        act.wait_ge(S["i_pp"], NB * (t - 1))
                    nc.scalar.activation(pr[:, t % 2], sc[:, t % 2], ACT.Exp, scale=SCALE).then_inc(S["i_exp"], 1)
                for kind, b, n in last_layer():
                    if kind == "router":
                        act.wait_ge(S["i_ct"], b + 1)
                        if b >= 2:
                            act.wait_ge(S["i_out"], b - 1)
                        nc.scalar.copy(c_f[:, b % 2, :], ps[:, 4, :]).then_inc(S["i_cf"], 1)
                        ln_scale(n, b, ln_in[:, n % 2, :, :])
                        act.wait_ge(S["g_ht"], b + 1)
                        nc.scalar.copy(h_f[:, b, :], ps[:, 7, :]).then_inc(S["g_hf"], 1)
                        act.wait_ge(S["g_d"], b + 1)
                        nc.scalar.activation(gates[:, 2, :, :], gates[:, 1, :, :], ACT.Exp).then_inc(S["g_exp"], 1)
                        act.wait_ge(S["g_oht"], b + 1)
                        if b >= 2:
                            act.wait_ge(S["e_o"], (NE - 1) * (b - 1))
                        nc.scalar.copy(oh_f[:, b % 2, :], ps[0:NE, 4, :]).then_inc(S["g_ohf"], 1)
                        nc.scalar.copy(oh_b[:, b % 2, :], ps[0:NE, 4, :]).then_inc(S["g_ohf"], 1)
                    elif kind == "experts":
                        for e in range(1, NE):
                            m = (NE - 1) * b + e - 1
                            act.wait_ge(S["e_h"], m + 1)
                            if m >= 2:
                                act.wait_ge(S["e_o"], m - 1)
                            nc.scalar.activation(hid[:, m % 2, :], ps[:, m % 2, :], ACT.Gelu, bias=col(f"b1_{e}"))\
                                .then_inc(S["e_g"], 1)
                    else:
                        ln_scale(n, b, ln_in[:, n % 2, :, :])
                        ln_scale(n + 1, b, x_t[:, TB * b:TB * b + TB, :])

        @block.vector
        def _(dve):
            steps = [0]

            def after(ins):
                steps[0] += 1
                ins.then_inc(S["dve"], 1)
                dve.wait_ge(S["dve"], steps[0])

            def ln_stats(n, add):
                u = n % 2
                if n >= 2:
                    dve.wait_ge(S["ln_x"], TB * (n - 1))
                add(ln_in[:, u, :, :])
                for t in range(TB):
                    last = nc.vector.bn_stats(ln_st[:, u, t, :], ln_in[:, u, t, :])
                after(last)
                for t in range(TB):
                    last = nc.vector.bn_aggr(ln_mv[:, u, t, :], ln_st[:, u, t, :])
                last.then_inc(S["ln_mv"], 1)

            nc.vector.memset(ones[:, :], 1.0)
            nc.vector.memset(v_aug[:, :], 1.0)
            nc.vector.memset(q_st[:, :, :, :].rearrange("p a h q -> p (a h q)").bitcast(F32), 0.0)
            after(nc.vector.memset(k_st[:, :, :, :], 1.0))
            nc.vector.memset(consts[:, 0:1], EPS)
            nc.vector.memset(consts[:, 1:2], -0.5)
            after(nc.vector.memset(consts[:, 2:3], MAGIC))
            nc.vector.memset(consts[:, 3:4], -1.0).then_inc(S["setup_dve"], 1)

            for kind, i in self_attention():
                if kind == "proj":
                    bq, bk, bv = (0, 1, 2) if i == 0 else (3, 6, 7) if i == 1 else (7, 7, 7)
                    for w, bank, k in (("q", bq, 0), ("k", bk, 1)):
                        dve.wait_ge(S[w + "_hi"], i + 1)
                        pt = parts[:, 2 * (i % 2) + k]
                        nc.vector.tensor_tensor(rest[:, k, :], ps[:, bank, :], pt[:, 0, :], ALU.subtract)\
                            .then_inc(S[w + "_res"], 1)
                        dve.wait_ge(S[w + "_mid"], i + 1)
                        nc.vector.tensor_tensor(pt[:, 2, :], rest[:, k, :], pt[:, 1, :], ALU.subtract)\
                            .then_inc(S[w + "_lo"], 1)
                elif kind == "a":
                    u, r = divmod(i, HALF * TB)
                    if r == 0 and u >= 2:
                        dve.wait_ge(S["m_t"], u - 1)
                    dve.wait_ge(S["a_s"], i + 1)
                    nc.vector.tensor_reduce(max_t[:, u % 2, r % TB, r // TB:r // TB + 1], ps[:, 4 + i % 2, :], AX_X,
                                            ALU.max, negate=True).then_inc(S["a_max"], 1)
                elif kind == "max":
                    dve.wait_ge(S["m_hi"], i + 1)
                    mp = max_p[:, i % 2]
                    nc.vector.tensor_tensor(max_r[:, :], ps[0:HALF, 7, :], mp[:, 0, :], ALU.subtract)\
                        .then_inc(S["m_res"], 1)
                    dve.wait_ge(S["m_mid"], i + 1)
                    nc.vector.tensor_tensor(mp[:, 2, :], max_r[:, :], mp[:, 1, :], ALU.subtract)\
                        .then_inc(S["m_lo"], 1)
                elif kind == "norm":
                    b, q = divmod(i, 4)
                    dve.wait_ge(S["ott"], i + 1)
                    o = ps[:, 7, :].rearrange("p (t j e) -> p t j e", t=TB, j=4)
                    after(nc.vector.reciprocal(recip[:, i % 2, :, :], o[:, :, :, HD]))
                    nc.vector.tensor_tensor(
                        d_t[:, TB * b:TB * b + TB, 32 * q:32 * q + 32].rearrange("p t (j e) -> p t j e", j=4),
                        o[:, :, :, 0:HD], recip[:, i % 2, :, :].unsqueeze(3).to_broadcast([P, TB, 4, HD]),
                        ALU.mult).then_inc(S["attn"], 1)
                elif kind == "ln_a":
                    b = i
                    dve.wait_ge(S["attn"], 4 * (b + 1))
                    ln_stats(i, lambda y: after(nc.vector.tensor_tensor(
                        y, d_t[:, TB * b:TB * b + TB, :], x_t[:, TB * b:TB * b + TB, :], ALU.add)))

            def residues(n, src, width):
                pt = parts[:, n % 4]
                dve.wait_ge(S["x_hi"], n + 1)
                nc.vector.tensor_tensor(rest[:, n % 2, 0:width], src, pt[:, 0, 0:width], ALU.subtract)\
                    .then_inc(S["x_res"], 1)
                dve.wait_ge(S["x_mid"], n + 1)
                nc.vector.tensor_tensor(pt[:, 2, 0:width], rest[:, n % 2, 0:width], pt[:, 1, 0:width], ALU.subtract)\
                    .then_inc(S["x_lo"], 1)

            def divide(bank, n, b, quad):
                o = ps[:, bank, :].rearrange("p (t j e) -> p t j e", t=TB, j=4)
                after(nc.vector.reciprocal(recip[:, n % 2, :, :], o[:, :, :, HD]))
                return nc.vector.tensor_tensor(
                    d_t[:, TB * b:TB * b + TB, 32 * quad:32 * quad + 32].rearrange("p t (j e) -> p t j e", j=4),
                    o[:, :, :, 0:HD], recip[:, n % 2, :, :].unsqueeze(3).to_broadcast([P, TB, 4, HD]), ALU.mult)

            def cross():
                for kind, b, t in cross_attention():
                    n = TB * b + t
                    if kind in ("k", "q"):
                        n = 0 if kind == "k" else 1 + b
                        width = NCTX if kind == "k" else SEQ
                        residues(n, ps[:, n % 2, 0:width], width)
                    elif kind == "s":
                        z = zs[:, b % 2, t, :, :]
                        if t == 0 and b >= 2:
                            dve.wait_ge(S["x_pt"], 4 * (4 * (b - 1)))
                        for i in range(3):
                            lo, hi = 6 * i, min(6 * i + 6, NH)
                            dve.wait_ge(S["x_s"], 3 * n + i + 1)
                            nc.vector.scalar_tensor_tensor(
                                z[:, lo:hi, :], ps[:, i, 0:(hi - lo) * CTX].rearrange("p (h k) -> p h k", k=CTX),
                                SCALE, mask[:, t:t + 1, :].to_broadcast([P, hi - lo, CTX]), ALU.mult, ALU.add)\
                                .then_inc(S["x_z"], 1)
                        dve.wait_ge(S["x_z"], 3 * (n + 1))
                        if n >= 2:
                            dve.wait_ge(S["x_sub"], n - 1)
                        nc.vector.tensor_reduce(x_mx[:, n % 2, :], z, AX_X, ALU.max).then_inc(S["x_mx"], 1)
                    elif kind == "pt":
                        dve.wait_ge(S["x_pt"], 4 * n + 4)
                        if n >= 2:
                            dve.wait_ge(S["x_pv"], n - 1)
                        nc.vector.tensor_copy(pt_b[:, n % 2, 3, :], ps[0:CTX, 4, :]).then_inc(S["x_pd"], 1)
                    elif kind == "norm":
                        dve.wait_ge(S["x_ott"], n + 1)
                        divide(6, n, b, t).then_inc(S["x_attn"], 1)
                    elif kind == "wo":
                        dve.wait_ge(S["x_wo"], b + 1)
                        ln_stats(NB + b, lambda y: after(nc.vector.tensor_tensor(
                            y, tiles(7), x_t[:, TB * b:TB * b + TB, :], ALU.add)))

            def rotated():
                after(nc.vector.memset(kr_st[:, :, :, :], 1.0))
                for kind, i in rotated_attention():
                    if kind in ("k", "q"):
                        n = 5 if kind == "k" else 6 + i
                        width = NCTX if kind == "k" else SEQ
                        dve.wait_ge(S["x_raw"], n + 1)
                        if n > 5:
                            dve.wait_ge(S["x_hi"], n)
                        for j, nm in ((0, "c" + kind + "_b"), (1, "c" + kind + "s_b")):
                            bank = 2 * j + n % 2
                            if kind == "k":
                                o_, s_ = (a.rearrange("p (b k) -> p b k", b=NB)
                                          for a in (rp[:, j, 0:width], ps[:, bank, 0:width]))
                                tab = rope_k[:, j:j + 1, :].to_broadcast([P, NB, CTX])
                            else:
                                o_, s_, tab = rp[:, j, :], ps[:, bank, :], rope_q[:, j, :]
                            last = nc.vector.scalar_tensor_tensor(o_, s_, col(nm), tab, ALU.add, ALU.mult)
                        after(last)
                        nc.vector.tensor_tensor(rp[:, 2, 0:width], rp[:, 0, 0:width], rp[:, 1, 0:width],
                                                ALU.add).then_inc(S["x_rope"], 1)
                        residues(n, rp[:, 2, 0:width], width)
                        if kind == "k":
                            dve.wait_ge(S["x_vraw"], 2)
                            nc.vector.tensor_tensor(
                                v_heads[0:CTX, 0:NB, :, 0:HD],
                                ps[0:CTX, 4, :].rearrange("p (t h e) -> p t h e", t=NB, h=NH),
                                rows[0:CTX, ROWS.index("cv_b"), :].rearrange("p (h e) -> p h e", h=NH)
                                .unsqueeze(1).to_broadcast([CTX, NB, NH, HD]), ALU.add).then_inc(S["x_v"], 1)
                    elif kind == "a":
                        b, t = divmod(i, TB)
                        if t == 0 and b >= 2:
                            dve.wait_ge(S["m_t"], 2 * NB + b - 1)
                        for j in range(3):
                            lo, hi = 6 * j, min(6 * j + 6, NH)
                            dve.wait_ge(S["c_s"], 3 * i + j + 1)
                            nc.vector.tensor_reduce(
                                cm_t[:, b % 2, t, lo:hi],
                                ps[:, 4 + (3 * i + j) % 2, 0:(hi - lo) * CTX].rearrange("p (h k) -> p h k", k=CTX),
                                AX_X, ALU.max, negate=True).then_inc(S["c_mx"], 1)
                    elif kind == "max":
                        mp = cm_p[:, i % 2]
                        dve.wait_ge(S["m_hi"], 2 * NB + i + 1)
                        nc.vector.tensor_tensor(cm_r[:, :], ps[0:NH, 7, :], mp[:, 0, :], ALU.subtract)\
                            .then_inc(S["m_res"], 1)
                        dve.wait_ge(S["m_mid"], 2 * NB + i + 1)
                        nc.vector.tensor_tensor(mp[:, 2, :], cm_r[:, :], mp[:, 1, :], ALU.subtract)\
                            .then_inc(S["m_lo"], 1)
                    elif kind == "norm":
                        dve.wait_ge(S["x_ott"], NT + i + 1)
                        divide(7, i, i // 4, i % 4).then_inc(S["x_attn"], 1)
                    elif kind == "wo":
                        dve.wait_ge(S["x_wo"], NB + i + 1)

                        def add(y, b=i):
                            after(nc.vector.tensor_tensor(y, tiles(7), row("co_b", TB), ALU.add))
                            after(nc.vector.tensor_tensor(y, y, x_t[:, TB * b:TB * b + TB, :], ALU.add))
                        ln_stats(4 * NB + i, add)

            if LAYERS > 1:
                cross()
            if LAYERS > 2:
                TH, SP_ = 1.0, [0.9, 0.2]
                for b in range(NB + 1):
                    if b < NB:
                        for f in range(FC):
                            n = FC * b + f
                            dve.wait_ge(S["f_r"], n + 1)
                            if b >= 2 and f == 0:
                                dve.wait_ge(S["f_yraw"], b - 1)
                            nc.vector.tensor_tensor(fh[:, b % 2, f, :], fr[:, n % 2, :], fr[:, n % 2, :], ALU.mult)\
                                .then_inc(S["f_sq"], 1)
                    if b > 0:
                        c = b - 1
                        stt = nc.vector.scalar_tensor_tensor
                        y = fy[:, c % 2, :]
                        dve.wait_ge(S["f_y"], c + 1)
                        nc.vector.tensor_scalar(fs[:, 0, :], y, TH, None, ALU.is_gt)
                        after(stt(fs[:, 1, :], y, SP_[0], y, ALU.mult, ALU.add))
                        after(stt(fs[:, 2, :], y, TH, fs[:, 1, :], ALU.is_gt, ALU.subtract))
                        acc, m, t_ = 0, 2, 1
                        for k in range(3):
                            new_acc, u_ = 3 + k % 2, 1
                            stt(fs[:, new_acc, :], fs[:, m, :], -TH, fs[:, acc, :], ALU.is_lt, ALU.add)
                            after(stt(fs[:, 1, :], fs[:, m, :], SP_[0], y, ALU.mult, ALU.subtract))
                            new_m = 5 if m == 2 else 2
                            after(stt(fs[:, new_m, :], fs[:, m, :], -TH, fs[:, 1, :], ALU.is_lt, ALU.add))
                            acc, m = new_acc, new_m
                        after(stt(fs[:, 0, :], fs[:, m, :], -TH, fs[:, acc, :], ALU.is_lt, ALU.add))
                        ln_stats(2 * NB + c, lambda o: after(stt(
                            o, fs[:, 0, :].rearrange("p (t c) -> p t c", t=TB), SP_[1],
                            x_t[:, TB * c:TB * c + TB, :], ALU.mult, ALU.add)))
            if LAYERS > 3:
                stt, tt, ts = nc.vector.scalar_tensor_tensor, nc.vector.tensor_tensor, nc.vector.tensor_scalar
                dve.wait_ge(S["r_sum"], 1)
                after(ts(w_mean[:, :], ps[:, 6, 0:4], 1.0 / (P * P), 1e-5, ALU.mult, ALU.max))
                after(nc.vector.reciprocal(w_inv[:, :], w_mean[:, :]))
                for w in range(4):
                    t = arg[:, 0, w * P:(w + 1) * P]
                    after(ts(t, mat("r" + "kvro"[w]), w_inv[:, w:w + 1], MAGIC, ALU.mult, ALU.add))
                    after(ts(t, t, MAGIC, 1.0, ALU.subtract, ALU.min))
                    ts(w_q[:, w, :], t, -1.0, None, ALU.max).then_inc(S["r_wq"], 1)
                ts(mix_c[:, :], cols[:, 2:5], -1.0, 1.0, ALU.mult, ALU.add)
                nc.vector.memset(alpha[:, 0:1], 0.0)
                nc.vector.memset(beta[:, 0:1], 0.0)
                nc.vector.memset(eps[:, 0:1], 0.0)
                nc.vector.memset(mixed[:, :, 0:1], 0.0)
                dve.wait_ge(S["r_eps"], 1)
                after(ts(log_w[:, 1:2], log_w[:, 0:1], -1.0, None, ALU.mult))
                freed = {}
                for kind, n, b, w in recurrent():
                    u = n % 2
                    as_tiles = lambda a: a.rearrange("p (t c) -> p t c", t=TB)
                    k, v = key_f[:, b % 2, :], val_f[:, b % 2, :]
                    first, lw = col("first"), log_w[:, 1:2]
                    was, now = eps[:, 0:SEQ], eps[:, 1:SEQ + 1]
                    if kind == "mix":
                        if w < 3:
                            if w == 0:
                                dve.wait_ge(S["ln_f"], 2 * NB + b + 1)
                            m = mixed[:, u, :]
                            if n >= 2:
                                dve.wait_ge(S["r_zt"], n - 1)
                            ts(m[:, 0:1], x_f[:, b, 0:1], 0.0, None, ALU.mult)
                            after(ts(m[:, 1:SEQ], x_f[:, b, 0:SEQ - 1], mix_c[:, w:w + 1], None, ALU.mult))
                            stt(m, x_f[:, b, :], cols[:, 2 + w:3 + w], m, ALU.mult, ALU.add).then_inc(S["r_mix"], 1)
                        else:
                            dve.wait_ge(S["r_tanh"], b + 1)
                            after(ts(gate, gate, 0.5, 0.5, ALU.mult, ALU.add))
                    elif kind == "rms":
                        rms = row("rms_" + "kvro"[w], TB)
                        if n >= 2:
                            dve.wait_ge(S["r_q"], TB * (n - 1))
                        dve.wait_ge(S["r_zt"], n + 1)
                        if w < 3:
                            tt(as_tiles(weighed[:, u, :]), tiles(n % 2), rms, ALU.mult).then_inc(S["r_u"], 1)
                        else:
                            tt(gated, tiles(n % 2), as_tiles(gate), ALU.mult).then_inc(S["r_z"], 1)
                            dve.wait_ge(S["r_z"], b + 1)
                            tt(as_tiles(weighed[:, u, :]), gated, rms, ALU.mult).then_inc(S["r_u"], 1)
                    elif kind == "sums":
                        dve.wait_ge(S["r_u"], n + 1)
                        nc.vector.tensor_reduce(tok[:, u, 1, :], as_tiles(weighed[:, u, :]), AX_X, ALU.max,
                                                apply_absolute_value=True)
                        dve.wait_ge(S["r_sq"], n + 1)
                        nc.vector.tensor_reduce(tok[:, u, 0, :], as_tiles(squares[:, u, :]), AX_X, ALU.add)\
                            .then_inc(S["r_ss"], 1)
                    elif kind == "scale":
                        dve.wait_ge(S["r_is"], n + 1)
                        after(nc.vector.reciprocal(tok[:, u, 6, :], tok[:, u, 4, :]))
                        tt(tok[:, u, 7, :], tok[:, u, 4, :], w_mean[:, w:w + 1].to_broadcast([P, TB]), ALU.mult)
                        tt(tok[:, u, 5, :], tok[:, u, 6, :], tok[:, u, 2, :], ALU.mult).then_inc(S["r_r2"], 1)
                    elif kind == "quant":
                        dve.wait_ge(S["r_q"], TB * (n + 1))
                        if n >= 2:
                            dve.wait_ge(S["r_xt"], n - 1)
                        ts(x_q[:, u, :], shifted_q[:, u, :], MAGIC, 127.0, ALU.subtract, ALU.min)\
                            .then_inc(S["r_xq"], 1)
                    elif kind == "lin":
                        dve.wait_ge(S["r_mm"], n + 1)
                        if u in freed:
                            dve.wait_ge(*freed.pop(u))
                        if w < 3:
                            freed[u] = (S["r_ktt"], 2 * b + w + 1) if w < 2 else (S["r_tanh"], b + 1)
                        tt(as_tiles(lin[:, u, :]), tiles(3), per_token(tok[:, u, 7, :]), ALU.mult)\
                            .then_inc(S["r_kt"], 1)
                        if w == 3:
                            dve.wait_ge(S["r_kt"], n + 1)
                            ln_stats(3 * NB + b, lambda y: after(tt(
                                y, as_tiles(lin[:, u, :]), x_t[:, TB * b:TB * b + TB, :], ALU.add)))
                    elif kind == "wkv1":
                        dve.wait_ge(S["r_kf"], 2 * b + 2)
                        after(nc.vector.tensor_tensor_scan(now, lw.to_broadcast([P, SEQ]), k, 0.0, ALU.add, ALU.max))
                        stt(arg[:, 0, :], was, lw, now, ALU.add, ALU.subtract)
                        tt(arg[:, 1, :], k, now, ALU.subtract).then_inc(S["r_arg1"], 1)
                    elif kind == "wkv2":
                        after(stt(wkv, k, first, was, ALU.add, ALU.max))
                        tt(arg[:, 2, :], was, wkv, ALU.subtract)
                        stt(arg[:, 3, :], k, first, wkv, ALU.add, ALU.subtract).then_inc(S["r_arg2"], 1)
                    elif kind == "wkv3":
                        dve.wait_ge(S["r_exp1"], b + 1)
                        nc.vector.tensor_tensor_scan(beta[:, 1:], ex[:, 0, :], ex[:, 1, :], 0.0, ALU.mult, ALU.add)
                        after(tt(arg[:, 0, :], ex[:, 1, :], v, ALU.mult))
                        after(nc.vector.tensor_tensor_scan(alpha[:, 1:], ex[:, 0, :], arg[:, 0, :], 0.0, ALU.mult,
                                                           ALU.add))
                    elif kind == "wkv4":
                        dve.wait_ge(S["r_exp2"], b + 1)
                        tt(arg[:, 1, :], ex[:, 2, :], beta[:, 0:SEQ], ALU.mult)
                        tt(arg[:, 2, :], ex[:, 2, :], alpha[:, 0:SEQ], ALU.mult)
                        after(tt(arg[:, 3, :], ex[:, 3, :], v, ALU.mult))
                        tt(arg[:, 0, :], arg[:, 1, :], ex[:, 3, :], ALU.add)
                        after(tt(arg[:, 2, :], arg[:, 2, :], arg[:, 3, :], ALU.add))
                        after(nc.vector.reciprocal(arg[:, 1, :], arg[:, 0, :]))
                        tt(wkv, arg[:, 2, :], arg[:, 1, :], ALU.mult).then_inc(S["r_w"], 1)
            if LAYERS > 4:
                rotated()
            if LAYERS > 5:
                i0 = ROWS.index("iq_b")
                for b in range(NB):
                    for t in range(TB):
                        g = TB * b + t
                        dve.wait_ge(S["i_raw"], g + 1)
                        tt(qkv[:, b, t, :], ps[:, g % 3, 0:3 * P],
                           rows[:, i0:i0 + 3, :].rearrange("p i c -> p (i c)"), ALU.add).then_inc(S["i_qkv"], 1)
                dve.wait_ge(S["i_qkv"], NT)
                all_pairs = [P, NB, NB, NH]
                for t in range(TB + 1):
                    if t < TB:
                        u = t % 2
                        after(tt(prod[:, u], qkv[:, :, t, 0:P].unsqueeze(2).to_broadcast([P, NB, NB, P]),
                                 qkv[:, :, t, P:2 * P].unsqueeze(1).to_broadcast([P, NB, NB, P]), ALU.mult))
                        after(nc.vector.tensor_reduce(sc[:, u].rearrange("p q s h -> p (q s h)"),
                                                      prod[:, u].rearrange("p q s (h e) -> p (q s h) e", h=NH),
                                                      AX_X, ALU.add))
                        most, total, inv = sc_n[:, 3 * u], sc_n[:, 3 * u + 1], sc_n[:, 3 * u + 2]
                        after(nc.vector.tensor_reduce(most, sc[:, u].rearrange("p q s h -> p q h s"), AX_X, ALU.max))
                        tt(sc[:, u], sc[:, u], most.unsqueeze(2).to_broadcast(all_pairs), ALU.subtract)\
                            .then_inc(S["i_sc"], 1)
                        dve.wait_ge(S["i_exp"], t + 1)
                        after(nc.vector.tensor_reduce(total, pr[:, u].rearrange("p q s h -> p q h s"), AX_X, ALU.add))
                        after(nc.vector.reciprocal(inv, total))
                        tt(pr[:, u], pr[:, u], inv.unsqueeze(2).to_broadcast(all_pairs), ALU.mult)\
                            .then_inc(S["i_p"], 1)
                    if t > 0:
                        for q in range(NB):
                            dve.wait_ge(S["i_pp"], NB * (t - 1) + q + 1)
                            nc.vector.tensor_reduce(d_t[:, TB * q + t - 1, :],
                                                    pv_t[:, (t - 1) % 2, q].rearrange("p s c -> p c s"),
                                                    AX_X, ALU.add).then_inc(S["i_ctx"], 1)
                for kind, b, n in last_layer():
                    xb, hb = x_t[:, TB * b:TB * b + TB, :], h_t[:, TB * b:TB * b + TB, :]
                    if kind == "router":
                        dve.wait_ge(S["i_out"], b + 1)

                        def add(y):
                            after(tt(y, tiles(5), row("io_b", TB), ALU.add))
                            after(tt(y, y, xb, ALU.add))
                        ln_stats(n, add)
                        dve.wait_ge(S["ln_x"], TB * (n + 1))
                        after(tt(hb, ln_in[:, n % 2, :, :], row("ln1_g", TB), ALU.mult))
                        tt(hb, hb, row("ln1_b", TB), ALU.add).then_inc(S["ln_g"], 1)
                        dve.wait_ge(S["g_raw"], b + 1)
                        g = [gates[:, i, :, :] for i in range(16)]
                        one = [g[12][:, :, i] for i in range(4)]
                        wide = lambda a: a.unsqueeze(2).to_broadcast([P, TB, NE])
                        after(tt(g[0], ps[:, 6, 0:TB * NE].rearrange("p (t e) -> p t e", t=TB),
                                 rows[:, ROWS.index("router_b"), 0:TB * NE].rearrange("p (t e) -> p t e", t=TB),
                                 ALU.add))
                        after(nc.vector.tensor_reduce(one[0], g[0], AX_X, ALU.max))
                        tt(g[1], g[0], wide(one[0]), ALU.subtract).then_inc(S["g_d"], 1)
                        dve.wait_ge(S["g_exp"], b + 1)
                        after(nc.vector.tensor_reduce(one[1], g[2], AX_X, ALU.add))
                        after(nc.vector.reciprocal(one[2], one[1]))
                        after(tt(g[3], g[2], wide(one[2]), ALU.mult))
                        p_i, p_j = (g[3].unsqueeze(a).to_broadcast([P, TB, NE, NE]) for a in (3, 2))
                        tt(rank[:, 0], p_j, p_i, ALU.is_ge)
                        after(tt(rank[:, 1], p_j, p_i, ALU.is_gt))
                        after(tt(rank[:, 0], rank[:, 0], rank[:, 1], ALU.subtract))
                        after(tt(rank[:, 2], rank[:, 0],
                                 tri[:, :].rearrange("p (e f) -> p e f", e=NE).unsqueeze(1)
                                 .to_broadcast([P, TB, NE, NE]), ALU.mult))
                        after(tt(rank[:, 0], rank[:, 2], rank[:, 1], ALU.add))
                        after(nc.vector.tensor_reduce(g[4], rank[:, 0], AX_X, ALU.add))
                        numbers = iota[:, :].unsqueeze(1).to_broadcast([P, TB, NE])
                        after(stt(g[5], g[4], 1.5, numbers, ALU.is_lt, ALU.mult))
                        after(nc.vector.tensor_reduce(one[3], g[5], AX_X, ALU.max))
                        if b >= 2:
                            dve.wait_ge(S["g_oht"], b - 1)
                        tt(g[8 + b % 2], numbers, wide(one[3]), ALU.is_equal).then_inc(S["g_oh"], 1)
                    elif kind == "norms":
                        dve.wait_ge(S["e_o"], (NE - 1) * (b + 1))
                        ln_stats(n, lambda y: after(tt(y, tiles(2 + b % 2), hb, ALU.add)))
                        dve.wait_ge(S["ln_x"], TB * (n + 1))
                        m = ln_in[:, n % 2, :, :]
                        after(tt(m, m, row("ln2_g", TB), ALU.mult))
                        after(tt(m, m, row("ln2_b", TB), ALU.add))
                        ln_stats(n + 1, lambda y: after(tt(y, m, xb, ALU.add)))

        @block.gpsimd
        def _(pool):
            steps = [0]

            def after(ins):
                steps[0] += 1
                ins.then_inc(S["pool"], 1)
                pool.wait_ge(S["pool"], steps[0])

            pool.wait_ge(S["load_s"], 16 * N_SMALL)
            nc.gpsimd.tensor_copy(ident_b[:, :], mat("ident")).then_inc(S["setup"], 1)

            def ln_scales(n):
                u = n % 2
                pool.wait_ge(S["ln_mv"], n + 1)
                mean, var = ln_mv[:, u, :, 0], ln_mv[:, u, :, 1]
                r = ln_rs[:, u, :, :]
                after(nc.gpsimd.tensor_tensor(r[:, :, 0], var, consts[:, 0:1].to_broadcast([P, TB]), ALU.add))
                after(nc.gpsimd.tensor_tensor(r[:, :, 1], r[:, :, 0], consts[:, 1:2].to_broadcast([P, TB]), ALU.pow))
                after(nc.gpsimd.tensor_tensor(r[:, :, 2], mean, r[:, :, 1], ALU.mult))
                nc.gpsimd.tensor_tensor(r[:, :, 3], r[:, :, 2], consts[:, 3:4].to_broadcast([P, TB]), ALU.mult)\
                    .then_inc(S["ln_rs"], 1)

            pool.wait_ge(S["setup_dve"], 1)
            for kind, i in self_attention():
                if kind == "ln_a":
                    ln_scales(i)

            def cross():
                for kind, b, t in cross_attention():
                    if kind == "s":
                        n = TB * b + t
                        z = zs[:, b % 2, t, :, :]
                        pool.wait_ge(S["x_mx"], n + 1)
                        nc.gpsimd.tensor_tensor(z, z, x_mx[:, n % 2, :].unsqueeze(2).to_broadcast([P, NH, CTX]),
                                                ALU.subtract).then_inc(S["x_sub"], 1)
                    elif kind == "wo":
                        ln_scales(NB + b)

            def rotated():
                for kind, i in rotated_attention():
                    if kind == "wo":
                        ln_scales(4 * NB + i)

            if LAYERS > 1:
                cross()
            if LAYERS > 2:
                for b in range(NB):
                    ln_scales(2 * NB + b)
            if LAYERS > 3:
                tt, ts = nc.gpsimd.tensor_tensor, nc.gpsimd.tensor_scalar
                for kind, n, b, w in recurrent():
                    k = tok[:, n % 2, :, :]
                    if kind == "sums":
                        pool.wait_ge(S["r_ss"], n + 1)
                        after(ts(k[:, 3, :], k[:, 0, :], 1.0 / P, 1e-8, ALU.mult, ALU.add))
                        after(tt(k[:, 2, :], k[:, 3, :], consts[:, 1:2].to_broadcast([P, TB]), ALU.pow))
                        after(tt(k[:, 6, :], k[:, 1, :], k[:, 2, :], ALU.mult))
                        ts(k[:, 4, :], k[:, 6, :], 1e-5, 1.0 / 127.0, ALU.max, ALU.mult).then_inc(S["r_is"], 1)
                    elif kind == "lin" and w == 3:
                        ln_scales(3 * NB + b)
            if LAYERS > 4:
                rotated()
            if LAYERS > 5:
                for t in range(TB):
                    for q in range(NB):
                        pool.wait_ge(S["i_p"], t + 1)
                        if t >= 2:
                            pool.wait_ge(S["i_ctx"], NB * (t - 2) + q + 1)
                        tt(pv_t[:, t % 2, q].rearrange("p s (h e) -> p s h e", h=NH),
                           pr[:, t % 2, q].unsqueeze(3).to_broadcast([P, NB, NH, HD]),
                           qkv[:, :, t, 2 * P:3 * P].rearrange("p s (h e) -> p s h e", h=NH), ALU.mult)\
                            .then_inc(S["i_pp"], 1)
                for kind, b, n in last_layer():
                    if kind == "router":
                        ln_scales(n)
                    elif kind == "norms":
                        ln_scales(n)
                        ln_scales(n + 1)


def head_last(w):
    return w.reshape(*w.shape[:-1], NH, HD).swapaxes(-1, -2).reshape(w.shape)


def swapped(w):
    return np.roll(w, P // 2, axis=-1)


def rope_tables():
    out = []
    inv = (1.0 / 10000.0 ** (np.arange(0, HD, 2, dtype=np.float32) / HD)).astype(np.float32)
    for n in (SEQ, CTX):
        t = np.arange(n, dtype=np.float32)
        f = np.outer((10.0 * (t / n)).astype(np.float32), inv).astype(np.float32).T
        cos, sin = np.cos(f), np.sin(f)
        tab = np.stack([np.concatenate([cos, cos]), np.concatenate([-sin, sin])], 1)
        out.append(np.repeat(tab, NH, axis=0).astype(np.float32))
    return out


def lay_out(i):
    f = {k: np.asarray(v) for k, v in i.items()}
    cq, ck = head_last(f["L1_xattn_Wq"].T), head_last(f["L1_xattn_Wk"].T)
    bq, bk = head_last(f["L1_xattn_bq"]), head_last(f["L1_xattn_bk"])
    inp, inb = f["L1_ffn_in_proj_w"].T, f["L1_ffn_in_proj_b"]
    fc, pj = f["L0_ffn_W_fc"].T, f["L0_ffn_W_proj"].T
    mats = {"q0": head_last(f["L0_attn_w_Q"]), "k0": head_last(f["L0_attn_w_K"]), "v0": f["L0_attn_w_V"],
            "xq": head_last(f["L0_xattn_wq"]), "xk": head_last(f["L0_xattn_wk"]), "xv": f["L0_xattn_wv"],
            "xo": f["L0_xattn_wo"], "rk": f["L1_attn_w_key"].T, "rv": f["L1_attn_w_value"].T,
            "rr": f["L1_attn_w_receptance"].T, "ro": f["L1_attn_w_output"].T,
            "cq": cq, "cqs": swapped(cq), "ck": ck, "cks": swapped(ck), "cv": f["L1_xattn_Wv"].T,
            "co": f["L1_xattn_Wo"].T, "iq": inp[:, 0:P], "ik": inp[:, P:2 * P], "iv": inp[:, 2 * P:],
            "io": f["L1_ffn_out_w"].T, "ident": np.eye(P, dtype=np.float32)}
    for c in range(FC):
        mats[f"fc{c}"] = fc[:, c * P:(c + 1) * P]
        mats[f"pj{c}"] = pj[c * P:(c + 1) * P, :]
    for e in range(NE):
        mats[f"w1_{e}"], mats[f"w2_{e}"] = f["L1_ffn_w1"][e].T, f["L1_ffn_w2"][e].T
    rows = {"cv_b": f["L1_xattn_bv"], "co_b": f["L1_xattn_bo"], "iq_b": inb[0:P], "ik_b": inb[P:2 * P],
            "iv_b": inb[2 * P:], "io_b": f["L1_ffn_out_b"], "ln1_g": f["L1_ffn_ln1_g"], "ln1_b": f["L1_ffn_ln1_b"],
            "ln2_g": f["L1_ffn_ln2_g"], "ln2_b": f["L1_ffn_ln2_b"], "rms_k": f["L1_attn_rms_key"],
            "rms_v": f["L1_attn_rms_value"], "rms_r": f["L1_attn_rms_receptance"], "rms_o": f["L1_attn_rms_output"],
            "router_b": np.tile(f["L1_ffn_router_b"], P // NE)}
    cols = {"decay": f["L1_attn_time_decay"], "first": f["L1_attn_time_first"],
            "mix_k": f["L1_attn_time_mix_key"].reshape(P), "mix_v": f["L1_attn_time_mix_value"].reshape(P),
            "mix_r": f["L1_attn_time_mix_receptance"].reshape(P),
            "cq_b": bq, "cqs_b": swapped(bq), "ck_b": bk, "cks_b": swapped(bk)}
    for e in range(NE):
        cols[f"b1_{e}"] = f["L1_ffn_b1"][e]
    rope_q, rope_k = rope_tables()
    pen = np.full((NE, NE, P), PENALTY, np.float32)
    pen[np.arange(NE), np.arange(NE)] = 0
    x = f["x"]
    out = {
        "x_t": x.reshape(NT, P, P).transpose(1, 0, 2), "x_f": x.transpose(2, 0, 1),
        "ctx_f": f["ctx_1024"].transpose(2, 0, 1).reshape(P, NCTX),
        "mask": f["mask_1x1xSxS2_ff0"].reshape(TB, P, CTX).transpose(1, 0, 2),
        "mats": np.stack([mats[n] for n in MATS], 1), "rows": np.stack([rows[n] for n in ROWS]),
        "cols": np.stack([cols[n] for n in COLS], 1), "router": f["L1_ffn_router_w"].T, "b2": f["L1_ffn_b2"],
        "rope_q": rope_q, "rope_k": rope_k,
        "tri": np.tile(np.tril(np.ones((NE, NE), np.float32), -1).reshape(1, -1), (P, 1)),
        "iota": np.tile(np.arange(NE, dtype=np.float32), (P, 1)),
        "pen": pen.astype(mybir.dt.np(BF16)),
    }
    return {k: np.ascontiguousarray(v) for k, v in out.items()}


def kernel(**inputs):
    import concourse.bacc as bacc
    from concourse.bass_utils import run_bass_kernel_spmd

    arrays = lay_out(inputs)
    nc = bacc.Bacc("TRN2", target_bir_lowering=False, num_devices=1)
    d = {n: nc.dram_tensor("in_" + n, a.shape, mybir.dt.from_np(a.dtype), kind="ExternalInput").ap()
         for n, a in arrays.items()}
    d["out"] = nc.dram_tensor("out_x", (NB, SEQ, P), F32, kind="ExternalOutput").ap()
    transformer(nc, d)
    r = run_bass_kernel_spmd(nc, [{"in_" + n: a for n, a in arrays.items()}], core_ids=[0])
    return r.results[0]["out_x"]
```

```python
from contextlib import ExitStack

import numpy as np
import concourse.bass as bass
from concourse import mybir

ALU = mybir.AluOpType
ACT = mybir.ActivationFunctionType
F32 = mybir.dt.float32
BF16 = mybir.dt.bfloat16
AX_X = mybir.AxisListType.X

P = 128
NB = 4
SEQ = 512
TB = SEQ // P
NT = NB * TB
NH = 16
HD = P // NH
CTX = 77
NCTX = NB * CTX
SCALE = HD ** -0.5
FC = 4
NE = 8
EPS = 1e-5
MAGIC = 1.5 * 2.0 ** 23
PENALTY = -1e30
NEG_LANES = 32

Q_PART = (0, 0, 1, 1, 0, 2)
K_PART = (0, 1, 0, 1, 2, 0)
SLOTS = len(Q_PART)
STACK = SLOTS * HD
MAX_ROW = P - 3

FFN_LN = 1
EARLY = (100, 104, 108, 116)
ROUND = (4, 5, 7)
HALF = NH // 2

MATS = ["q0", "k0", "v0", "xq", "xk", "xv", "xo", "fc0", "fc1", "fc2", "fc3", "pj0", "pj1", "pj2", "pj3",
        "rk", "rv", "rr", "ro", "cq", "cqs", "ck", "cks", "cv", "co", "iq", "ik", "iv", "io"]
MATS += [f"w1_{e}" for e in range(NE)] + [f"w2_{e}" for e in range(NE)] + ["ident"]
ROWS = ["cv_b", "co_b", "iq_b", "ik_b", "iv_b", "io_b", "ln1_g", "ln1_b", "ln2_g", "ln2_b",
        "rms_k", "rms_v", "rms_r", "rms_o", "router_b"]
COLS = ["decay", "first", "mix_k", "mix_v", "mix_r", "cq_b", "cqs_b", "ck_b", "cks_b"]
COLS += [f"b1_{e}" for e in range(NE)]


def transformer(nc, d):
    ctx = ExitStack()
    with ctx:
        def sb(name, shape, dt=F32):
            return ctx.enter_context(nc.sbuf_tensor(name, shape, dt))

        mats = sb("mats", [P, len(MATS), P])
        rows = sb("rows", [P, len(ROWS), P])
        cols = sb("cols", [P, len(COLS)])
        router = sb("router", [P, NE])
        b2 = sb("b2", [NE, P])
        ctx_f = sb("ctx_f", [P, NCTX])
        mask = sb("mask", [P, TB, CTX])
        rope_q = sb("rope_q", [P, 2, SEQ])
        rope_k = sb("rope_k", [P, 2, CTX])
        tri = sb("tri", [P, NE * NE])
        iota = sb("iota", [P, NE])
        ident_b = sb("ident_b", [P, P], BF16)
        ones = sb("ones", [P, P])
        pen = sb("pen", [NE, NE, P], BF16)
        consts = sb("consts", [P, 4])
        x_t = sb("x_t", [P, NT, P])
        x_f = sb("x_f", [P, NB, SEQ])
        d_t = sb("d_t", [P, NT, P])
        ln_in = sb("ln_in", [P, 2, TB, P])
        ln_st = sb("ln_st", [P, 2, TB, 6])
        ln_mv = sb("ln_mv", [P, 2, TB, 2])
        ln_rs = sb("ln_rs", [P, 2, TB, 4])
        parts = sb("parts", [P, 4, 3, SEQ], BF16)
        rest = sb("rest", [P, 2, SEQ])
        v_aug = sb("v_aug", [P, NT * NH * (HD + 1) + NEG_LANES])
        o_f = sb("o_f", [P, 2, SEQ])
        recip = sb("recip", [P, 2, TB, 4])
        q_st = sb("q_st", [P, 2, NH, SEQ], BF16)
        max_t = sb("max_t", [P, 2, TB, HALF])
        max_p = sb("max_p", [HALF, 2, 3, SEQ], BF16)
        max_r = sb("max_r", [HALF, SEQ])
        w_q = sb("w_q", [P, 4, P], BF16)
        w_abs = sb("w_abs", [P, 4])
        w_mean = sb("w_mean", [P, 4])
        w_inv = sb("w_inv", [P, 4])
        mix_c = sb("mix_c", [P, 3])
        log_w = sb("log_w", [P, 2])
        tok = sb("tok", [P, 2, 8, TB])
        arena = sb("arena", [P, 16384])

        ps = ctx.enter_context(nc.psum_tensor("ps", [P, 8, 512], F32))

        names = """load_x load_x1 load_w load_s setup setup_dve q_raw k_raw v_raw q_hi k_hi v_sb q_mid k_mid q_res
            k_res q_lo k_lo a_s a_max m_t m_hi m_res m_mid m_lo st exp pv ot ott attn ln_mv ln_rs ln_x ln_g
            ln_t ln_f x_raw x_rope x_hi x_res x_mid x_lo x_vraw x_v x_s x_z x_mx x_sub x_p x_pt x_pa x_pd
            x_pv c_s c_mx c_st c_exp x_ot x_ott x_attn x_at x_af x_wo f_h f_r f_sq f_yraw f_y r_abs r_sum
            r_wq r_mix r_zt r_u r_sq r_ss r_is r_r2 r_q r_xq r_xt r_xf r_mm r_kt r_ktt r_kf r_eps r_arg1
            r_exp1 r_ev r_arg2 r_exp2 r_w r_z r_tanh i_raw i_qkv i_sc i_exp i_p i_pp i_ct i_cf i_out g_ht
            g_hf g_raw g_d g_exp g_oh g_oht g_ohf e_h e_g e_o out dve pool""".split()
        names += [f"stack_dma{b}" for b in range(NB)] + [f"m_dma{u}" for u in range(2 * NB)]
        names += [f"x_dma{n}" for n in range(2 * (NB + 1))]
        S = {n: ctx.enter_context(nc.semaphore("s_" + n)) for n in names}

        def mat(n):
            return mats[:, MATS.index(n), :]

        def row(n, tiles):
            return rows[:, ROWS.index(n):ROWS.index(n) + 1, :].to_broadcast([P, tiles, P])

        def col(n):
            return cols[:, COLS.index(n):COLS.index(n) + 1]

        def per_token(ap, width=P):
            return ap.unsqueeze(2).to_broadcast([P, ap.shape[1], width])

        def tiles(bank):
            return ps[:, bank, :].rearrange("p (t c) -> p t c", t=TB)

        VW = NH * (HD + 1)
        v_heads = v_aug[:, 0:NT * VW].rearrange("p (g h e) -> p g h e", g=NT, h=NH)

        def v_lhs(rows_, g, h):
            at = g * VW + h * (HD + 1)
            return v_aug[0:rows_, at:at + NEG_LANES]

        def stack(t, b, rows_, h, lo, hi):
            at = 64 * (b % 2)
            return t[at:at + rows_, b // 2, h, lo:hi]

        def tall(t, b, rows_, h, lo, hi):
            return t[0:rows_, b % 2, h, lo:hi]

        k_st = arena[:, 8192:].bitcast(BF16).rearrange("p (u h q) -> p u h q", u=2, h=NH)
        e_buf = arena[:, 0:8192].rearrange("p (u h c q) -> p u h c q", u=2, h=4, c=2)
        zs = arena[:, 0:2 * TB * NH * CTX].rearrange("p (u t h k) -> p u t h k", u=2, t=TB, h=NH)
        at_ = 2 * TB * NH * CTX
        kc_st = arena[:, at_:at_ + NH * CTX].bitcast(BF16).rearrange("p (u h k) -> p u h k", u=2, h=NH)
        at_ += NH * CTX
        pt_b = arena[0:CTX, at_:at_ + 2 * 4 * SEQ].rearrange("p (u h q) -> p u h q", u=2, h=4)
        at_ += 2 * 4 * SEQ
        x_mx = arena[:, at_:at_ + 2 * NH].rearrange("p (u h) -> p u h", u=2)
        at_ += 32
        a_f = arena[:, at_:at_ + SEQ]
        at_ += SEQ
        w_sizes = arena[:, at_:at_ + 4 * P]
        at_ += 4 * P
        assert 8192 <= at_ <= 16384
        rp = d_t[:, 0:3 * TB, :].rearrange("p (i t) c -> p i (t c)", i=3)
        e_c = arena[0:CTX, 0:4096].rearrange("p (u h q) -> p u h q", u=2, h=4)
        cm_t = arena[:, 4096:4096 + 2 * TB * NH].rearrange("p (u t h) -> p u t h", u=2, t=TB)
        cm_p = arena[0:NH, 4224:4224 + 3 * SEQ].bitcast(BF16).rearrange("p (u j q) -> p u j q", u=2, j=3)
        cm_r = arena[0:NH, 15360:15360 + SEQ]
        ca_f = arena[:, 5760:5760 + SEQ]
        kr_st = arena[:, 6272:6272 + 2 * NH * CTX].bitcast(BF16).rearrange("p (b h k) -> p b h k", b=NB, h=NH)
        fr = arena[:, 0:1024].rearrange("p (u q) -> p u q", u=2)
        fh = arena[:, 1024:1024 + 2 * FC * SEQ].rearrange("p (u f q) -> p u f q", u=2, f=FC)
        fy = arena[:, 5120:5120 + 1024].rearrange("p (u q) -> p u q", u=2)
        fs = arena[:, 6144:6144 + 6 * 512].rearrange("p (i q) -> p i q", i=6)

        r0 = q_st[:, :, :, :].rearrange("p u h q -> p (u h q)").bitcast(F32)

        def two(at):
            return r0[:, at:at + 2 * SEQ].rearrange("p (u q) -> p u q", u=2)
        mixed, weighed, squares, shifted_q = (arena[:, 2 * SEQ * i:2 * SEQ * (i + 1)].rearrange("p (u q) -> p u q", u=2)
                                              for i in range(4))
        lin = two(8 * SEQ)
        x_q, x_qf = (two(5120).bitcast(BF16)[:, i, :].rearrange("p (u q) -> p u q", u=2) for i in range(2))
        key_f, val_f = two(6144), two(7168)
        r1 = arena[:, 9216:16384]
        arg, ex = (r1[:, 2048 * i:2048 * i + 2048].rearrange("p (i q) -> p i q", i=4) for i in range(2))
        alpha, beta, eps = (r1[:, 4096 + 514 * i:4096 + 514 * i + SEQ + 1] for i in range(3))
        wkv, gate = (r1[:, 5638 + SEQ * i:5638 + SEQ * i + SEQ] for i in range(2))
        gated = d_t[:, 0:TB, :]
        qkv = arena[:, 9216:9216 + NT * 3 * P].rearrange("p (b t c) -> p b t c", b=NB, t=TB)
        sc, pr = (r0[:, 6144 + 512 * i:6656 + 512 * i].rearrange("p (u q s h) -> p u q s h", u=2, q=NB, s=NB)
                  for i in range(2))
        sc_n = r0[:, 7168:7168 + 6 * NB * NH].rearrange("p (i q h) -> p i q h", i=6, q=NB)
        prod = arena[:, 0:2 * NB * NB * P].rearrange("p (u q s c) -> p u q s c", u=2, q=NB, s=NB)
        pv_t = arena[:, 4096:8192].rearrange("p (u q s c) -> p u q s c", u=2, q=NB, s=NB)
        h_t = r0[:, 0:2048].rearrange("p (g c) -> p g c", g=NT)
        h_f = r0[:, 2048:4096].rearrange("p (b q) -> p b q", b=NB)
        c_f = r0[:, 4096:5120].rearrange("p (b q) -> p b q", b=2)
        rank = arena[:, 8192:8960].rearrange("p (i t e f) -> p i t e f", i=3, t=TB, e=NE)
        hid = arena[:, 15360:16384].rearrange("p (u q) -> p u q", u=2)
        oh_f = x_f[0:NE, :, :]
        oh_b = r0[0:NE, 5120:6144].bitcast(BF16).rearrange("p (b q) -> p b q", b=NB)
        gates = r0[:, 7552:8064].rearrange("p (i t e) -> p i t e", i=16, t=TB)

        block = ctx.enter_context(nc.Block())

        def with_banks(steps, uses):
            n = 0
            for kind, i in steps:
                banks = [ROUND[(n + j) % 3] for j in range(uses.get(kind, 0))]
                n += len(banks)
                yield kind, i, banks

        def self_attention():
            for kind, i, banks in with_banks(self_steps(), {"a": 1, "max": 1, "norm": 1, "ln_b": 1, "proj": 3,
                                                                  "cross": 2}):
                yield kind, i, ([0, 1, 2], [3, 6, 7])[i] if kind == "proj" and i < 2 else banks

        def rotated_attention():
            yield from with_banks(rotated_steps(), {"q": 2, "a": 3, "max": 1, "norm": 1, "at": 1, "wo": 1,
                                                    "ln_b": 1, "qkv": 4})

        def self_steps():
            made = 0
            yield ("proj", 0)
            yield ("stack", 0)
            yield ("proj", 1)
            yield ("stack", 1)
            n_a, late = NB * NH * TB, None
            for k in range(NB * NH * 2):
                if k in (16, 40):
                    yield ("proj", 2 if k == 16 else 3)
                if k in (32, 64):
                    yield ("stack", 1 + k // 32)
                if k in EARLY:
                    yield ("cross", EARLY.index(k))
                ahead = []
                if late is not None:
                    ahead.append(("max", late))
                    late = None
                while made < min(n_a, 2 * k + 48):
                    ahead.append(("a", made))
                    made += 1
                    if made % (HALF * TB) == 0:
                        late = made // (HALF * TB) - 1
                        if k == 0:
                            ahead.append(("max", late))
                            late = None
                ahead.insert(1 if k > 0 else len(ahead), ("b_first", k))
                yield from ahead
                g, hh = k // 4, k % 4
                yield ("b", k)
                if hh == 1 and g > 0:
                    yield ("pv_first", g - 1)
                if hh == 3 and g > 0:
                    yield ("pv", g - 1)
                if hh == 0 and g > 2 and g % 2 == 1:
                    yield ("copy", g // 2 - 1)
                if hh == 2 and g > 2 and g % 2 == 1:
                    yield ("norm", g // 2 - 1)
                    if (g // 2) % 4 == 0:
                        yield ("ln_a", g // 8 - 1)
                if hh == 3 and g % 8 == 3 and g > 8:
                    yield ("ln_b", g // 8 - 1)
            g = NB * NH * 2 // 4
            yield ("pv_first", g - 1)
            yield ("pv", g - 1)
            yield ("copy", g // 2 - 1)
            yield ("norm", g // 2 - 1)
            yield ("ln_a", NB - 1)

        def cross_attention():
            for k in range(NT + 11):
                if k == 1:
                    yield ("ln_b", -1, 0)
                if k == 2:
                    yield ("q", NB - 1, 0)
                for kind, lag in (("pt", 5), ("s", 0), ("p", 1), ("pv", 6), ("norm", 7)):
                    if 0 <= k - lag < NT:
                        yield (kind, (k - lag) // TB, (k - lag) % TB)
                for kind, lag in (("at", 8), ("wo", 9), ("ln_b", 12)):
                    if 0 <= k - lag < NT and (k - lag) % TB == TB - 1:
                        yield (kind, (k - lag) // TB, 0)

        KEYS = [("k", 0, (4, 5, 6))]

        def rotated_steps():
            yield ("stack", 1)
            made = 0
            for i in range(NB * NH // 2 + 8):
                while made < min(NT, i // 2 + 6, TB * (2 + (i > 8) + (i > 16))):
                    if made == TB:
                        yield ("q", NB - 1)
                    yield ("a", made)
                    made += 1
                    if made % TB == 0:
                        yield ("max", made // TB - 1)
                if i < NB * NH // 2:
                    yield ("b", i)
                if i in (8, 16):
                    yield ("stack", 1 + i // 8)
                for kind, lag in (("pv", 2), ("copy", 3), ("norm", 4)):
                    if i >= lag and (i - lag) % 2 == 0 and (i - lag) // 2 < NT:
                        yield (kind, (i - lag) // 2)
                for kind, lag in (("at", 11), ("wo", 12), ("ln_b", 16), ("qkv", 17)):
                    if i >= lag and (i - lag) % (NH // 2) == 0 and (i - lag) // (NH // 2) < NB:
                        yield (kind, (i - lag) // (NH // 2))
            yield ("ln_b", NB - 1)
            yield ("qkv", NB - 1)

        def recurrent():
            slots, n = [], 0
            for s in range(4 * NB + 4):
                b, w = (s // 4, s % 4) if s % 4 < 3 else (s // 4 - 1, 3)
                there = 0 <= b < NB
                slots.append((n, b, w) if there else None)
                n += there
            for s in range(len(slots) + 6):
                if s == FFN_LN:
                    yield ("ln_b", 0, -1, 0)
                b = (s - 5) // 4
                chain = s % 4 in (1, 2) and 0 <= b < NB
                for kind, lag in (("mix", 0), ("wkv", 1), ("lin", 3), ("quant", 2), ("rms", 0), ("wkv", 2),
                                  ("scale", 1), ("sums", 0), ("turned", 3), ("ln_b", 5)):
                    if kind == "wkv":
                        if chain:
                            yield (f"wkv{2 * (s % 4 - 1) + lag}", 0, b, 0)
                    elif 0 <= s - lag < len(slots) and slots[s - lag]:
                        if kind != "ln_b" or slots[s - lag][2] == 3:
                            yield (kind, *slots[s - lag])
                if s >= 14 and s % 4 == 2 and (s - 14) // 4 < NB - 1:
                    yield ("project", 0, (s - 14) // 4, 0)

        def unit(u):
            return u // 2, (u % 2) * HALF

        def last_layer():
            for kind, g in (("score", 0), ("score", 1), ("weigh", 0), ("score", 2), ("weigh", 1), ("turn", 0),
                            ("score", 3), ("out", 0), ("weigh", 2), ("turn", 1), ("out", 1), ("h", 0),
                            ("h_f", 0), ("weigh", 3), ("prob", 0), ("pick", 0), ("hot", 0)):
                yield (kind, g, 0)
            between = {(0, 1): [("turn", 2), ("h", 1)], (0, 2): [("out", 2)], (0, 3): [("h_f", 1)],
                       (0, 4): [("prob", 1), ("pick", 1)], (0, 5): [("h", 2)], (0, 6): [("turn", 3)],
                       (0, 7): [("hot", 1), ("h_f", 2)],
                       (1, 1): [("prob", 2), ("pick", 2)], (1, 2): [("out", 3)], (1, 3): [("sum1", 0)],
                       (1, 4): [("hot", 2)], (1, 5): [("h", 3), ("norm1", 0)], (1, 6): [("sum2", 0)],
                       (1, 7): [("h_f", 3)],
                       (2, 1): [("prob", 3), ("pick", 3)], (2, 2): [("norm2", 0)], (2, 3): [("sum1", 1)],
                       (2, 4): [("hot", 3)]}
            for g in range(2, TB + 1):
                for e, kind in ((2, "sum1"), (4, "norm1"), (5, "sum2"), (7, "norm2")):
                    if (g, e) != (2, 2):
                        between[g, e] = between.get((g, e), []) + [(kind, g - 1)]
            for g in range(TB + 1):
                for e in range(1, NE):
                    if g < TB or e == 1:
                        yield ("expert", g, e)
                    for what in between.get((g, e), []):
                        yield (*what, 0)

        def norm_of(kind, b):
            return {"out": 5 * NB + b, "sum1": 5 * NB + TB + 2 * b, "sum2": 5 * NB + TB + 2 * b + 1}[kind]

        def group(g):
            return x_t[:, :, :].rearrange("p (b t) c -> p b t c", b=NB)[:, :, g, :]

        def final(b):
            return norm_of("sum2", b)

        N_SMALL = 13

        @block.sync
        def _(sp):
            sp.dma_start(x_f[:, 0, :], d["x_f"][:, 0, :]).then_inc(S["load_x"], 16)
            sp.dma_start(mats[:, 0:3, :], d["mats"][:, 0:3, :]).then_inc(S["load_x"], 16)
            sp.dma_start(x_f[:, 1:NB, :], d["x_f"][:, 1:NB, :]).then_inc(S["load_x1"], 16)
            sp.dma_start(cols[:, :], d["cols"]).then_inc(S["load_s"], 16)
            sp.dma_start(mats[:, len(MATS) - 1, :], d["mats"][:, len(MATS) - 1, :]).then_inc(S["load_s"], 16)
            sp.dma_start(ctx_f[:, :], d["ctx_f"]).then_inc(S["load_s"], 16)
            sp.dma_start(x_t[:, :, :], d["x_t"]).then_inc(S["load_s"], 16)
            sp.dma_start(mask[:, :, :], d["mask"]).then_inc(S["load_s"], 16)
            sp.dma_start(rope_q[:, :, :], d["rope_q"]).then_inc(S["load_s"], 16)
            sp.dma_start(rope_k[:, :, :], d["rope_k"]).then_inc(S["load_s"], 16)
            sp.dma_start(router[:, :], d["router"]).then_inc(S["load_s"], 16)
            sp.dma_start(b2[:, :], d["b2"]).then_inc(S["load_s"], 16)
            sp.dma_start(tri[:, :], d["tri"]).then_inc(S["load_s"], 16)
            sp.dma_start(iota[:, :], d["iota"]).then_inc(S["load_s"], 16)
            sp.dma_start(pen[:, :, :], d["pen"]).then_inc(S["load_s"], 16)
            sp.dma_start(rows[:, :, :], d["rows"].partition_broadcast(P)).then_inc(S["load_s"], 16)
            sp.dma_start(mats[:, 3:len(MATS) - 1, :], d["mats"][:, 3:len(MATS) - 1, :]).then_inc(S["load_w"], 16)

            def stacks(t, b, src, part_of):
                for s in range(SLOTS):
                    at = s * HD
                    sp.dma_start(t[at:at + HD, b % 2, :, :], src[:, part_of[s], :])\
                      .then_inc(S[f"stack_dma{b}"], 16)

            def cross_stack(n, t, b, width, part_of, columns):
                for s in range(SLOTS):
                    at = 64 * (b % 2) + s * HD
                    sp.dma_start(t[at:at + HD, b // 2, :, :], parts[:, n % 4, part_of[s], columns:columns + width])\
                      .then_inc(S[f"x_dma{n}"], 16)

            for kind, i, banks in self_attention():
                if kind == "stack":
                    sp.wait_ge(S["q_lo"], i + 1)
                    sp.wait_ge(S["setup"], 1 + i % 2)
                    if i >= 2:
                        sp.wait_ge(S["st"], NH * 2 * (i - 1))
                    stacks(q_st, i, parts[:, 2 * (i % 2)], Q_PART)
                    sp.wait_ge(S["k_lo"], i + 1)
                    sp.wait_ge(S["setup_dve"], 1 + i % 2)
                    stacks(k_st, i, parts[:, 2 * (i % 2) + 1], K_PART)
                elif kind == "cross" and i < 3:
                    sp.wait_ge(S["x_lo"], i + 1)
                    sp.wait_ge(S["st"], (NB - 1) * NH * 2)
                    if i == 0:
                        for c in range(NB):
                            cross_stack(0, kc_st, c, CTX, K_PART, c * CTX)
                    else:
                        cross_stack(i, q_st, i - 1, SEQ, Q_PART, 0)
                elif kind == "max":
                    b, h0 = unit(i)
                    sp.wait_ge(S["m_lo"], i + 1)
                    for j in range(3):
                        at = MAX_ROW + j
                        sp.dma_start(q_st[at:at + 1, b % 2, h0:h0 + HALF, :], max_p[:, i % 2, j, :])\
                          .then_inc(S[f"m_dma{i}"], 16)

            def cross():
                for b in range(2, NB):
                    sp.wait_ge(S["x_lo"], b + 2)
                    sp.wait_ge(S["st"], NB * NH * 2)
                    cross_stack(1 + b, q_st, b, SEQ, Q_PART, 0)

            def rotated(steps):
                for kind, i, banks in steps:
                    if kind == "k":
                        sp.wait_ge(S["x_lo"], 6)
                        sp.wait_ge(S["setup_dve"], 3)
                        for s in range(SLOTS):
                            for c in range(NB):
                                sp.dma_start(kr_st[s * HD:s * HD + HD, c, :, :],
                                             parts[:, 5 % 4, K_PART[s], c * CTX:(c + 1) * CTX])\
                                  .then_inc(S["x_dma5"], 16)
                    elif kind == "stack":
                        sp.wait_ge(S["x_lo"], 7 + i)
                        sp.wait_ge(S["setup"], 5 + i % 2)
                        if i >= 2:
                            sp.wait_ge(S["c_st"], NH // 2 * (i - 1))
                        for s in range(SLOTS):
                            sp.dma_start(q_st[s * HD:s * HD + HD, i % 2, :, :], parts[:, (6 + i) % 4, Q_PART[s], :])\
                              .then_inc(S[f"x_dma{6 + i}"], 16)
                    elif kind == "max":
                        sp.wait_ge(S["m_lo"], 2 * NB + i + 1)
                        for j in range(3):
                            at = MAX_ROW + j
                            sp.dma_start(q_st[at:at + 1, i % 2, :, :], cm_p[:, i % 2, j, :])\
                              .then_inc(S[f"m_dma{i}"], 16)

            cross()
            rotated(KEYS)
            rotated([("stack", 0, ())])
            rotated(rotated_attention())
            for g in range(TB):
                sp.wait_ge(S["ln_x"], TB * (final(g) + 1))
                for b in range(NB):
                    sp.dma_start(d["out"][b][P * g:P * g + P, :], group(g)[:, b, :]).then_inc(S["out"], 16)
            sp.wait_ge(S["out"], 16 * NT)

        @block.tensor
        def _(pe):
            readers = [[] for _ in range(8)]

            def take(bank, *by):
                for s, n in readers[bank]:
                    pe.wait_ge(S[s], n)
                readers[bank] = list(by)
                return ps[:, bank, :]

            def mm(out, lhs, rhs, start=True, stop=True, **k):
                return nc.tensor.matmul(out, lhs, rhs, start=start, stop=stop, **k)

            ident = mat("ident")

            def turn(out, src, n=TB):
                for t in range(n):
                    last = nc.tensor.transpose(out[:, t * P:(t + 1) * P], src[:, t, :], ident)
                return last

            def ln_b(n, bank=7):
                pe.wait_ge(S["ln_x"], TB * (n + 1))
                out = take(bank, ("ln_f", n + 1))
                b = n % NB
                turn(out, x_t[:, TB * b:TB * b + TB, :]).then_inc(S["ln_t"], 1)

            def cross_v(x, bank):
                out = take(bank, ("x_v", x + 1))
                for c in range(NB):
                    last = mm(out[0:CTX, c * P:(c + 1) * P], ctx_f[:, c * CTX:(c + 1) * CTX], mat("xc"[x] + "v"))
                last.then_inc(S["x_vraw"], 1)

            def cross_project(n, banks):
                if n == 0:
                    pe.wait_ge(S["load_w"], 16)
                    mm(take(banks[0], ("x_res", 1))[:, 0:NCTX], mat("xk"), ctx_f[:, :]).then_inc(S["x_raw"], 1)
                    cross_v(0, banks[1])
                else:
                    pe.wait_ge(S["ln_f"], n)
                    mm(take(banks[0], ("x_res", n + 1)), mat("xq"), x_f[:, n - 1, :]).then_inc(S["x_raw"], 1)

            pe.wait_ge(S["load_x"], 32)
            for kind, i, banks in self_attention():
                if kind == "proj":
                    bq, bk, bv = banks
                    if i == 1:
                        pe.wait_ge(S["load_x1"], 16)
                    for w, bank, res in (("q", bq, "q_res"), ("k", bk, "k_res")):
                        out = take(bank, (res, i + 1))
                        mm(out, mat(w + "0"), x_f[:, i, :]).then_inc(S[w + "_raw"], 1)
                    out = take(bv, ("v_sb", i + 1))
                    for t in range(TB):
                        last = mm(out[:, t * P:(t + 1) * P], x_f[:, i, t * P:(t + 1) * P], mat("v0"))
                    last.then_inc(S["v_raw"], 1)
                elif kind == "cross":
                    cross_project(i, banks)
                elif kind == "a":
                    u, r = divmod(i, HALF * TB)
                    b, h0 = unit(u)
                    h, t = h0 + r // TB, r % TB
                    if r == 0:
                        pe.wait_ge(S[f"stack_dma{b}"], 16 * 2 * SLOTS)
                    out = take(banks[0], ("a_max", i + 1))
                    mm(out, tall(q_st, b, MAX_ROW, h, t * P, t * P + P), tall(k_st, b, MAX_ROW, h, 0, SEQ))\
                        .then_inc(S["a_s"], 1)
                elif kind == "max":
                    if i == 0:
                        pe.wait_ge(S["load_s"], 16 * N_SMALL)
                    pe.wait_ge(S["a_max"], HALF * TB * (i + 1))
                    out = take(banks[0], ("m_res", i + 1))
                    for t in range(TB):
                        last = nc.tensor.transpose(out[0:HALF, t * P:(t + 1) * P], max_t[:, i % 2, t, :], ident)
                    last.then_inc(S["m_t"], 1)
                elif kind in ("b_first", "b"):
                    g, hh = divmod(i, 4)
                    q, sp_ = divmod(g, 2)
                    b, h = q // 4, 4 * (q % 4) + hh
                    if i % 16 == 0 and kind == "b_first":
                        pe.wait_ge(S[f"m_dma{i // 16}"], 48)
                    j = kind == "b"
                    c = 2 * sp_ + j
                    out = take(2 * (i % 2) + j, ("exp", i + 1))
                    last = mm(out, tall(k_st, b, P, h, c * P, c * P + P), tall(q_st, b, P, h, 0, SEQ))
                    if kind == "b":
                        last.then_inc(S["st"], 1)
                elif kind in ("pv_first", "pv"):
                    q, sp_ = divmod(i, 2)
                    b, j = q // 4, kind == "pv"
                    if j == 0:
                        pe.wait_ge(S["exp"], 4 * (i + 1))
                    if j == 0 and sp_ == 0:
                        pe.wait_ge(S["v_sb"], b + 1)
                        take(6, ("ot", q + 1))
                    for hh in range(4):
                        last = mm(ps[32 * hh:32 * hh + 32, 6, :],
                                  v_lhs(P, TB * b + 2 * sp_ + j, 4 * (q % 4) + hh),
                                  e_buf[:, i % 2, hh, int(j), :],
                                  start=(sp_ == 0 and j == 0), stop=(sp_ == 1 and j == 1))
                    if kind == "pv":
                        last.then_inc(S["pv"], 1)
                elif kind == "norm":
                    pe.wait_ge(S["ot"], i + 1)
                    turn(take(banks[0], ("attn", i + 1)), o_f[:, i % 2, :].rearrange("p (t c) -> p t c", t=TB))\
                        .then_inc(S["ott"], 1)
                elif kind == "ln_b":
                    ln_b(i, banks[0])

            def cross():
                for kind, b, t in cross_attention():
                    n = TB * b + t
                    if kind == "q":
                        cross_project(1 + b, (7,))
                    elif kind == "s":
                        if t == 0:
                            pe.wait_ge(S["x_dma0"], 16 * SLOTS * NB)
                            pe.wait_ge(S[f"x_dma{1 + b}"], 16 * SLOTS)
                        for i in range(3):
                            out = take(i, ("x_z", 3 * n + i + 1))
                            for h in range(6 * i, min(6 * i + 6, NH)):
                                at = (h - 6 * i) * CTX
                                last = mm(out[:, at:at + CTX], stack(q_st, b, STACK, h, t * P, t * P + P),
                                          stack(kc_st, b, STACK, h, 0, CTX))
                            last.then_inc(S["x_s"], 1)
                    elif kind == "pt":
                        if t == 0:
                            pe.wait_ge(S["x_p"], n + TB)
                        for j in range(4):
                            out = take(3 + j % 2, ("x_pd", n + 1) if j == 3 else ("x_pa", 3 * n + j + 1))
                            for tt in range(TB):
                                last = nc.tensor.transpose(out[0:CTX, tt * P:(tt + 1) * P],
                                                           zs[:, b % 2, tt, 4 * t + j, :], ident)
                            last.then_inc(S["x_pt"], 1)
                    elif kind == "pv":
                        take(5, ("x_ot", n + 1))
                        pe.wait_ge(S["x_pa"], 3 * (n + 1))
                        pe.wait_ge(S["x_pd"], n + 1)
                        pe.wait_ge(S["x_v"], 1)
                        for j in range(4):
                            last = mm(ps[32 * j:32 * j + 32, 5, :], v_lhs(CTX, b, 4 * t + j), pt_b[:, n % 2, j, :])
                        last.then_inc(S["x_pv"], 1)
                    elif kind == "norm":
                        pe.wait_ge(S["x_ot"], n + 1)
                        turn(take(6, ("x_attn", n + 1)), o_f[:, n % 2, :].rearrange("p (t c) -> p t c", t=TB))\
                            .then_inc(S["x_ott"], 1)
                    elif kind == "at":
                        pe.wait_ge(S["x_attn"], 4 * (b + 1))
                        turn(take(6, ("x_af", b + 1)), d_t[:, TB * b:TB * b + TB, :]).then_inc(S["x_at"], 1)
                    elif kind == "wo":
                        pe.wait_ge(S["x_af"], b + 1)
                        out = take(7, ("ln_mv", NB + b + 1))
                        for c in range(TB):
                            last = mm(out[:, c * P:(c + 1) * P], a_f[:, c * P:(c + 1) * P], mat("xo"))
                        last.then_inc(S["x_wo"], 1)
                    elif kind == "ln_b":
                        ln_b(NB + b)

            def rotated(steps):
                for kind, i, banks in steps:
                    if kind in ("k", "q"):
                        n = 5 if kind == "k" else 6 + i
                        width = NCTX if kind == "k" else SEQ
                        rhs = ctx_f[:, :] if kind == "k" else x_f[:, i, :]
                        if kind == "q":
                            pe.wait_ge(S["ln_f"], 3 * NB + i + 1)
                        mm(take(banks[0], ("x_rope", n - 4))[:, 0:width], mat("c" + kind), rhs)
                        mm(take(banks[1], ("x_rope", n - 4))[:, 0:width], mat("c" + kind + "s"), rhs)\
                            .then_inc(S["x_raw"], 1)
                        if kind == "k":
                            cross_v(1, banks[2])
                    elif kind == "a":
                        b, t = divmod(i, TB)
                        if t == 0:
                            pe.wait_ge(S["x_dma5"], 16 * SLOTS * NB)
                            pe.wait_ge(S[f"x_dma{6 + b}"], 16 * SLOTS)
                        for j in range(3):
                            out = take(banks[j], ("c_mx", 3 * i + j + 1))
                            for h in range(6 * j, min(6 * j + 6, NH)):
                                at = (h - 6 * j) * CTX
                                last = mm(out[:, at:at + CTX], tall(q_st, b, MAX_ROW, h, t * P, t * P + P),
                                          kr_st[0:MAX_ROW, b, h, :])
                            last.then_inc(S["c_s"], 1)
                    elif kind == "max":
                        pe.wait_ge(S["c_mx"], 3 * TB * (i + 1))
                        out = take(banks[0], ("m_res", 2 * NB + i + 1))
                        for t in range(TB):
                            last = nc.tensor.transpose(out[0:NH, t * P:(t + 1) * P], cm_t[:, i % 2, t, :], ident)
                        last.then_inc(S["m_t"], 1)
                    elif kind == "b":
                        b, h = divmod(2 * i, NH)
                        if h == 0:
                            pe.wait_ge(S[f"m_dma{b}"], 96)
                        for j in range(2):
                            out = take(2 * (i % 2) + j, ("c_exp", i + 1))
                            last = mm(out[0:CTX, :], kr_st[:, b, h + j, :], tall(q_st, b, P, h + j, 0, SEQ))
                        last.then_inc(S["c_st"], 1)
                    elif kind == "pv":
                        pe.wait_ge(S["c_exp"], 2 * (i + 1))
                        take(6, ("x_ot", NT + i + 1))
                        if i == 0:
                            pe.wait_ge(S["x_v"], 2)
                        for j in range(4):
                            last = mm(ps[32 * j:32 * j + 32, 6, :], v_lhs(CTX, i // 4, 4 * (i % 4) + j),
                                      e_c[:, i % 2, j, :])
                        last.then_inc(S["x_pv"], 1)
                    elif kind == "norm":
                        pe.wait_ge(S["x_ot"], NT + i + 1)
                        turn(take(banks[0], ("x_attn", NT + i + 1)), o_f[:, i % 2, :].rearrange("p (t c) -> p t c", t=TB))\
                            .then_inc(S["x_ott"], 1)
                    elif kind == "at":
                        pe.wait_ge(S["x_attn"], NT + TB * (i + 1))
                        turn(take(banks[0], ("x_af", NB + i + 1)), d_t[:, TB * i:TB * i + TB, :]).then_inc(S["x_at"], 1)
                    elif kind == "wo":
                        pe.wait_ge(S["x_af"], NB + i + 1)
                        out = take(banks[0], ("ln_mv", 4 * NB + i + 1))
                        for c in range(TB):
                            last = mm(out[:, c * P:(c + 1) * P], ca_f[:, c * P:(c + 1) * P], mat("co"))
                        last.then_inc(S["x_wo"], 1)
                    elif kind == "ln_b":
                        ln_b(4 * NB + i, banks[0])
                    elif kind == "qkv":
                        pe.wait_ge(S["ln_f"], 4 * NB + i + 1)
                        i0 = MATS.index("iq")
                        for t in range(TB):
                            g = TB * i + t
                            mm(take(banks[t], ("i_qkv", g + 1))[:, 0:3 * P], x_f[:, i, t * P:(t + 1) * P],
                               mats[:, i0:i0 + 3, :]).then_inc(S["i_raw"], 1)

            cross()
            for b in range(NB + 1):
                if b == 1:
                    ln_b(2 * NB - 1)
                if b < NB:
                    pe.wait_ge(S["ln_f"], NB + b + 1)
                    for f in range(FC):
                        n = FC * b + f
                        mm(take(n % 3, ("f_r", n + 1)), mat(f"fc{f}"), x_f[:, b, :]).then_inc(S["f_h"], 1)
                if b > 0:
                    c = b - 1
                    pe.wait_ge(S["f_sq"], FC * (c + 1))
                    out = take(3 + c % 2, ("f_y", c + 1))
                    for t in range(TB):
                        for f in range(FC):
                            last = mm(out[:, t * P:(t + 1) * P], fh[:, c % 2, f, t * P:(t + 1) * P],
                                      mat(f"pj{f}"), start=(f == 0), stop=(f == FC - 1))
                    last.then_inc(S["f_yraw"], 1)
                if b > 1:
                    ln_b(2 * NB + b - 2)
            pe.wait_ge(S["r_abs"], 4)
            pe.wait_ge(S["setup"], 4)
            mm(take(6, ("r_wq", 4))[:, 0:4], ones[:, :], w_abs[:, :]).then_inc(S["r_sum"], 1)
            rotated(KEYS)
            for kind, n, b, w in recurrent():
                if kind == "project":
                    rotated([("q", b, (4, 5))])
                    continue
                if kind == "mix":
                    if w < 3:
                        pe.wait_ge(S["r_mix"], 3 * b + w + 1)
                        out, src = take(n % 2, ("r_u", n + 1), ("r_sq", TB * (n + 1))), mixed[:, n % 2, :]
                    else:
                        pe.wait_ge(S["r_w"], b + 1)
                        out, src = take(n % 2, ("r_z", b + 1)), wkv
                    turn(out, src.rearrange("p (t c) -> p t c", t=TB)).then_inc(S["r_zt"], 1)
                elif kind == "quant":
                    pe.wait_ge(S["r_xq"], n + 1)
                    out = take(2, ("r_xf", n + 1)).bitcast(BF16)
                    for t in range(TB):
                        last = nc.tensor.transpose(out[:, t * P:(t + 1) * P], x_q[:, n % 2, t * P:(t + 1) * P],
                                                   ident_b[:, :])
                    last.then_inc(S["r_xt"], 1)
                elif kind == "lin":
                    pe.wait_ge(S["r_xf"], n + 1)
                    if n == 0:
                        pe.wait_ge(S["r_wq"], 4)
                    out = take(3, ("r_kt", n + 1))
                    for t in range(TB):
                        last = mm(out[:, t * P:(t + 1) * P], x_qf[:, n % 2, t * P:(t + 1) * P], w_q[:, w, :])
                    last.then_inc(S["r_mm"], 1)
                elif kind == "turned" and w < 2:
                    pe.wait_ge(S["r_kt"], n + 1)
                    turn(take(4 + w, ("r_kf", 2 * b + w + 1)),
                         lin[:, n % 2, :].rearrange("p (t c) -> p t c", t=TB)).then_inc(S["r_ktt"], 1)
                elif kind == "ln_b":
                    ln_b(3 * NB + b)
            rotated(rotated_attention())
            for kind, b, e in last_layer():
                if kind == "turn":
                    out = take(4, ("i_cf", b + 1))
                    for q in range(NB):
                        pe.wait_ge(S["i_pp"], NB * b + q + 1)
                        for k in range(NB):
                            last = mm(out[:, q * P:(q + 1) * P], pv_t[:, b % 2, q, k, :], ident,
                                      start=(k == 0), stop=(k == NB - 1))
                    last.then_inc(S["i_ct"], 1)
                elif kind == "out":
                    pe.wait_ge(S["i_cf"], b + 1)
                    out = take(5, ("ln_mv", norm_of("out", b) + 1))
                    for t in range(TB):
                        last = mm(out[:, t * P:(t + 1) * P], c_f[:, b % 2, t * P:(t + 1) * P], mat("io"))
                    last.then_inc(S["i_out"], 1)
                elif kind == "h_f":
                    pe.wait_ge(S["ln_g"], b + 1)
                    turn(take(6, ("g_hf", b + 1)), h_t[:, TB * b:TB * b + TB, :]).then_inc(S["g_ht"], 1)
                elif kind == "prob":
                    pe.wait_ge(S["g_hf"], b + 1)
                    out = take(7, ("g_d", b + 1))
                    for t in range(TB):
                        last = mm(out[:, t * NE:(t + 1) * NE], h_f[:, b, t * P:(t + 1) * P], router[:, :])
                    last.then_inc(S["g_raw"], 1)
                elif kind == "hot":
                    pe.wait_ge(S["g_oh"], b + 1)
                    out = take(7, ("g_ohf", 2 * b + 2))
                    for t in range(TB):
                        last = nc.tensor.transpose(out[0:NE, t * P:(t + 1) * P], gates[:, 8 + b % 2, t, :], ident)
                    last.then_inc(S["g_oht"], 1)
                elif kind == "expert":
                    m = (NE - 1) * b + e - 1
                    if b < NB:
                        if e == 1:
                            pe.wait_ge(S["g_ohf"], 2 * b + 2)
                            acc = take(2 + b % 2, ("ln_mv", norm_of("sum1", b) + 1))
                            for t in range(TB):
                                mm(acc[:, t * P:(t + 1) * P], oh_f[:, b, t * P:(t + 1) * P], b2[:, :],
                                   start=(t == 0), stop=False, skip_group_check=True)
                        h = take(m % 2, ("e_g", m + 1))
                        mm(h, mat(f"w1_{e}"), h_f[:, b, :], stop=False)
                        mm(h, pen[:, e, :], oh_b[:, b, :], start=False).then_inc(S["e_h"], 1)
                    if m > 0:
                        b_, e_ = divmod(m - 1, NE - 1)
                        pe.wait_ge(S["e_g"], m)
                        for t in range(TB):
                            last = mm(ps[:, 2 + b_ % 2, t * P:(t + 1) * P], hid[:, (m - 1) % 2, t * P:(t + 1) * P],
                                      mat(f"w2_{e_ + 1}"), start=False, stop=(e_ == NE - 2), skip_group_check=True)
                        last.then_inc(S["e_o"], 1)

        @block.scalar
        def _(act):
            def ln_scale(n, b, out):
                act.wait_ge(S["ln_rs"], n + 1)
                u = n % 2
                for t in range(TB):
                    nc.scalar.activation(out[:, t, :], ln_in[:, u, t, :], ACT.Identity,
                                         scale=ln_rs[:, u, t, 1:2], bias=ln_rs[:, u, t, 3:4])\
                        .then_inc(S["ln_x"], 1)

            def ln_apply(n, bank=7):
                b = n % NB
                ln_scale(n, b, x_t[:, TB * b:TB * b + TB, :])
                act.wait_ge(S["ln_t"], n + 1)
                nc.scalar.copy(x_f[:, b, :], ps[:, bank, :]).then_inc(S["ln_f"], 1)

            def high_and_middle(n, src, width):
                if n >= 4:
                    act.wait_ge(S[f"x_dma{n - 4}"], 16 * SLOTS * (NB if n % 5 == 4 else 1))
                nc.scalar.copy(parts[:, n % 4, 0, 0:width], src).then_inc(S["x_hi"], 1)
                act.wait_ge(S["x_res"], n + 1)
                nc.scalar.copy(parts[:, n % 4, 1, 0:width], rest[:, n % 2, 0:width]).then_inc(S["x_mid"], 1)

            def cross_project(n, banks):
                width = SEQ if n else NCTX
                act.wait_ge(S["x_raw"], n + 1)
                high_and_middle(n, ps[:, banks[0], 0:width], width)
                if n == 0:
                    act.wait_ge(S["x_vraw"], 1)
                    nc.scalar.copy(v_heads[0:CTX, 0:NB, :, 0:HD],
                                   ps[0:CTX, banks[1], :].rearrange("p (t h e) -> p t h e", t=NB, h=NH))\
                        .then_inc(S["x_v"], 1)

            for kind, i, banks in self_attention():
                if kind == "proj":
                    bq, bk, bv = banks
                    for w, bank, k in (("q", bq, 0), ("k", bk, 1)):
                        act.wait_ge(S[w + "_raw"], i + 1)
                        if i >= 2:
                            act.wait_ge(S[f"stack_dma{i - 2}"], 16 * 2 * SLOTS)
                        nc.scalar.copy(parts[:, 2 * (i % 2) + k, 0, :], ps[:, bank, :]).then_inc(S[w + "_hi"], 1)
                        act.wait_ge(S[w + "_res"], i + 1)
                        nc.scalar.copy(parts[:, 2 * (i % 2) + k, 1, :], rest[:, k, :]).then_inc(S[w + "_mid"], 1)
                    act.wait_ge(S["v_raw"], i + 1)
                    act.wait_ge(S["setup"], 3)
                    nc.scalar.copy(v_heads[:, TB * i:TB * i + TB, :, 0:HD],
                                   ps[:, bv, :].rearrange("p (t h e) -> p t h e", t=TB, h=NH))\
                        .then_inc(S["v_sb"], 1)
                elif kind == "cross":
                    cross_project(i, banks)
                elif kind == "max":
                    act.wait_ge(S["m_t"], i + 1)
                    if i >= 2:
                        act.wait_ge(S[f"m_dma{i - 2}"], 48)
                    nc.scalar.copy(max_p[:, i % 2, 0, :], ps[0:HALF, banks[0], :]).then_inc(S["m_hi"], 1)
                    act.wait_ge(S["m_res"], i + 1)
                    nc.scalar.copy(max_p[:, i % 2, 1, :], max_r[:, :]).then_inc(S["m_mid"], 1)
                elif kind == "b":
                    g, hh = divmod(i, 4)
                    if hh == 0 and g >= 2:
                        act.wait_ge(S["pv"], g - 1)
                    act.wait_ge(S["st"], i + 1)
                    nc.scalar.activation(e_buf[:, g % 2, hh, :, :], ps[:, 2 * (i % 2):2 * (i % 2) + 2, :], ACT.Exp,
                                         scale=SCALE).then_inc(S["exp"], 1)
                elif kind == "copy":
                    act.wait_ge(S["pv"], 2 * (i + 1))
                    if i >= 2:
                        act.wait_ge(S["ott"], i - 1)
                    nc.scalar.copy(o_f[:, i % 2, :], ps[:, 6, :]).then_inc(S["ot"], 1)
                elif kind == "ln_b":
                    ln_apply(i, banks[0])

            def cross():
                for kind, b, t in cross_attention():
                    n = TB * b + t
                    if kind == "q":
                        cross_project(1 + b, (7,))
                    elif kind == "p":
                        z = zs[:, b % 2, t, :, :]
                        act.wait_ge(S["x_sub"], n + 1)
                        nc.scalar.activation(z, z, ACT.Exp).then_inc(S["x_p"], 1)
                    elif kind == "pt":
                        for j in range(3):
                            act.wait_ge(S["x_pt"], 4 * n + j + 1)
                            if n >= 2 and j == 0:
                                act.wait_ge(S["x_pv"], n - 1)
                            nc.scalar.copy(pt_b[:, n % 2, j, :], ps[0:CTX, 3 + j % 2, :]).then_inc(S["x_pa"], 1)
                    elif kind == "pv":
                        act.wait_ge(S["x_pv"], n + 1)
                        if n >= 2:
                            act.wait_ge(S["x_ott"], n - 1)
                        nc.scalar.copy(o_f[:, n % 2, :], ps[:, 5, :]).then_inc(S["x_ot"], 1)
                    elif kind == "at":
                        act.wait_ge(S["x_at"], b + 1)
                        if b:
                            act.wait_ge(S["x_wo"], b)
                        nc.scalar.copy(a_f[:, :], ps[:, 6, :]).then_inc(S["x_af"], 1)
                    elif kind == "ln_b":
                        ln_apply(NB + b)

            def rotated(steps):
                for kind, i, banks in steps:
                    if kind in ("k", "q"):
                        n = 5 if kind == "k" else 6 + i
                        width = NCTX if kind == "k" else SEQ
                        act.wait_ge(S["x_rope"], n - 4)
                        high_and_middle(n, rp[:, 2, 0:width], width)
                    elif kind == "max":
                        act.wait_ge(S["m_t"], 2 * NB + i + 1)
                        if i >= 2:
                            act.wait_ge(S[f"m_dma{i - 2}"], 96)
                        nc.scalar.copy(cm_p[:, i % 2, 0, :], ps[0:NH, banks[0], :]).then_inc(S["m_hi"], 1)
                        act.wait_ge(S["m_res"], 2 * NB + i + 1)
                        nc.scalar.copy(cm_p[:, i % 2, 1, :], cm_r[:, :]).then_inc(S["m_mid"], 1)
                    elif kind == "b":
                        g = i // 2
                        if i % 2 == 0 and g >= 2:
                            act.wait_ge(S["x_pv"], NT + g - 1)
                        act.wait_ge(S["c_st"], i + 1)
                        j, bank = 2 * (i % 2), 2 * (i % 2)
                        nc.scalar.activation(e_c[:, g % 2, j:j + 2, :], ps[0:CTX, bank:bank + 2, :], ACT.Exp,
                                             scale=SCALE).then_inc(S["c_exp"], 1)
                    elif kind == "copy":
                        act.wait_ge(S["x_pv"], NT + i + 1)
                        if i >= 2:
                            act.wait_ge(S["x_ott"], NT + i - 1)
                        nc.scalar.copy(o_f[:, i % 2, :], ps[:, 6, :]).then_inc(S["x_ot"], 1)
                    elif kind == "at":
                        act.wait_ge(S["x_at"], NB + i + 1)
                        if i:
                            act.wait_ge(S["x_wo"], NB + i)
                        nc.scalar.copy(ca_f[:, :], ps[:, banks[0], :]).then_inc(S["x_af"], 1)
                    elif kind == "ln_b":
                        ln_apply(4 * NB + i, banks[0])

            cross()
            for w in range(4):
                nc.scalar.activation(w_sizes[:, w * P:(w + 1) * P], mat("r" + "kvro"[w]), ACT.Abs,
                                     accum_out=w_abs[:, w:w + 1])\
                    .then_inc(S["r_abs"], 1)
            for b in range(NB + 1):
                if b == 1:
                    ln_apply(2 * NB - 1)
                if b < NB:
                    for f in range(FC):
                        n = FC * b + f
                        act.wait_ge(S["f_h"], n + 1)
                        if n >= 2:
                            act.wait_ge(S["f_sq"], n - 1)
                        nc.scalar.activation(fr[:, n % 2, :], ps[:, n % 3, :], ACT.Relu).then_inc(S["f_r"], 1)
                if b > 0:
                    act.wait_ge(S["f_yraw"], b)
                    if b > 2:
                        act.wait_ge(S["ln_mv"], 2 * NB + b - 2)
                    nc.scalar.copy(fy[:, (b - 1) % 2, :], ps[:, 3 + (b - 1) % 2, :]).then_inc(S["f_y"], 1)
                if b > 1:
                    ln_apply(2 * NB + b - 2)
            nc.scalar.activation(log_w[:, 0:1], col("decay"), ACT.Exp).then_inc(S["r_eps"], 1)
            rotated(KEYS)
            for kind, n, b, w in recurrent():
                if kind == "project":
                    rotated([("q", b, (4, 5))])
                    continue
                u = n % 2
                if kind == "rms":
                    if n >= 2:
                        act.wait_ge(S["r_is"], n - 1)
                    if w < 3:
                        act.wait_ge(S["r_u"], n + 1)
                        src = ps[:, u, :]
                    else:
                        act.wait_ge(S["r_z"], b + 1)
                        src = gated.rearrange("p t c -> p (t c)")
                    for t in range(TB):
                        nc.scalar.activation(squares[:, u, t * P:(t + 1) * P], src[:, t * P:(t + 1) * P],
                                             ACT.Square, accum_out=tok[:, u, 0, t:t + 1])\
                            .then_inc(S["r_sq"], 1)
                elif kind == "scale":
                    act.wait_ge(S["r_r2"], n + 1)
                    if n >= 2:
                        act.wait_ge(S["r_xq"], n - 1)
                    for t in range(TB):
                        nc.scalar.activation(shifted_q[:, u, t * P:(t + 1) * P], weighed[:, u, t * P:(t + 1) * P],
                                             ACT.Identity, scale=tok[:, u, 5, t:t + 1], bias=consts[:, 2:3])\
                            .then_inc(S["r_q"], 1)
                elif kind == "quant":
                    act.wait_ge(S["r_xt"], n + 1)
                    if n >= 2:
                        act.wait_ge(S["r_mm"], n - 1)
                    nc.scalar.copy(x_qf[:, u, :], ps[:, 2, :].bitcast(BF16)[:, 0:SEQ]).then_inc(S["r_xf"], 1)
                elif kind == "turned" and w < 2:
                    act.wait_ge(S["r_ktt"], 2 * b + w + 1)
                    if b >= 2:
                        act.wait_ge(S["r_w"], b - 1)
                    nc.scalar.copy((key_f, val_f)[w][:, b % 2, :], ps[:, 4 + w, :]).then_inc(S["r_kf"], 1)
                elif kind == "turned" and w == 2:
                    act.wait_ge(S["r_kt"], n + 1)
                    if b:
                        act.wait_ge(S["r_z"], b)
                    nc.scalar.activation(gate, lin[:, u, :], ACT.Tanh, scale=0.5).then_inc(S["r_tanh"], 1)
                elif kind == "ln_b":
                    ln_apply(3 * NB + b)
                elif kind == "wkv2":
                    act.wait_ge(S["r_arg1"], b + 1)
                    if b:
                        act.wait_ge(S["r_w"], b)
                    nc.scalar.activation(ex[:, 0:2, :], arg[:, 0:2, :], ACT.Exp).then_inc(S["r_exp1"], 1)
                elif kind == "wkv3":
                    act.wait_ge(S["r_arg2"], b + 1)
                    nc.scalar.activation(ex[:, 2:4, :], arg[:, 2:4, :], ACT.Exp).then_inc(S["r_exp2"], 1)
            rotated(rotated_attention())
            for kind, b, e in last_layer():
                if kind == "score":
                    act.wait_ge(S["i_sc"], b + 1)
                    if b >= 2:
                        act.wait_ge(S["i_pp"], NB * (b - 1))
                    nc.scalar.activation(pr[:, b % 2], sc[:, b % 2], ACT.Exp, scale=SCALE).then_inc(S["i_exp"], 1)
                elif kind == "turn":
                    act.wait_ge(S["i_ct"], b + 1)
                    if b >= 2:
                        act.wait_ge(S["i_out"], b - 1)
                    nc.scalar.copy(c_f[:, b % 2, :], ps[:, 4, :]).then_inc(S["i_cf"], 1)
                elif kind == "h":
                    ln_scale(norm_of("out", b), b, ln_in[:, norm_of("out", b) % 2, :, :])
                elif kind == "h_f":
                    act.wait_ge(S["g_ht"], b + 1)
                    nc.scalar.copy(h_f[:, b, :], ps[:, 6, :]).then_inc(S["g_hf"], 1)
                elif kind == "prob":
                    act.wait_ge(S["g_d"], b + 1)
                    nc.scalar.activation(gates[:, 2, :, :], gates[:, 1, :, :], ACT.Exp).then_inc(S["g_exp"], 1)
                elif kind == "hot":
                    act.wait_ge(S["g_oht"], b + 1)
                    nc.scalar.copy(oh_f[:, b, :], ps[0:NE, 7, :]).then_inc(S["g_ohf"], 1)
                    nc.scalar.copy(oh_b[:, b, :], ps[0:NE, 7, :]).then_inc(S["g_ohf"], 1)
                elif kind == "expert" and b < NB:
                    m = (NE - 1) * b + e - 1
                    act.wait_ge(S["e_h"], m + 1)
                    if m >= 2:
                        act.wait_ge(S["e_o"], m - 1)
                    nc.scalar.activation(hid[:, m % 2, :], ps[:, m % 2, :], ACT.Gelu, bias=col(f"b1_{e}"))\
                        .then_inc(S["e_g"], 1)
                elif kind == "norm1":
                    n = norm_of("sum1", b)
                    ln_scale(n, b, ln_in[:, n % 2, :, :])
                elif kind == "norm2":
                    ln_scale(norm_of("sum2", b), b, group(b))

        @block.vector
        def _(dve):
            steps = [0]

            def after(ins):
                steps[0] += 1
                ins.then_inc(S["dve"], 1)
                dve.wait_ge(S["dve"], steps[0])

            def ln_stats(n, add):
                u = n % 2
                if n >= 2:
                    dve.wait_ge(S["ln_x"], TB * (n - 1))
                add(ln_in[:, u, :, :])
                for t in range(TB):
                    last = nc.vector.bn_stats(ln_st[:, u, t, :], ln_in[:, u, t, :])
                after(last)
                for t in range(TB):
                    last = nc.vector.bn_aggr(ln_mv[:, u, t, :], ln_st[:, u, t, :])
                last.then_inc(S["ln_mv"], 1)

            nc.vector.memset(consts[:, 0:1], EPS)
            nc.vector.memset(consts[:, 1:2], -0.5)
            nc.vector.memset(consts[:, 2:3], MAGIC)
            nc.vector.memset(consts[:, 3:4], -1.0)
            ones_2 = float(np.array([0x3F803F80], np.uint32).view(np.float32)[0])
            words = arena[:, 8192:].rearrange("p (u w) -> p u w", u=2)
            nc.vector.memset(words[:, 0, :], ones_2).then_inc(S["setup_dve"], 1)

            def residues(n, src, width):
                pt = parts[:, n % 4]
                dve.wait_ge(S["x_hi"], n + 1)
                nc.vector.tensor_tensor(rest[:, n % 2, 0:width], src, pt[:, 0, 0:width], ALU.subtract)\
                    .then_inc(S["x_res"], 1)
                dve.wait_ge(S["x_mid"], n + 1)
                nc.vector.tensor_tensor(pt[:, 2, 0:width], rest[:, n % 2, 0:width], pt[:, 1, 0:width], ALU.subtract)\
                    .then_inc(S["x_lo"], 1)

            for kind, i, banks in self_attention():
                if kind == "proj":
                    bq, bk, bv = banks
                    for w, bank, k in (("q", bq, 0), ("k", bk, 1)):
                        dve.wait_ge(S[w + "_hi"], i + 1)
                        pt = parts[:, 2 * (i % 2) + k]
                        nc.vector.tensor_tensor(rest[:, k, :], ps[:, bank, :], pt[:, 0, :], ALU.subtract)\
                            .then_inc(S[w + "_res"], 1)
                        dve.wait_ge(S[w + "_mid"], i + 1)
                        nc.vector.tensor_tensor(pt[:, 2, :], rest[:, k, :], pt[:, 1, :], ALU.subtract)\
                            .then_inc(S[w + "_lo"], 1)
                    if i == 1:
                        nc.vector.memset(words[:, 1, :], ones_2).then_inc(S["setup_dve"], 1)
                elif kind == "a":
                    u, r = divmod(i, HALF * TB)
                    if r == 0 and u >= 2:
                        dve.wait_ge(S["m_t"], u - 1)
                    dve.wait_ge(S["a_s"], i + 1)
                    nc.vector.tensor_reduce(max_t[:, u % 2, r % TB, r // TB:r // TB + 1], ps[:, banks[0], :], AX_X,
                                            ALU.max, negate=True).then_inc(S["a_max"], 1)
                elif kind == "cross":
                    width = SEQ if i else NCTX
                    residues(i, ps[:, banks[0], 0:width], width)
                elif kind == "max":
                    dve.wait_ge(S["m_hi"], i + 1)
                    mp = max_p[:, i % 2]
                    nc.vector.tensor_tensor(max_r[:, :], ps[0:HALF, banks[0], :], mp[:, 0, :], ALU.subtract)\
                        .then_inc(S["m_res"], 1)
                    dve.wait_ge(S["m_mid"], i + 1)
                    nc.vector.tensor_tensor(mp[:, 2, :], max_r[:, :], mp[:, 1, :], ALU.subtract)\
                        .then_inc(S["m_lo"], 1)
                elif kind == "norm":
                    b, q = divmod(i, 4)
                    dve.wait_ge(S["ott"], i + 1)
                    o = ps[:, banks[0], :].rearrange("p (t j e) -> p t j e", t=TB, j=4)
                    after(nc.vector.reciprocal(recip[:, i % 2, :, :], o[:, :, :, HD]))
                    nc.vector.tensor_tensor(
                        d_t[:, TB * b:TB * b + TB, 32 * q:32 * q + 32].rearrange("p t (j e) -> p t j e", j=4),
                        o[:, :, :, 0:HD], recip[:, i % 2, :, :].unsqueeze(3).to_broadcast([P, TB, 4, HD]),
                        ALU.mult).then_inc(S["attn"], 1)
                elif kind == "ln_a":
                    b = i
                    dve.wait_ge(S["attn"], 4 * (b + 1))
                    ln_stats(i, lambda y: after(nc.vector.tensor_tensor(
                        y, d_t[:, TB * b:TB * b + TB, :], x_t[:, TB * b:TB * b + TB, :], ALU.add)))

            def divide(bank, n, b, quad):
                o = ps[:, bank, :].rearrange("p (t j e) -> p t j e", t=TB, j=4)
                after(nc.vector.reciprocal(recip[:, n % 2, :, :], o[:, :, :, HD]))
                return nc.vector.tensor_tensor(
                    d_t[:, TB * b:TB * b + TB, 32 * quad:32 * quad + 32].rearrange("p t (j e) -> p t j e", j=4),
                    o[:, :, :, 0:HD], recip[:, n % 2, :, :].unsqueeze(3).to_broadcast([P, TB, 4, HD]), ALU.mult)

            def cross():
                for kind, b, t in cross_attention():
                    n = TB * b + t
                    if kind == "q":
                        residues(1 + b, ps[:, 7, :], SEQ)
                    elif kind == "s":
                        z = zs[:, b % 2, t, :, :]
                        if t == 0 and b >= 2:
                            dve.wait_ge(S["x_pt"], 4 * (4 * (b - 1)))
                        for i in range(3):
                            lo, hi = 6 * i, min(6 * i + 6, NH)
                            dve.wait_ge(S["x_s"], 3 * n + i + 1)
                            nc.vector.scalar_tensor_tensor(
                                z[:, lo:hi, :], ps[:, i, 0:(hi - lo) * CTX].rearrange("p (h k) -> p h k", k=CTX),
                                SCALE, mask[:, t:t + 1, :].to_broadcast([P, hi - lo, CTX]), ALU.mult, ALU.add)\
                                .then_inc(S["x_z"], 1)
                        dve.wait_ge(S["x_z"], 3 * (n + 1))
                        if n >= 2:
                            dve.wait_ge(S["x_sub"], n - 1)
                        nc.vector.tensor_reduce(x_mx[:, n % 2, :], z, AX_X, ALU.max).then_inc(S["x_mx"], 1)
                    elif kind == "pt":
                        dve.wait_ge(S["x_pt"], 4 * n + 4)
                        if n >= 2:
                            dve.wait_ge(S["x_pv"], n - 1)
                        nc.vector.tensor_copy(pt_b[:, n % 2, 3, :], ps[0:CTX, 4, :]).then_inc(S["x_pd"], 1)
                    elif kind == "norm":
                        dve.wait_ge(S["x_ott"], n + 1)
                        divide(6, n, b, t).then_inc(S["x_attn"], 1)
                    elif kind == "wo":
                        dve.wait_ge(S["x_wo"], b + 1)
                        ln_stats(NB + b, lambda y: after(nc.vector.tensor_tensor(
                            y, tiles(7), x_t[:, TB * b:TB * b + TB, :], ALU.add)))

            qkv_banks = {}

            def qkv_bias(b, t):
                g, i0 = TB * b + t, ROWS.index("iq_b")
                dve.wait_ge(S["i_raw"], g + 1)
                nc.vector.tensor_tensor(qkv[:, b, t, :], ps[:, qkv_banks[b][t], 0:3 * P],
                                        rows[:, i0:i0 + 3, :].rearrange("p i c -> p (i c)"), ALU.add)\
                    .then_inc(S["i_qkv"], 1)

            def rotated(steps):
                for kind, i, banks in steps:
                    if kind == "k":
                        nc.vector.memset(arena[:, 6272:6272 + 2 * NH * CTX], ones_2).then_inc(S["setup_dve"], 1)
                    if kind in ("k", "q"):
                        n = 5 if kind == "k" else 6 + i
                        width = NCTX if kind == "k" else SEQ
                        dve.wait_ge(S["x_raw"], n + 1)
                        if n > 5:
                            dve.wait_ge(S["x_hi"], n)
                        for j, nm in ((0, "c" + kind + "_b"), (1, "c" + kind + "s_b")):
                            bank = banks[j]
                            if kind == "k":
                                o_, s_ = (a.rearrange("p (b k) -> p b k", b=NB)
                                          for a in (rp[:, j, 0:width], ps[:, bank, 0:width]))
                                tab = rope_k[:, j:j + 1, :].to_broadcast([P, NB, CTX])
                            else:
                                o_, s_, tab = rp[:, j, :], ps[:, bank, :], rope_q[:, j, :]
                            last = nc.vector.scalar_tensor_tensor(o_, s_, col(nm), tab, ALU.add, ALU.mult)
                        after(last)
                        nc.vector.tensor_tensor(rp[:, 2, 0:width], rp[:, 0, 0:width], rp[:, 1, 0:width],
                                                ALU.add).then_inc(S["x_rope"], 1)
                        residues(n, rp[:, 2, 0:width], width)
                        if kind == "k":
                            dve.wait_ge(S["x_vraw"], 2)
                            nc.vector.tensor_tensor(
                                v_heads[0:CTX, 0:NB, :, 0:HD],
                                ps[0:CTX, banks[2], :].rearrange("p (t h e) -> p t h e", t=NB, h=NH),
                                rows[0:CTX, ROWS.index("cv_b"), :].rearrange("p (h e) -> p h e", h=NH)
                                .unsqueeze(1).to_broadcast([CTX, NB, NH, HD]), ALU.add).then_inc(S["x_v"], 1)
                    elif kind == "a":
                        b, t = divmod(i, TB)
                        if t == 0 and b >= 2:
                            dve.wait_ge(S["m_t"], 2 * NB + b - 1)
                        for j in range(3):
                            lo, hi = 6 * j, min(6 * j + 6, NH)
                            dve.wait_ge(S["c_s"], 3 * i + j + 1)
                            nc.vector.tensor_reduce(
                                cm_t[:, b % 2, t, lo:hi],
                                ps[:, banks[j], 0:(hi - lo) * CTX].rearrange("p (h k) -> p h k", k=CTX),
                                AX_X, ALU.max, negate=True).then_inc(S["c_mx"], 1)
                    elif kind == "max":
                        mp = cm_p[:, i % 2]
                        dve.wait_ge(S["m_hi"], 2 * NB + i + 1)
                        nc.vector.tensor_tensor(cm_r[:, :], ps[0:NH, banks[0], :], mp[:, 0, :], ALU.subtract)\
                            .then_inc(S["m_res"], 1)
                        dve.wait_ge(S["m_mid"], 2 * NB + i + 1)
                        nc.vector.tensor_tensor(mp[:, 2, :], cm_r[:, :], mp[:, 1, :], ALU.subtract)\
                            .then_inc(S["m_lo"], 1)
                    elif kind == "norm":
                        dve.wait_ge(S["x_ott"], NT + i + 1)
                        divide(banks[0], i, i // 4, i % 4).then_inc(S["x_attn"], 1)
                    elif kind == "wo":
                        dve.wait_ge(S["x_wo"], NB + i + 1)

                        def add(y, b=i):
                            after(nc.vector.tensor_tensor(y, tiles(banks[0]), row("co_b", TB), ALU.add))
                            after(nc.vector.tensor_tensor(y, y, x_t[:, TB * b:TB * b + TB, :], ALU.add))
                        ln_stats(4 * NB + i, add)
                    elif kind == "qkv":
                        qkv_banks[i] = banks
                        for t in range(TB if i < NB - 1 else 0):
                            qkv_bias(i, t)

            cross()
            TH, SP_ = 1.0, [0.9, 0.2]
            for b in range(NB + 1):
                if b > 0:
                    c = b - 1
                    stt = nc.vector.scalar_tensor_tensor
                    y = fy[:, c % 2, :]
                    dve.wait_ge(S["f_y"], c + 1)
                    nc.vector.tensor_scalar(fs[:, 0, :], y, TH, None, ALU.is_gt)
                    after(stt(fs[:, 1, :], y, SP_[0], y, ALU.mult, ALU.add))
                    after(stt(fs[:, 2, :], y, TH, fs[:, 1, :], ALU.is_gt, ALU.subtract))
                    acc, m, t_ = 0, 2, 1
                    for k in range(3):
                        new_acc, u_ = 3 + k % 2, 1
                        stt(fs[:, new_acc, :], fs[:, m, :], -TH, fs[:, acc, :], ALU.is_lt, ALU.add)
                        after(stt(fs[:, 1, :], fs[:, m, :], SP_[0], y, ALU.mult, ALU.subtract))
                        new_m = 5 if m == 2 else 2
                        after(stt(fs[:, new_m, :], fs[:, m, :], -TH, fs[:, 1, :], ALU.is_lt, ALU.add))
                        acc, m = new_acc, new_m
                    after(stt(fs[:, 0, :], fs[:, m, :], -TH, fs[:, acc, :], ALU.is_lt, ALU.add))
                    ln_stats(2 * NB + c, lambda o: after(stt(
                        o, fs[:, 0, :].rearrange("p (t c) -> p t c", t=TB), SP_[1],
                        x_t[:, TB * c:TB * c + TB, :], ALU.mult, ALU.add)))
            stt, tt, ts = nc.vector.scalar_tensor_tensor, nc.vector.tensor_tensor, nc.vector.tensor_scalar
            dve.wait_ge(S["r_sum"], 1)
            after(ts(w_mean[:, :], ps[:, 6, 0:4], 1.0 / (P * P), 1e-5, ALU.mult, ALU.max))
            after(nc.vector.reciprocal(w_inv[:, :], w_mean[:, :]))
            for w in range(4):
                t = arg[:, 0, w * P:(w + 1) * P]
                after(ts(t, mat("r" + "kvro"[w]), w_inv[:, w:w + 1], MAGIC, ALU.mult, ALU.add))
                after(ts(t, t, MAGIC, 1.0, ALU.subtract, ALU.min))
                ts(w_q[:, w, :], t, -1.0, None, ALU.max).then_inc(S["r_wq"], 1)
            ts(mix_c[:, :], cols[:, 2:5], -1.0, 1.0, ALU.mult, ALU.add)
            nc.vector.memset(alpha[:, 0:1], 0.0)
            nc.vector.memset(beta[:, 0:1], 0.0)
            nc.vector.memset(eps[:, 0:1], 0.0)
            nc.vector.memset(mixed[:, :, 0:1], 0.0)
            dve.wait_ge(S["r_eps"], 1)
            after(ts(log_w[:, 1:2], log_w[:, 0:1], -1.0, None, ALU.mult))
            freed = {}
            rotated(KEYS)
            for kind, n, b, w in recurrent():
                if kind == "project":
                    rotated([("q", b, (4, 5))])
                    continue
                u = n % 2
                as_tiles = lambda a: a.rearrange("p (t c) -> p t c", t=TB)
                k, v = key_f[:, b % 2, :], val_f[:, b % 2, :]
                first, lw = col("first"), log_w[:, 1:2]
                was, now = eps[:, 0:SEQ], eps[:, 1:SEQ + 1]
                if kind == "mix":
                    if w < 3:
                        if w == 0:
                            dve.wait_ge(S["ln_f"], 2 * NB + b + 1)
                        m = mixed[:, u, :]
                        if n >= 2:
                            dve.wait_ge(S["r_zt"], n - 1)
                        ts(m[:, 0:1], x_f[:, b, 0:1], 0.0, None, ALU.mult)
                        after(ts(m[:, 1:SEQ], x_f[:, b, 0:SEQ - 1], mix_c[:, w:w + 1], None, ALU.mult))
                        stt(m, x_f[:, b, :], cols[:, 2 + w:3 + w], m, ALU.mult, ALU.add).then_inc(S["r_mix"], 1)
                    else:
                        dve.wait_ge(S["r_tanh"], b + 1)
                        after(ts(gate, gate, 0.5, 0.5, ALU.mult, ALU.add))
                elif kind == "rms":
                    rms = row("rms_" + "kvro"[w], TB)
                    if n >= 2:
                        dve.wait_ge(S["r_q"], TB * (n - 1))
                    dve.wait_ge(S["r_zt"], n + 1)
                    if w < 3:
                        tt(as_tiles(weighed[:, u, :]), tiles(n % 2), rms, ALU.mult).then_inc(S["r_u"], 1)
                    else:
                        tt(gated, tiles(n % 2), as_tiles(gate), ALU.mult).then_inc(S["r_z"], 1)
                        dve.wait_ge(S["r_z"], b + 1)
                        tt(as_tiles(weighed[:, u, :]), gated, rms, ALU.mult).then_inc(S["r_u"], 1)
                elif kind == "sums":
                    dve.wait_ge(S["r_u"], n + 1)
                    nc.vector.tensor_reduce(tok[:, u, 1, :], as_tiles(weighed[:, u, :]), AX_X, ALU.max,
                                            apply_absolute_value=True).then_inc(S["r_ss"], 1)
                elif kind == "scale":
                    dve.wait_ge(S["r_is"], n + 1)
                    after(nc.vector.reciprocal(tok[:, u, 6, :], tok[:, u, 4, :]))
                    tt(tok[:, u, 7, :], tok[:, u, 4, :], w_mean[:, w:w + 1].to_broadcast([P, TB]), ALU.mult)
                    tt(tok[:, u, 5, :], tok[:, u, 6, :], tok[:, u, 2, :], ALU.mult).then_inc(S["r_r2"], 1)
                elif kind == "quant":
                    dve.wait_ge(S["r_q"], TB * (n + 1))
                    if n >= 2:
                        dve.wait_ge(S["r_xt"], n - 1)
                    ts(x_q[:, u, :], shifted_q[:, u, :], MAGIC, 127.0, ALU.subtract, ALU.min)\
                        .then_inc(S["r_xq"], 1)
                elif kind == "lin":
                    dve.wait_ge(S["r_mm"], n + 1)
                    if u in freed:
                        dve.wait_ge(*freed.pop(u))
                    if w < 3:
                        freed[u] = (S["r_ktt"], 2 * b + w + 1) if w < 2 else (S["r_tanh"], b + 1)
                    tt(as_tiles(lin[:, u, :]), tiles(3), per_token(tok[:, u, 7, :]), ALU.mult)\
                        .then_inc(S["r_kt"], 1)
                    if w == 3:
                        dve.wait_ge(S["r_kt"], n + 1)
                        ln_stats(3 * NB + b, lambda y: after(tt(
                            y, as_tiles(lin[:, u, :]), x_t[:, TB * b:TB * b + TB, :], ALU.add)))
                elif kind == "wkv1":
                    dve.wait_ge(S["r_kf"], 2 * b + 2)
                    after(nc.vector.tensor_tensor_scan(now, lw.to_broadcast([P, SEQ]), k, 0.0, ALU.add, ALU.max))
                    stt(arg[:, 0, :], was, lw, now, ALU.add, ALU.subtract)
                    tt(arg[:, 1, :], k, now, ALU.subtract).then_inc(S["r_arg1"], 1)
                elif kind == "wkv2":
                    after(stt(wkv, k, first, was, ALU.add, ALU.max))
                    tt(arg[:, 2, :], was, wkv, ALU.subtract)
                    stt(arg[:, 3, :], k, first, wkv, ALU.add, ALU.subtract).then_inc(S["r_arg2"], 1)
                elif kind == "wkv3":
                    dve.wait_ge(S["r_exp1"], b + 1)
                    nc.vector.tensor_tensor_scan(beta[:, 1:], ex[:, 0, :], ex[:, 1, :], 0.0, ALU.mult, ALU.add)
                    after(tt(arg[:, 0, :], ex[:, 1, :], v, ALU.mult))
                    after(nc.vector.tensor_tensor_scan(alpha[:, 1:], ex[:, 0, :], arg[:, 0, :], 0.0, ALU.mult,
                                                       ALU.add))
                elif kind == "wkv4":
                    dve.wait_ge(S["r_exp2"], b + 1)
                    tt(arg[:, 1, :], ex[:, 2, :], beta[:, 0:SEQ], ALU.mult)
                    after(tt(arg[:, 2, :], ex[:, 2, :], alpha[:, 0:SEQ], ALU.mult))
                    dve.wait_ge(S["r_ev"], b + 1)
                    tt(arg[:, 0, :], arg[:, 1, :], ex[:, 3, :], ALU.add)
                    after(tt(arg[:, 2, :], arg[:, 2, :], arg[:, 3, :], ALU.add))
                    after(nc.vector.reciprocal(arg[:, 1, :], arg[:, 0, :]))
                    tt(wkv, arg[:, 2, :], arg[:, 1, :], ALU.mult).then_inc(S["r_w"], 1)
            rotated(rotated_attention())
            all_pairs = [P, NB, NB, NH]
            g = [gates[:, i, :, :] for i in range(16)]
            one = [g[12][:, :, i] for i in range(4)]
            wide = lambda a: a.unsqueeze(2).to_broadcast([P, TB, NE])
            for kind, b, e in last_layer():
                if kind == "expert":
                    continue
                xb, hb = group(b), h_t[:, TB * b:TB * b + TB, :]
                if kind == "score":
                    u = b % 2
                    most = sc_n[:, 3 * u]
                    qkv_bias(NB - 1, b)
                    dve.wait_ge(S["i_qkv"], TB * (NB - 1) + b + 1)
                    after(tt(prod[:, u], qkv[:, :, b, 0:P].unsqueeze(2).to_broadcast([P, NB, NB, P]),
                             qkv[:, :, b, P:2 * P].unsqueeze(1).to_broadcast([P, NB, NB, P]), ALU.mult))
                    after(nc.vector.tensor_reduce(sc[:, u].rearrange("p q s h -> p (q s h)"),
                                                  prod[:, u].rearrange("p q s (h e) -> p (q s h) e", h=NH),
                                                  AX_X, ALU.add))
                    after(nc.vector.tensor_reduce(most, sc[:, u].rearrange("p q s h -> p q h s"), AX_X, ALU.max))
                    tt(sc[:, u], sc[:, u], most.unsqueeze(2).to_broadcast(all_pairs), ALU.subtract)\
                        .then_inc(S["i_sc"], 1)
                elif kind == "weigh":
                    u = b % 2
                    total, inv = sc_n[:, 3 * u + 1], sc_n[:, 3 * u + 2]
                    dve.wait_ge(S["i_exp"], b + 1)
                    after(nc.vector.tensor_reduce(total, pr[:, u].rearrange("p q s h -> p q h s"), AX_X, ALU.add))
                    after(nc.vector.reciprocal(inv, total))
                    tt(pr[:, u], pr[:, u], inv.unsqueeze(2).to_broadcast(all_pairs), ALU.mult)\
                        .then_inc(S["i_p"], 1)
                elif kind == "out":
                    dve.wait_ge(S["i_out"], b + 1)

                    def add(y):
                        after(tt(y, tiles(5), row("io_b", TB), ALU.add))
                        after(tt(y, y, xb, ALU.add))
                    ln_stats(norm_of("out", b), add)
                elif kind == "h":
                    n = norm_of("out", b)
                    dve.wait_ge(S["ln_x"], TB * (n + 1))
                    after(tt(hb, ln_in[:, n % 2, :, :], row("ln1_g", TB), ALU.mult))
                    tt(hb, hb, row("ln1_b", TB), ALU.add).then_inc(S["ln_g"], 1)
                elif kind == "prob":
                    dve.wait_ge(S["g_raw"], b + 1)
                    after(tt(g[0], ps[:, 7, 0:TB * NE].rearrange("p (t e) -> p t e", t=TB),
                             rows[:, ROWS.index("router_b"), 0:TB * NE].rearrange("p (t e) -> p t e", t=TB),
                             ALU.add))
                    after(nc.vector.tensor_reduce(one[0], g[0], AX_X, ALU.max))
                    tt(g[1], g[0], wide(one[0]), ALU.subtract).then_inc(S["g_d"], 1)
                elif kind == "pick":
                    dve.wait_ge(S["g_exp"], b + 1)
                    after(nc.vector.tensor_reduce(one[1], g[2], AX_X, ALU.add))
                    after(nc.vector.reciprocal(one[2], one[1]))
                    after(tt(g[3], g[2], wide(one[2]), ALU.mult))
                    p_i, p_j = (g[3].unsqueeze(a).to_broadcast([P, TB, NE, NE]) for a in (3, 2))
                    tt(rank[:, 0], p_j, p_i, ALU.is_ge)
                    after(tt(rank[:, 1], p_j, p_i, ALU.is_gt))
                    after(tt(rank[:, 0], rank[:, 0], rank[:, 1], ALU.subtract))
                    after(tt(rank[:, 2], rank[:, 0],
                             tri[:, :].rearrange("p (e f) -> p e f", e=NE).unsqueeze(1)
                             .to_broadcast([P, TB, NE, NE]), ALU.mult))
                    after(tt(rank[:, 0], rank[:, 2], rank[:, 1], ALU.add))
                    after(nc.vector.tensor_reduce(g[4], rank[:, 0], AX_X, ALU.add))
                    numbers = iota[:, :].unsqueeze(1).to_broadcast([P, TB, NE])
                    after(stt(g[5], g[4], 1.5, numbers, ALU.is_lt, ALU.mult))
                    after(nc.vector.tensor_reduce(one[3], g[5], AX_X, ALU.max))
                    if b >= 2:
                        dve.wait_ge(S["g_oht"], b - 1)
                    tt(g[8 + b % 2], numbers, wide(one[3]), ALU.is_equal).then_inc(S["g_oh"], 1)
                elif kind == "sum1":
                    dve.wait_ge(S["e_o"], (NE - 1) * (b + 1))
                    ln_stats(norm_of("sum1", b), lambda y: after(tt(y, tiles(2 + b % 2), hb, ALU.add)))
                elif kind == "sum2":
                    n = norm_of("sum1", b)
                    dve.wait_ge(S["ln_x"], TB * (n + 1))
                    m = ln_in[:, n % 2, :, :]
                    after(tt(m, m, row("ln2_g", TB), ALU.mult))
                    after(tt(m, m, row("ln2_b", TB), ALU.add))
                    ln_stats(n + 1, lambda y: after(tt(y, m, xb, ALU.add)))

        @block.gpsimd
        def _(pool):
            steps = [0]

            def after(ins):
                steps[0] += 1
                ins.then_inc(S["pool"], 1)
                pool.wait_ge(S["pool"], steps[0])

            def zeros(u):
                nc.gpsimd.memset(q_st[:, u, :, :].rearrange("p h q -> p (h q)").bitcast(F32), 0.0)\
                    .then_inc(S["setup"], 1)

            zeros(0)
            zeros(1)
            nc.gpsimd.memset(v_aug[:, :], 1.0).then_inc(S["setup"], 1)
            nc.gpsimd.memset(ones[:, :], 1.0)
            pool.wait_ge(S["load_s"], 16 * N_SMALL)
            nc.gpsimd.tensor_copy(ident_b[:, :], mat("ident")).then_inc(S["setup"], 1)

            def ln_scales(n):
                u = n % 2
                pool.wait_ge(S["ln_mv"], n + 1)
                mean, var = ln_mv[:, u, :, 0], ln_mv[:, u, :, 1]
                r = ln_rs[:, u, :, :]
                after(nc.gpsimd.tensor_tensor(r[:, :, 0], var, consts[:, 0:1].to_broadcast([P, TB]), ALU.add))
                after(nc.gpsimd.tensor_tensor(r[:, :, 1], r[:, :, 0], consts[:, 1:2].to_broadcast([P, TB]), ALU.pow))
                after(nc.gpsimd.tensor_tensor(r[:, :, 2], mean, r[:, :, 1], ALU.mult))
                nc.gpsimd.tensor_tensor(r[:, :, 3], r[:, :, 2], consts[:, 3:4].to_broadcast([P, TB]), ALU.mult)\
                    .then_inc(S["ln_rs"], 1)

            pool.wait_ge(S["setup_dve"], 1)
            for kind, i, banks in self_attention():
                if kind == "ln_a":
                    ln_scales(i)

            def cross():
                for kind, b, t in cross_attention():
                    if kind == "s":
                        n = TB * b + t
                        z = zs[:, b % 2, t, :, :]
                        pool.wait_ge(S["x_mx"], n + 1)
                        nc.gpsimd.tensor_tensor(z, z, x_mx[:, n % 2, :].unsqueeze(2).to_broadcast([P, NH, CTX]),
                                                ALU.subtract).then_inc(S["x_sub"], 1)
                    elif kind == "wo":
                        ln_scales(NB + b)

            def rotated(steps):
                pool.wait_ge(S["ln_mv"], 4 * NB)
                zeros(1)
                for kind, i, banks in steps:
                    if kind == "wo":
                        ln_scales(4 * NB + i)

            cross()
            for b in range(NB + 1):
                if b < NB:
                    for f in range(FC):
                        n = FC * b + f
                        pool.wait_ge(S["f_r"], n + 1)
                        if b >= 2 and f == 0:
                            pool.wait_ge(S["f_yraw"], b - 1)
                        nc.gpsimd.tensor_tensor(fh[:, b % 2, f, :], fr[:, n % 2, :], fr[:, n % 2, :], ALU.mult)\
                            .then_inc(S["f_sq"], 1)
                if b > 1:
                    ln_scales(2 * NB + b - 2)
            ln_scales(3 * NB - 1)
            tt, ts = nc.gpsimd.tensor_tensor, nc.gpsimd.tensor_scalar
            zeros(0)
            for kind, n, b, w in recurrent():
                k = tok[:, n % 2, :, :]
                if kind == "sums":
                    pool.wait_ge(S["r_ss"], n + 1)
                    pool.wait_ge(S["r_sq"], TB * (n + 1))
                    after(ts(k[:, 3, :], k[:, 0, :], 1.0 / P, 1e-8, ALU.mult, ALU.add))
                    after(tt(k[:, 2, :], k[:, 3, :], consts[:, 1:2].to_broadcast([P, TB]), ALU.pow))
                    after(tt(k[:, 6, :], k[:, 1, :], k[:, 2, :], ALU.mult))
                    ts(k[:, 4, :], k[:, 6, :], 1e-5, 1.0 / 127.0, ALU.max, ALU.mult).then_inc(S["r_is"], 1)
                elif kind == "wkv3":
                    pool.wait_ge(S["r_exp2"], b + 1)
                    tt(arg[:, 3, :], ex[:, 3, :], val_f[:, b % 2, :], ALU.mult).then_inc(S["r_ev"], 1)
                elif kind == "lin" and w == 3:
                    ln_scales(3 * NB + b)
            rotated(rotated_attention())
            for kind, b, e in last_layer():
                if kind == "weigh":
                    pool.wait_ge(S["i_p"], b + 1)
                    if b >= 2:
                        pool.wait_ge(S["i_ct"], b - 1)
                    for q in range(NB):
                        tt(pv_t[:, b % 2, q].rearrange("p s (h e) -> p s h e", h=NH),
                           pr[:, b % 2, q].unsqueeze(3).to_broadcast([P, NB, NH, HD]),
                           qkv[:, :, b, 2 * P:3 * P].rearrange("p s (h e) -> p s h e", h=NH), ALU.mult)\
                            .then_inc(S["i_pp"], 1)
                elif kind in ("out", "sum1", "sum2"):
                    ln_scales(norm_of(kind, b))


def head_last(w):
    return w.reshape(*w.shape[:-1], NH, HD).swapaxes(-1, -2).reshape(w.shape)


def swapped(w):
    return np.roll(w, P // 2, axis=-1)


def rope_tables():
    out = []
    inv = (1.0 / 10000.0 ** (np.arange(0, HD, 2, dtype=np.float32) / HD)).astype(np.float32)
    for n in (SEQ, CTX):
        t = np.arange(n, dtype=np.float32)
        f = np.outer((10.0 * (t / n)).astype(np.float32), inv).astype(np.float32).T
        cos, sin = np.cos(f), np.sin(f)
        tab = np.stack([np.concatenate([cos, cos]), np.concatenate([-sin, sin])], 1)
        out.append(np.repeat(tab, NH, axis=0).astype(np.float32))
    return out


def lay_out(i):
    f = {k: np.asarray(v) for k, v in i.items()}
    cq, ck = head_last(f["L1_xattn_Wq"].T), head_last(f["L1_xattn_Wk"].T)
    bq, bk = head_last(f["L1_xattn_bq"]), head_last(f["L1_xattn_bk"])
    inp, inb = f["L1_ffn_in_proj_w"].T, f["L1_ffn_in_proj_b"]
    fc, pj = f["L0_ffn_W_fc"].T, f["L0_ffn_W_proj"].T
    mats = {"q0": head_last(f["L0_attn_w_Q"]), "k0": head_last(f["L0_attn_w_K"]), "v0": f["L0_attn_w_V"],
            "xq": head_last(f["L0_xattn_wq"]), "xk": head_last(f["L0_xattn_wk"]), "xv": f["L0_xattn_wv"],
            "xo": f["L0_xattn_wo"], "rk": f["L1_attn_w_key"].T, "rv": f["L1_attn_w_value"].T,
            "rr": f["L1_attn_w_receptance"].T, "ro": f["L1_attn_w_output"].T,
            "cq": cq, "cqs": swapped(cq), "ck": ck, "cks": swapped(ck), "cv": f["L1_xattn_Wv"].T,
            "co": f["L1_xattn_Wo"].T, "iq": inp[:, 0:P], "ik": inp[:, P:2 * P], "iv": inp[:, 2 * P:],
            "io": f["L1_ffn_out_w"].T, "ident": np.eye(P, dtype=np.float32)}
    for c in range(FC):
        mats[f"fc{c}"] = fc[:, c * P:(c + 1) * P]
        mats[f"pj{c}"] = pj[c * P:(c + 1) * P, :]
    for e in range(NE):
        mats[f"w1_{e}"], mats[f"w2_{e}"] = f["L1_ffn_w1"][e].T, f["L1_ffn_w2"][e].T
    rows = {"cv_b": f["L1_xattn_bv"], "co_b": f["L1_xattn_bo"], "iq_b": inb[0:P], "ik_b": inb[P:2 * P],
            "iv_b": inb[2 * P:], "io_b": f["L1_ffn_out_b"], "ln1_g": f["L1_ffn_ln1_g"], "ln1_b": f["L1_ffn_ln1_b"],
            "ln2_g": f["L1_ffn_ln2_g"], "ln2_b": f["L1_ffn_ln2_b"], "rms_k": f["L1_attn_rms_key"],
            "rms_v": f["L1_attn_rms_value"], "rms_r": f["L1_attn_rms_receptance"], "rms_o": f["L1_attn_rms_output"],
            "router_b": np.tile(f["L1_ffn_router_b"], P // NE)}
    cols = {"decay": f["L1_attn_time_decay"], "first": f["L1_attn_time_first"],
            "mix_k": f["L1_attn_time_mix_key"].reshape(P), "mix_v": f["L1_attn_time_mix_value"].reshape(P),
            "mix_r": f["L1_attn_time_mix_receptance"].reshape(P),
            "cq_b": bq, "cqs_b": swapped(bq), "ck_b": bk, "cks_b": swapped(bk)}
    for e in range(NE):
        cols[f"b1_{e}"] = f["L1_ffn_b1"][e]
    rope_q, rope_k = rope_tables()
    pen = np.full((NE, NE, P), PENALTY, np.float32)
    pen[np.arange(NE), np.arange(NE)] = 0
    x = f["x"]
    out = {
        "x_t": x.reshape(NT, P, P).transpose(1, 0, 2), "x_f": x.transpose(2, 0, 1),
        "ctx_f": f["ctx_1024"].transpose(2, 0, 1).reshape(P, NCTX),
        "mask": f["mask_1x1xSxS2_ff0"].reshape(TB, P, CTX).transpose(1, 0, 2),
        "mats": np.stack([mats[n] for n in MATS], 1), "rows": np.stack([rows[n] for n in ROWS]),
        "cols": np.stack([cols[n] for n in COLS], 1), "router": f["L1_ffn_router_w"].T, "b2": f["L1_ffn_b2"],
        "rope_q": rope_q, "rope_k": rope_k,
        "tri": np.tile(np.tril(np.ones((NE, NE), np.float32), -1).reshape(1, -1), (P, 1)),
        "iota": np.tile(np.arange(NE, dtype=np.float32), (P, 1)),
        "pen": pen.astype(mybir.dt.np(BF16)),
    }
    return {k: np.ascontiguousarray(v) for k, v in out.items()}


def kernel(**inputs):
    import concourse.bacc as bacc
    from concourse.bass_utils import run_bass_kernel_spmd

    arrays = lay_out(inputs)
    nc = bacc.Bacc("TRN2", target_bir_lowering=False, num_devices=1)
    d = {n: nc.dram_tensor("in_" + n, a.shape, mybir.dt.from_np(a.dtype), kind="ExternalInput").ap()
         for n, a in arrays.items()}
    d["out"] = nc.dram_tensor("out_x", (NB, SEQ, P), F32, kind="ExternalOutput").ap()
    transformer(nc, d)
    r = run_bass_kernel_spmd(nc, [{"in_" + n: a for n, a in arrays.items()}], core_ids=[0])
    return r.results[0]["out_x"]
```
